# Optimizing a Trainium2 kernel written in Bass

```python
import numpy as np
import jax
import jax.numpy as jnp

def _softmax(x, axis=-1):
    return jax.nn.softmax(x, axis=axis)

def _gelu(x):
    return jax.nn.gelu(x, approximate=True)

def _silu(x):
    return jax.nn.silu(x)

def _sigmoid(x):
    return jax.nn.sigmoid(x)

def _layernorm(x, axis=-1, eps=1e-05):
    m = jnp.mean(x, axis=axis, keepdims=True)
    v = jnp.var(x, axis=axis, keepdims=True)
    return (x - m) / jnp.sqrt(v + eps)

def _scatter_add(tgt, idx, src, axis=0):
    return tgt.at[idx].add(src)

def _segment_sum(src, seg, n):
    return jax.ops.segment_sum(src, seg, n)
kernel_name = 'mk_seq_preln_d2_jaxref_r8_574696'

def setup_inputs(seed: int=0):
    np.random.seed(seed)
    _w = jnp.asarray

    def _L0_attn_setup():
        import jax, jax.numpy as jnp
        import numpy as np
        B, T, C = (64, 32, 128)
        N_HEAD, HEAD_SIZE, KV_RANK = (16, 64, 128)
        BLOCK_SIZE = 32
        key = jax.random.key(seed)
        ks = jax.random.split(key, 5)
        HD = N_HEAD * HEAD_SIZE

        def init(k, shape):
            fan_in = shape[0]
            bound = 1.0 / np.sqrt(fan_in)
            return jax.random.uniform(k, shape, jnp.float32, -bound, bound)
        return {'x': jax.random.normal(ks[0], (B, T, C), jnp.float32), 'w_kv_down': init(ks[1], (C, KV_RANK)), 'w_kv_up': init(ks[2], (KV_RANK, 2 * HD)), 'w_q': init(ks[3], (C, HD)), 'w_out': init(ks[4], (HD, C))}
    _L0_attn_in = _L0_attn_setup()

    def _L0_ffn_setup():
        import jax, jax.numpy as jnp
        import numpy as np
        import math
        B, T, D, H, E, TOPK, CAPF = (4, 256, 128, 16, 8, 2, 2.0)
        HD = D // H

        def layernorm(x, g, b, eps=1e-05):
            m = jnp.mean(x, -1, keepdims=True)
            v = jnp.mean(jnp.square(x - m), -1, keepdims=True)
            return (x - m) * jax.lax.rsqrt(v + eps) * g + b

        def block_forward(x, ln1_g, ln1_b, Wqkv, Wproj, ln2_g, ln2_b, Wgate, W1, b1, W2, b2):
            Bb, Tt, d = x.shape
            hd = HD
            half = hd // 2
            h = layernorm(x, ln1_g, ln1_b)
            qkv = (h @ Wqkv).reshape(Bb, Tt, H, 3 * hd)
            q, k, v = (qkv[..., :hd], qkv[..., hd:2 * hd], qkv[..., 2 * hd:])
            inv_freq = 1.0 / 10000.0 ** (jnp.arange(0, hd, 2, dtype=jnp.float32) / hd)
            ang = jnp.arange(Tt, dtype=jnp.float32)[:, None] * inv_freq
            sin = jnp.sin(ang)[None, :, None, :].astype(x.dtype)
            cos = jnp.cos(ang)[None, :, None, :].astype(x.dtype)

            def rope(t):
                t1, t2 = (t[..., :half], t[..., half:])
                return jnp.concatenate([t1 * cos - t2 * sin, t1 * sin + t2 * cos], -1)
            q, k = (rope(q), rope(k))
            scores = jnp.einsum('bqhd,bkhd->bhqk', q, k) / math.sqrt(hd)
            causal = jnp.tril(jnp.ones((Tt, Tt), dtype=bool))
            scores = jnp.where(causal, scores, jnp.asarray(-1000000000.0, scores.dtype))
            probs = jax.nn.softmax(scores, axis=-1)
            attn = jnp.einsum('bhqk,bkhd->bqhd', probs, v).reshape(Bb, Tt, d) @ Wproj
            x = x + attn
            h2 = layernorm(x, ln2_g, ln2_b)
            flat = h2.reshape(-1, d)
            N = flat.shape[0]
            capacity = int(math.ceil(CAPF * N / E))
            gates = jax.nn.softmax((flat @ Wgate).astype(jnp.float32), -1).astype(flat.dtype)
            _, top_inds = jax.lax.top_k(gates, TOPK)
            mask = jnp.zeros((N, E), dtype=bool).at[jnp.arange(N)[:, None], top_inds].set(True)
            pos = jnp.cumsum(mask.astype(jnp.int32), axis=0) * mask - 1
            keep = (pos < capacity) & mask
            t_flat = jnp.repeat(jnp.arange(N), TOPK)
            e_flat = top_inds.reshape(-1)
            p = pos[t_flat, e_flat]
            kp = keep[t_flat, e_flat]
            p_eff = jnp.where(kp, p, capacity)
            exp_in = jnp.zeros((E, capacity, d), flat.dtype).at[e_flat, p_eff].set(flat[t_flat], mode='drop')
            hmid = jax.nn.gelu(jnp.einsum('ecd,edf->ecf', exp_in, W1) + b1[:, None, :], approximate=False)
            exp_out = jnp.einsum('ecf,efd->ecd', hmid, W2) + b2[:, None, :]
            gate = gates[t_flat, e_flat] * kp.astype(flat.dtype)
            p_g = jnp.minimum(p_eff, capacity - 1)
            moe = jnp.zeros((N, d), flat.dtype).at[t_flat].add(exp_out[e_flat, p_g] * gate[:, None])
            return x + moe.reshape(Bb, Tt, d)
        key = jax.random.key(seed)
        ks = jax.random.split(key, 8)
        s = 0.02
        return {'x': jax.random.normal(ks[0], (B, T, D), jnp.float32), 'ln1_g': jnp.ones((D,), jnp.float32), 'ln1_b': jnp.zeros((D,), jnp.float32), 'Wqkv': jax.random.normal(ks[1], (D, 3 * D), jnp.float32) * s, 'Wproj': jax.random.normal(ks[2], (D, D), jnp.float32) * s, 'ln2_g': jnp.ones((D,), jnp.float32), 'ln2_b': jnp.zeros((D,), jnp.float32), 'Wgate': jax.random.normal(ks[3], (D, E), jnp.float32) * s, 'W1': jax.random.normal(ks[4], (E, D, 4 * D), jnp.float32) * s, 'b1': jnp.zeros((E, 4 * D), jnp.float32), 'W2': jax.random.normal(ks[5], (E, 4 * D, D), jnp.float32) * s, 'b2': jnp.zeros((E, D), jnp.float32)}
    _L0_ffn_in = _L0_ffn_setup()

    def _L1_attn_setup():
        import jax, jax.numpy as jnp
        import numpy as np
        D_IN = 128
        D_OUT = 128
        NUM_HEADS = 16
        HEAD_DIM = D_OUT // NUM_HEADS
        key = jax.random.key(seed)
        ks = jax.random.split(key, 6)
        scale = 0.02
        x = jax.random.normal(ks[0], (4, 256, D_IN), dtype=jnp.float32)
        Wq = jax.random.normal(ks[1], (D_IN, D_OUT), dtype=jnp.float32) * scale
        Wk = jax.random.normal(ks[2], (D_IN, D_OUT), dtype=jnp.float32) * scale
        Wv = jax.random.normal(ks[3], (D_IN, D_OUT), dtype=jnp.float32) * scale
        Wo = jax.random.normal(ks[4], (D_OUT, D_OUT), dtype=jnp.float32) * scale
        bo = jax.random.normal(ks[5], (D_OUT,), dtype=jnp.float32) * scale
        return {'x': x, 'Wq': Wq, 'Wk': Wk, 'Wv': Wv, 'Wo': Wo, 'bo': bo}
    _L1_attn_in = _L1_attn_setup()

    def _L1_ffn_setup():
        import jax, jax.numpy as jnp
        import numpy as np
        DIM = 128
        HIDDEN = 384
        SCALE = 1.0 / 127.0

        def _dequant(w_int, dtype):
            return w_int.astype(dtype) * jnp.asarray(SCALE, dtype)
        key = jax.random.key(seed)
        k_x, k_g, k_u, k_d = jax.random.split(key, 4)
        x = jax.random.normal(k_x, (4, 256, DIM), dtype=jnp.float32)
        w_gate = jax.random.randint(k_g, (HIDDEN, DIM), -127, 128, dtype=jnp.int32)
        w_up = jax.random.randint(k_u, (HIDDEN, DIM), -127, 128, dtype=jnp.int32)
        w_down = jax.random.randint(k_d, (DIM, HIDDEN), -127, 128, dtype=jnp.int32)
        return {'x': x, 'w_gate': w_gate, 'w_up': w_up, 'w_down': w_down}
    _L1_ffn_in = _L1_ffn_setup()
    _d = {'L0_attn_x': _L0_attn_in['x'], 'L0_attn_w_kv_down': _L0_attn_in['w_kv_down'], 'L0_attn_w_kv_up': _L0_attn_in['w_kv_up'], 'L0_attn_w_q': _L0_attn_in['w_q'], 'L0_attn_w_out': _L0_attn_in['w_out'], 'L0_ffn_ln1_g': _L0_ffn_in['ln1_g'], 'L0_ffn_ln1_b': _L0_ffn_in['ln1_b'], 'L0_ffn_Wqkv': _L0_ffn_in['Wqkv'], 'L0_ffn_Wproj': _L0_ffn_in['Wproj'], 'L0_ffn_ln2_g': _L0_ffn_in['ln2_g'], 'L0_ffn_ln2_b': _L0_ffn_in['ln2_b'], 'L0_ffn_Wgate': _L0_ffn_in['Wgate'], 'L0_ffn_W1': _L0_ffn_in['W1'], 'L0_ffn_b1': _L0_ffn_in['b1'], 'L0_ffn_W2': _L0_ffn_in['W2'], 'L0_ffn_b2': _L0_ffn_in['b2'], 'L1_attn_Wq': _L1_attn_in['Wq'], 'L1_attn_Wk': _L1_attn_in['Wk'], 'L1_attn_Wv': _L1_attn_in['Wv'], 'L1_attn_Wo': _L1_attn_in['Wo'], 'L1_attn_bo': _L1_attn_in['bo'], 'L1_ffn_w_gate': _L1_ffn_in['w_gate'], 'L1_ffn_w_up': _L1_ffn_in['w_up'], 'L1_ffn_w_down': _L1_ffn_in['w_down']}
    _x0 = _d['L0_attn_x']
    _d['L0_attn_x'] = jax.random.normal(jax.random.fold_in(jax.random.key(seed), 1), (4, 512, 128), dtype=_x0.dtype)
    del _x0
    return _d

def reference(L0_attn_x, L0_attn_w_kv_down, L0_attn_w_kv_up, L0_attn_w_q, L0_attn_w_out, L0_ffn_ln1_g, L0_ffn_ln1_b, L0_ffn_Wqkv, L0_ffn_Wproj, L0_ffn_ln2_g, L0_ffn_ln2_b, L0_ffn_Wgate, L0_ffn_W1, L0_ffn_b1, L0_ffn_W2, L0_ffn_b2, L1_attn_Wq, L1_attn_Wk, L1_attn_Wv, L1_attn_Wo, L1_attn_bo, L1_ffn_w_gate, L1_ffn_w_up, L1_ffn_w_down):

    def _L0_attn_ref(x, w_kv_down, w_kv_up, w_q, w_out):
        import jax, jax.numpy as jnp
        import numpy as np
        B, T, C = (64, 32, 128)
        N_HEAD, HEAD_SIZE, KV_RANK = (16, 64, 128)
        BLOCK_SIZE = 32
        Bx, Tx, Cx = x.shape
        HD = N_HEAD * HEAD_SIZE
        latent_kv = x @ w_kv_down
        kv = latent_kv @ w_kv_up
        k, v = (kv[..., :HD], kv[..., HD:])
        k = k.reshape(Bx, Tx, N_HEAD, HEAD_SIZE)
        v = v.reshape(Bx, Tx, N_HEAD, HEAD_SIZE)
        q = (x @ w_q).reshape(Bx, Tx, N_HEAD, HEAD_SIZE)
        scale = HEAD_SIZE ** (-0.5)
        att = jnp.einsum('bqhd,bkhd->bhqk', q, k) * scale
        causal = jnp.tril(jnp.ones((Tx, Tx), dtype=bool))
        att = jnp.where(causal, att, -jnp.inf)
        att = jax.nn.softmax(att, axis=-1)
        y = jnp.einsum('bhqk,bkhd->bqhd', att, v)
        y = y.reshape(Bx, Tx, HD)
        return y @ w_out

    def _L0_ffn_ref(x, ln1_g, ln1_b, Wqkv, Wproj, ln2_g, ln2_b, Wgate, W1, b1, W2, b2):
        import jax, jax.numpy as jnp
        import numpy as np
        import math
        B, T, D, H, E, TOPK, CAPF = (4, 256, 128, 16, 8, 2, 2.0)
        HD = D // H

        def layernorm(x, g, b, eps=1e-05):
            m = jnp.mean(x, -1, keepdims=True)
            v = jnp.mean(jnp.square(x - m), -1, keepdims=True)
            return (x - m) * jax.lax.rsqrt(v + eps) * g + b

        def block_forward(x, ln1_g, ln1_b, Wqkv, Wproj, ln2_g, ln2_b, Wgate, W1, b1, W2, b2):
            Bb, Tt, d = x.shape
            hd = HD
            half = hd // 2
            h = layernorm(x, ln1_g, ln1_b)
            qkv = (h @ Wqkv).reshape(Bb, Tt, H, 3 * hd)
            q, k, v = (qkv[..., :hd], qkv[..., hd:2 * hd], qkv[..., 2 * hd:])
            inv_freq = 1.0 / 10000.0 ** (jnp.arange(0, hd, 2, dtype=jnp.float32) / hd)
            ang = jnp.arange(Tt, dtype=jnp.float32)[:, None] * inv_freq
            sin = jnp.sin(ang)[None, :, None, :].astype(x.dtype)
            cos = jnp.cos(ang)[None, :, None, :].astype(x.dtype)

            def rope(t):
                t1, t2 = (t[..., :half], t[..., half:])
                return jnp.concatenate([t1 * cos - t2 * sin, t1 * sin + t2 * cos], -1)
            q, k = (rope(q), rope(k))
            scores = jnp.einsum('bqhd,bkhd->bhqk', q, k) / math.sqrt(hd)
            causal = jnp.tril(jnp.ones((Tt, Tt), dtype=bool))
            scores = jnp.where(causal, scores, jnp.asarray(-1000000000.0, scores.dtype))
            probs = jax.nn.softmax(scores, axis=-1)
            attn = jnp.einsum('bhqk,bkhd->bqhd', probs, v).reshape(Bb, Tt, d) @ Wproj
            x = x + attn
            h2 = layernorm(x, ln2_g, ln2_b)
            flat = h2.reshape(-1, d)
            N = flat.shape[0]
            capacity = int(math.ceil(CAPF * N / E))
            gates = jax.nn.softmax((flat @ Wgate).astype(jnp.float32), -1).astype(flat.dtype)
            _, top_inds = jax.lax.top_k(gates, TOPK)
            mask = jnp.zeros((N, E), dtype=bool).at[jnp.arange(N)[:, None], top_inds].set(True)
            pos = jnp.cumsum(mask.astype(jnp.int32), axis=0) * mask - 1
            keep = (pos < capacity) & mask
            t_flat = jnp.repeat(jnp.arange(N), TOPK)
            e_flat = top_inds.reshape(-1)
            p = pos[t_flat, e_flat]
            kp = keep[t_flat, e_flat]
            p_eff = jnp.where(kp, p, capacity)
            exp_in = jnp.zeros((E, capacity, d), flat.dtype).at[e_flat, p_eff].set(flat[t_flat], mode='drop')
            hmid = jax.nn.gelu(jnp.einsum('ecd,edf->ecf', exp_in, W1) + b1[:, None, :], approximate=False)
            exp_out = jnp.einsum('ecf,efd->ecd', hmid, W2) + b2[:, None, :]
            gate = gates[t_flat, e_flat] * kp.astype(flat.dtype)
            p_g = jnp.minimum(p_eff, capacity - 1)
            moe = jnp.zeros((N, d), flat.dtype).at[t_flat].add(exp_out[e_flat, p_g] * gate[:, None])
            return x + moe.reshape(Bb, Tt, d)
        return block_forward(x, ln1_g, ln1_b, Wqkv, Wproj, ln2_g, ln2_b, Wgate, W1, b1, W2, b2)

    def _L1_attn_ref(x, Wq, Wk, Wv, Wo, bo):
        import jax, jax.numpy as jnp
        import numpy as np
        D_IN = 128
        D_OUT = 128
        NUM_HEADS = 16
        HEAD_DIM = D_OUT // NUM_HEADS
        b, n, _ = x.shape

        def split_heads(t):
            return t.reshape(b, n, NUM_HEADS, HEAD_DIM).transpose(0, 2, 1, 3)
        q = split_heads(x @ Wq)
        k = split_heads(x @ Wk)
        v = split_heads(x @ Wv)
        scores = jnp.einsum('bhqd,bhkd->bhqk', q, k) / jnp.sqrt(jnp.float32(HEAD_DIM))
        causal = jnp.tril(jnp.ones((n, n), dtype=bool))
        scores = jnp.where(causal, scores, -jnp.inf)
        attn = jax.nn.softmax(scores, axis=-1)
        ctx = jnp.einsum('bhqk,bhkd->bhqd', attn, v)
        ctx = ctx.transpose(0, 2, 1, 3).reshape(b, n, D_OUT)
        return ctx @ Wo + bo

    def _L1_ffn_ref(x, w_gate, w_up, w_down):
        import jax, jax.numpy as jnp
        import numpy as np
        DIM = 128
        HIDDEN = 384
        SCALE = 1.0 / 127.0

        def _dequant(w_int, dtype):
            return w_int.astype(dtype) * jnp.asarray(SCALE, dtype)
        wg = _dequant(w_gate, x.dtype)
        wu = _dequant(w_up, x.dtype)
        wd = _dequant(w_down, x.dtype)
        gate = jnp.einsum('bsd,hd->bsh', x, wg)
        up = jnp.einsum('bsd,hd->bsh', x, wu)
        h = jax.nn.silu(gate) * up
        return jnp.einsum('bsh,dh->bsd', h, wd)
    x = L0_attn_x
    x = x + _L0_attn_ref(_layernorm(x, axis=-1), L0_attn_w_kv_down, L0_attn_w_kv_up, L0_attn_w_q, L0_attn_w_out)
    x = x + _L0_ffn_ref(_layernorm(x, axis=-1), L0_ffn_ln1_g, L0_ffn_ln1_b, L0_ffn_Wqkv, L0_ffn_Wproj, L0_ffn_ln2_g, L0_ffn_ln2_b, L0_ffn_Wgate, L0_ffn_W1, L0_ffn_b1, L0_ffn_W2, L0_ffn_b2)
    x = x + _L1_attn_ref(_layernorm(x, axis=-1), L1_attn_Wq, L1_attn_Wk, L1_attn_Wv, L1_attn_Wo, L1_attn_bo)
    x = x + _L1_ffn_ref(_layernorm(x, axis=-1), L1_ffn_w_gate, L1_ffn_w_up, L1_ffn_w_down)
    return x

_drawn_inputs = setup_inputs


def setup_inputs(seed=0):
    import zlib

    import numpy as np

    out = dict(_drawn_inputs(seed))
    spreads = {'L0_ffn_ln1_g': (1.0, 0.6),
     'L0_ffn_ln1_b': (0.0, 0.8),
     'L0_ffn_ln2_g': (1.0, 0.6),
     'L0_ffn_ln2_b': (0.0, 0.8),
     'L0_ffn_b1': (0.0, 0.8),
     'L0_ffn_b2': (0.0, 0.521)}
    factors = {'L0_attn_w_q': 6.536,
     'L0_ffn_Wqkv': 8.0,
     'L0_ffn_Wproj': 8.0,
     'L0_ffn_Wgate': 3.593,
     'L0_ffn_W1': 6.419,
     'L0_ffn_W2': 5.886,
     'L1_attn_Wq': 8.0,
     'L1_attn_Wk': 8.0,
     'L1_attn_Wv': 8.0,
     'L1_attn_Wo': 8.0,
     'L1_attn_bo': 10.362}
    for name, (base, spread) in spreads.items():
        noise = np.random.default_rng([zlib.crc32(name.encode()), seed]).standard_normal(out[name].shape)
        drawn = base * np.exp(spread * noise) if base else spread * noise
        out[name] = jnp.asarray(drawn.astype(out[name].dtype))
    for name, factor in factors.items():
        out[name] = (out[name] * factor).astype(out[name].dtype)
    return out
```

```python
from contextlib import ExitStack

import numpy as np

import concourse.bass as bass
from concourse import mybir

F32 = mybir.dt.float32
BF16 = mybir.dt.bfloat16
I32 = mybir.dt.int32
ALU = mybir.AluOpType
ACT = mybir.ActivationFunctionType
AX_X = mybir.AxisListType.X

P = 128
B, T, C = 4, 512, 128
TILES = T // P
HEADS = 16
HD_A = 64
HD_S = C // HEADS
PIECES = 3
STACK = PIECES * PIECES * HD_S
EXPERTS, FFN, CAP = 8, 512, 512
FT = FFN // P
HID = 384
HT = HID // P
EPS = 1e-5
GROUP = 4
PAIR_TILES = 5
ST_TILES = HEADS // 2 * PAIR_TILES
GROUP_TILES = GROUP // 2 * PAIR_TILES
AHEAD = 13
CONSTS, TABLES = 4, 5
LAG = 2
P_RING = 5
ST_BANKS = 3
PV_BANKS = 2
WORK_BANKS = 3


def pair_tile(n):
    a, k = 2 * (n // PAIR_TILES), n % PAIR_TILES
    return [
        [(a, 0, 0, 512)],
        [(a, 1, 0, 384), (a, 3, 384, 128)],
        [(a + 1, 0, 0, 512)],
        [(a, 2, 0, 256), (a + 1, 2, 256, 256)],
        [(a + 1, 1, 0, 384), (a + 1, 3, 384, 128)],
    ][k]


def max_tile(m):
    a, k = 2 * (m // PAIR_TILES), m % PAIR_TILES
    return [
        [(a, 3, 0, 512)],
        [(a, 2, 0, 384), (a, 0, 384, 128)],
        [(a + 1, 3, 0, 512)],
        [(a, 1, 0, 256), (a + 1, 1, 256, 256)],
        [(a + 1, 2, 0, 384), (a + 1, 0, 384, 128)],
    ][k]


class Tally:

    def __init__(self, sem, per, start=0):
        self.sem, self.per, self.start = sem, per, start

    def at(self, b, k):
        return b * self.per + (self.start + k)


class Work:

    def __init__(self, names, ready, free):
        self.names = names
        self.ready = Tally(ready, len(names))
        uses = [len(range(k, len(names), WORK_BANKS)) for k in range(WORK_BANKS)]
        self.free = [Tally(s, u, 1) for s, u in zip(free, uses)]
        self.index = {name: n for n, name in enumerate(names)}

    def bank(self, name):
        return self.index[name] % WORK_BANKS

    def wait_free(self, eng, b, name):
        n = self.index[name]
        t = self.free[n % WORK_BANKS]
        eng.wait_ge(t.sem, t.at(b, n // WORK_BANKS))

    def wait_copied(self, eng, b, name):
        n = self.index[name]
        t = self.free[n % WORK_BANKS]
        eng.wait_ge(t.sem, t.at(b, n // WORK_BANKS + 1))

    def wait_ready(self, eng, b, name):
        eng.wait_ge(self.ready.sem, self.ready.at(b, self.index[name] + 1))


def attention_tail():
    names = []
    for n in range(ST_TILES + LAG):
        if n + AHEAD < ST_TILES:
            names.append(f"max{n + AHEAD}")
        if n % GROUP_TILES == GROUP_TILES - 2 and n // GROUP_TILES + 1 < HEADS // GROUP:
            names.append(f"turn{n // GROUP_TILES + 1}")
    return names + ["out"]


def attention_head():
    return [f"max{m}" for m in range(GROUP_TILES)] + [f"max{m}" for m in range(GROUP_TILES, AHEAD)] + ["turn0"]


def program(nc, x, w_down, w_upv, w_qT, w_kT, w_out, ln1g, ln1b, b_wq, b_wqr, b_wk, b_wkr, b_wv, b_wo,
            ln2g, ln2b, w_gate, w1, b1, w2, b2, c_wq, c_wk, c_wv, c_wo, c_bo, f_gate, f_up, f_down,
            ident_d, mask_d, maskT_d, cos_d, sin_d, sel_d, tri_d, order_d, out):
    with ExitStack() as ctx:
        def sb(name, shape, dt=F32):
            return ctx.enter_context(nc.sbuf_tensor(name, shape, dt))

        def sem(name):
            return ctx.enter_context(nc.semaphore(name))

        work = [ctx.enter_context(nc.psum_tensor(f"work{k}", [P, 512], F32)) for k in range(WORK_BANKS)]
        st = [ctx.enter_context(nc.psum_tensor(f"scores{k}", [P, 512], F32)) for k in range(ST_BANKS)]
        pv = [ctx.enter_context(nc.psum_tensor(f"values{k}", [P, 512], F32)) for k in range(PV_BANKS)]

        X = sb("X", [P, B * TILES, C])
        U = sb("U", [P, B * TILES, C])
        H = sb("H", [P, TILES, C])
        stats = sb("stats", [P, TILES, 6])
        mean = sb("mean", [P, TILES, 4])
        mv = sb("mv", [P, TILES, 2])
        Ub = sb("Ub", [P, TILES, C])
        veps = sb("veps", [P, TILES])
        rstd = sb("rstd", [P, TILES])
        neghalf = sb("neghalf", [P, TILES])
        hT = sb("hT", [P, T])
        latT = sb("latT", [P, T])
        yT = sb("yT", [P, HEADS // 2, T])
        rsum = sb("rsum", [P, T])
        QP = sb("QP", [P, HEADS, T])
        QK = QP[:, :, :].bitcast(BF16).rearrange("p h (s t) -> p s h t", s=2)
        QS, KS = QK[:, 0], QK[:, 1]
        V = sb("V", [P, TILES * 2 * 1152])
        VA = V[:, 0:TILES * HEADS * P].rearrange("p (i h c) -> p i h c", i=TILES, h=HEADS)
        VS = V[:, :].rearrange("p (i s c) -> p i s c", i=TILES, s=2)
        PT = sb("PT", [P, P_RING, 512])
        MX = sb("MX", [P, 2, TILES, GROUP])
        MR = sb("MR", [P, TILES, GROUP])
        MS = sb("MS", [P, TILES, P], BF16)
        MT = sb("MT", [P, 2, T], BF16)
        rot = sb("rot", [P, 2, T])
        piece = sb("piece", [P, 2, PIECES, T], BF16)
        qk = sb("qk", [P, 2, T])
        identf = sb("identf", [P, P])
        identb = sb("identb", [P, P], BF16)
        maskb = sb("maskb", [P, P], BF16)
        maskTb = sb("maskTb", [P, P], BF16)
        selb = sb("selb", [P, GROUP, P], BF16)
        cos = sb("cos", [P, T])
        sin = sb("sin", [P, T])
        trib = sb("trib", [P, P], BF16)
        onesb = sb("onesb", [P, P], BF16)
        Wd = sb("Wd", [P, P])
        early = sb("early", [P, HEADS * (P + HD_A)])
        M = early[:, 0:HEADS * P].rearrange("p (h c) -> p h c", h=HEADS)
        Wv = early[:, HEADS * P:]
        Wo = sb("Wo", [P, HEADS // 2, C])
        WqT = yT[:, 0:2, :].rearrange("p a (b c) -> p (a b) c", c=C)
        WkT = yT[:, 2:4, :].rearrange("p a (b c) -> p (a b) c", c=C)
        small = sb("small", [P, 10, C])
        BWq, BWqr, BWk, BWkr, BWv, BWo, CWq, CWk, CWv, CWo = [small[:, k, :] for k in range(10)]
        bos = sb("bos", [P, TILES, C])
        ln = sb("ln", [P, 4])
        Wg = sb("Wg", [P, EXPERTS])
        W1 = sb("W1", [P, EXPERTS, FFN])
        b1s = sb("b1s", [P, EXPERTS, FT])
        W2 = sb("W2", [P, EXPERTS * FT, C])
        b2s = sb("b2s", [EXPERTS, C])
        WfI = early[:, 0:3 * HID].bitcast(I32)
        Wf = early[:, 3 * HID:6 * HID]
        hidF = yT[:, 0:HT, :]
        siluF = yT[:, HT:2 * HT, :]
        lg = sb("lg", [P, TILES, EXPERTS])
        lmax = sb("lmax", [P, TILES])
        lsum = sb("lsum", [P, TILES])
        gates = sb("gates", [P, TILES, EXPERTS])
        rank = sb("rank", [P, TILES, EXPERTS])
        order = sb("order", [P, TILES, EXPERTS])
        gsel = sb("gsel", [P, TILES, EXPERTS])
        maskf = sb("maskf", [P, TILES, EXPERTS])
        before = sb("before", [P, TILES + 1, EXPERTS])
        maskb16 = sb("maskb16", [P, TILES, EXPERTS], BF16)
        before16 = sb("before16", [P, TILES, EXPERTS], BF16)
        keep = sb("keep", [P, TILES, EXPERTS])
        ge = sb("ge", [P, TILES, EXPERTS])
        geT = sb("geT", [EXPERTS, TILES, P])
        acc = sb("acc", [P, TILES, C])

        scratch = nc.dram_tensor("scratch", [2, PIECES, HEADS, HD_S, T], BF16).ap()

        loaded_x, loaded_a, loaded_const = sem("loaded_x"), sem("loaded_a"), sem("loaded_const")
        loaded_tables = sem("loaded_tables")
        loaded_b, loaded_moe, loaded_f = sem("loaded_b"), sem("loaded_moe"), sem("loaded_f")
        setup = sem("setup")
        folded, fold_free = sem("folded"), sem("fold_free")
        zeroed = sem("zeroed")
        stored = sem("stored")
        ffn_weights = sem("ffn_weights")

        class Stage:

            def __init__(self, tag, names, dve_steps, pv_uses=0, norms=1):
                self.work = Work(names, sem(f"{tag}_product_ready"),
                                 [sem(f"{tag}_bank{k}_free") for k in range(WORK_BANKS)])
                self.var = Tally(sem(f"{tag}_variance_ready"), norms)
                self.rstd = Tally(sem(f"{tag}_rstd_ready"), norms)
                self.normed = Tally(sem(f"{tag}_normed"), 1)
                self.step = Tally(sem(f"{tag}_vector_step"), dve_steps)
                self.done = Tally(sem(f"{tag}_batch_done"), 1)
                if pv_uses:
                    self.scores = Tally(sem(f"{tag}_scores_ready"), ST_TILES)
                    self.probs = Tally(sem(f"{tag}_probs_ready"), ST_TILES, ST_BANKS)
                    self.pv = Tally(sem(f"{tag}_probs_used"), ST_TILES, P_RING)
                    self.y = Tally(sem(f"{tag}_y_ready"), pv_uses, PV_BANKS)
                    self.pieces = Tally(sem(f"{tag}_maxima_split"), HEADS // GROUP)

        a_names = ["hT", "lat"]
        for h in range(HEADS):
            if 2 <= h < 2 + 2 * TILES:
                a_names.append(f"v{h - 2}")
            a_names.append(f"q{h}")
        a_names += attention_head() + attention_tail()

        def s_names(rope):
            return (["hT"] + (["q", "qr", "k", "kr"] if rope else ["q", "k"]) + ["v"]
                    + attention_head() + attention_tail())

        m_names = ["hT", "logits", "count", "gT", "b2"] + [f"h{e}.{f}" for e in range(EXPERTS) for f in range(FT)]
        f_names = ["hT"] + [f"{w}{f}" for f in range(HT) for w in "gu"] + ["out"]
        A = Stage("a", a_names, 31, HEADS)
        SB = Stage("b", s_names(True), 29, 2, 2)
        M_ = Stage("m", m_names, 25)
        SC = Stage("c", s_names(False), 23, 2)
        F_ = Stage("f", f_names, 3)
        s_split = {"b": Tally(sem("b_pieces_ready"), 2), "c": Tally(sem("c_pieces_ready"), 2)}
        s_spilt = {"b": Tally(sem("b_pieces_in_dram"), 32), "c": Tally(sem("c_pieces_in_dram"), 32)}
        s_stack = {"b": Tally(sem("b_stacks_ready"), 16 * 18), "c": Tally(sem("c_stacks_ready"), 16 * 18)}
        m_exp = Tally(sem("m_exp_ready"), 1)
        m_masks = Tally(sem("m_masks_ready"), 1)
        m_gate = Tally(sem("m_gates_ready"), 1)
        m_out = Tally(sem("m_expert_ready"), EXPERTS)
        m_acc = Tally(sem("m_expert_added"), EXPERTS, PV_BANKS)
        stages = [A, SB, M_, SC, F_]

        def hid2(e):
            return yT[:, e % 2 * FT:(e % 2 + 1) * FT, :]

        def value_blocks(k):
            i, half = k // 2, k % 2
            dst = VA[:, i, half * 8:(half + 1) * 8, :].rearrange("p (a b) c -> p a (b c)", b=2)
            dst = dst.rearrange("p a (q c) -> p a q c", c=HD_A)[:, :, 0:4:3, :]
            src = work[A.work.bank(f"v{k}")][:, :].rearrange("p (a q c) -> p a q c", q=2, c=HD_A)
            return dst, src

        block = ctx.enter_context(nc.Block())

        @block.sync
        def _(sp):
            for s in stages:
                for t in s.work.free:
                    sp.sem_inc(t.sem, t.start)
            for s in (A, SB, SC):
                for t in (s.probs, s.pv, s.y):
                    sp.sem_inc(t.sem, t.start)
            sp.sem_inc(m_acc.sem, m_acc.start)
            sp.sem_inc(fold_free, WORK_BANKS)
            sp.dma_start(X[:, :, :], x.rearrange("(t p) c -> p t c", p=P)).then_inc(loaded_x, 16)
            for dst, src in ((identf[:, :], ident_d), (cos[:, :], cos_d), (sin[:, :], sin_d),
                             (order[:, :, :], order_d)):
                sp.dma_start(dst, src).then_inc(loaded_const, 16)
            for dst, src in ((WqT, w_qT.rearrange("(a p) c -> p a c", p=P)),
                             (WkT, w_kT.rearrange("(a p) c -> p a c", p=P)),
                             (Wd[:, :], w_down), (Wv[:, :], w_upv),
                             (Wo[:, :, :], w_out.rearrange("(a p) c -> p a c", p=P))):
                sp.dma_start(dst, src).then_inc(loaded_a, 16)
            for dst, src in ((BWq, b_wq), (BWqr, b_wqr), (BWk, b_wk), (BWkr, b_wkr), (BWv, b_wv), (BWo, b_wo),
                             (CWq, c_wq), (CWk, c_wk), (CWv, c_wv), (CWo, c_wo),
                             (bos[:, :, :], c_bo.to_broadcast([P, TILES, C])),
                             (ln[:, 0:1], ln1g), (ln[:, 1:2], ln1b), (ln[:, 2:3], ln2g), (ln[:, 3:4], ln2b)):
                sp.dma_start(dst, src).then_inc(loaded_b, 16)
            for dst, src in ((Wg[:, :], w_gate), (W1[:, :, :], w1.rearrange("e d f -> d e f")),
                             (b1s[:, :, :], b1.rearrange("p (e f) -> p e f", e=EXPERTS)),
                             (W2[:, :, :], w2.rearrange("(a p) c -> p a c", p=P)), (b2s[:, :], b2)):
                sp.dma_start(dst, src).then_inc(loaded_moe, 16)

            def stack_pieces(tag):
                with sp.Fori(0, B) as b:
                    for w in range(2):
                        sp.wait_ge(s_split[tag].sem, s_split[tag].at(b, w + 1))
                        sp.dma_start(scratch[w].rearrange("g h d t -> (h d) g t"), piece[:, w, :, :]
                                     ).then_inc(s_spilt[tag].sem, 16)
                        sp.wait_ge(s_spilt[tag].sem, s_spilt[tag].at(b, 16 * (w + 1)))
                        for r in range(PIECES):
                            for g in range(PIECES):
                                row = (r * PIECES + g) * HD_S
                                dst = (QS, KS)[w][row:row + HD_S, :, :]
                                src = scratch[w, (g, r)[w]].rearrange("h d t -> d h t")
                                sp.dma_start(dst, src).then_inc(s_stack[tag].sem, 16)

            stack_pieces("b")
            A.work.wait_copied(sp, B - 1, "out")
            for dst, src in ((WfI[:, 0:HID], f_gate), (WfI[:, HID:2 * HID], f_up),
                             (WfI[:, 2 * HID:3 * HID].rearrange("p (a c) -> p a c", c=C),
                              f_down.rearrange("(a p) c -> p a c", p=P))):
                sp.dma_start(dst, src).then_inc(loaded_f, 16)
            stack_pieces("c")
            with sp.Fori(0, B) as b:
                F_.work.wait_copied(sp, b, "out")
                sp.dma_start(out.rearrange("(t p) c -> p t c", p=P)[:, bass.ds(b * TILES, TILES), :],
                             X[:, bass.ds(b * TILES, TILES), :]).then_inc(stored, 16)
            sp.wait_ge(stored, 16 * B)

        @block.gpsimd
        def _(pool):
            for dst, src in ((identb[:, :], ident_d), (maskb[:, :], mask_d), (maskTb[:, :], maskT_d),
                             (selb[:, :, :], sel_d), (trib[:, :], tri_d)):
                pool.dma_start(dst, src).then_inc(loaded_tables, 16)
            nc.gpsimd.memset(neghalf[:, :], -0.5).then_inc(setup, 1)
            nc.gpsimd.memset(VA, 1.0).then_inc(setup, 1)
            nc.gpsimd.memset(MS[:, :, :], 0.0).then_inc(setup, 1)
            nc.gpsimd.memset(onesb[:, :], 1.0).then_inc(setup, 1)
            nc.gpsimd.memset(before[:, 0, :], 0.0).then_inc(setup, 1)
            pool.wait_ge(setup, 5)

            def inverse_root(s, b, k):
                pool.wait_ge(s.var.sem, s.var.at(b, k + 1))
                nc.gpsimd.tensor_tensor(rstd[:, :], veps[:, :], neghalf[:, :], ALU.pow).then_inc(s.rstd.sem, 1)

            with pool.Fori(0, B) as b:
                inverse_root(A, b, 0)
            A.work.wait_copied(pool, B - 1, "out")
            nc.gpsimd.memset(V[:, :], 0.0).then_inc(zeroed, 1)
            pool.wait_ge(zeroed, 1)
            for i in range(TILES):
                for s in range(2):
                    stripes = VS[:, i, s, 64 - 64 * s:64 - 64 * s + 8 * 136].rearrange("p (h c) -> p h c", c=136)
                    nc.gpsimd.memset(stripes[:, :, 0:HD_S], 1.0).then_inc(zeroed, 1)
            with pool.Fori(0, B) as b:
                inverse_root(SB, b, 0)
                inverse_root(SB, b, 1)
            for s in (M_, SC, F_):
                with pool.Fori(0, B) as b:
                    inverse_root(s, b, 0)

        @block.tensor
        def _(pe):
            def turn_h(s, b):
                pe.wait_ge(s.normed.sem, s.normed.at(b, 1))
                s.work.wait_free(pe, b, "hT")
                for i in range(TILES):
                    last = pe.transpose(work[s.work.bank("hT")][:, i * P:(i + 1) * P], H[:, i, :], identf[:, :])
                last.then_inc(s.work.ready.sem, 1)

            def product(s, b, name, lhsT, rhs):
                s.work.wait_free(pe, b, name)
                pe.matmul(work[s.work.bank(name)][:, :], lhsT, rhs, start=True, stop=True
                          ).then_inc(s.work.ready.sem, 1)

            def max_scores(s, b, m, q_of, k_of):
                name = f"max{m}"
                s.work.wait_free(pe, b, name)
                bank = work[s.work.bank(name)]
                for h, i, c, w in max_tile(m):
                    pe.matmul(bank[:, c:c + w], q_of(h, i * P, (i + 1) * P), k_of(h, 0, w), start=True, stop=False)
                    last = pe.matmul(bank[:, c + w - P:c + w], identb[:, :], maskb[:, :], start=False, stop=True)
                last.then_inc(s.work.ready.sem, 1)

            def turn_max(s, b, g):
                pe.wait_ge(s.pieces.sem, s.pieces.at(b, g + 1))
                s.work.wait_free(pe, b, f"turn{g}")
                bank = work[s.work.bank(f"turn{g}")][:, :].bitcast(BF16)
                for i in range(TILES):
                    last = pe.transpose(bank[:, i * P:(i + 1) * P], MS[:, i, :], identb[:, :])
                last.then_inc(s.work.ready.sem, 1)

            def scores(s, b, n, q_of, k_of):
                g = n // GROUP_TILES
                if n % GROUP_TILES == 0:
                    s.work.wait_copied(pe, b, f"turn{g}")
                pe.wait_ge(s.probs.sem, s.probs.at(b, max(n - ST_BANKS + 1, 0)))
                bank = st[n % ST_BANKS]
                for h, j, c, w in pair_tile(n):
                    q0 = j * P
                    pe.matmul(bank[:, c:c + w], k_of(h, q0, q0 + P), q_of(h, q0, q0 + w), start=True, stop=False)
                    pe.matmul(bank[:, c:c + P], identb[:, :], maskTb[:, :], start=False, stop=False)
                    last = pe.matmul(bank[:, c:c + w], selb[:, h % GROUP, :], MT[:, g % 2, q0:q0 + w],
                                     start=False, stop=True)
                last.then_inc(s.scores.sem, 1)

            def values(s, b, n, v_of, per_bank):
                pe.wait_ge(s.probs.sem, s.probs.at(b, n + 1))
                for h, j, c, w in pair_tile(n):
                    use = h // per_bank
                    first = j == 0 and h % per_bank == 0
                    if first:
                        pe.wait_ge(s.y.sem, s.y.at(b, use - PV_BANKS + 1))
                    final = h % per_bank == per_bank - 1 and (j == 2 if h % 2 == 0 else j == 3)
                    last = pe.matmul(pv[use % PV_BANKS][:, T - w:T], v_of(h, j), PT[:, n % P_RING, c:c + w],
                                     start=first, stop=final)
                last.then_inc(s.pv.sem, 1)

            def attention(s, b, q_of, k_of, v_of, per_bank):
                for m in range(AHEAD):
                    max_scores(s, b, m, q_of, k_of)
                turn_max(s, b, 0)
                for n in range(ST_TILES + LAG):
                    if n < ST_TILES:
                        scores(s, b, n, q_of, k_of)
                    if n + AHEAD < ST_TILES:
                        max_scores(s, b, n + AHEAD, q_of, k_of)
                    if n % GROUP_TILES == GROUP_TILES - 2 and n // GROUP_TILES + 1 < HEADS // GROUP:
                        turn_max(s, b, n // GROUP_TILES + 1)
                    if n >= LAG:
                        values(s, b, n - LAG, v_of, per_bank)

            def output(s, b, rows):
                pe.wait_ge(s.y.sem, s.y.at(b, s.y.per))
                s.work.wait_free(pe, b, "out")
                bank = work[s.work.bank("out")]
                for i in range(TILES):
                    for k, (y, w) in enumerate(rows):
                        last = pe.matmul(bank[:, i * C:(i + 1) * C], y[:, i * P:(i + 1) * P], w,
                                         start=k == 0, stop=k == len(rows) - 1)
                last.then_inc(s.work.ready.sem, 1)

            pe.wait_ge(loaded_a, 16 * 5)
            pe.wait_ge(loaded_const, 16 * CONSTS)
            pe.wait_ge(loaded_tables, 16 * TABLES)
            pe.wait_ge(setup, 5)
            for h in range(HEADS):
                if h >= WORK_BANKS:
                    pe.wait_ge(fold_free, h + 1)
                r = slice(64 * (h % 2), 64 * (h % 2) + 64)
                pe.matmul(work[h % WORK_BANKS][:, 0:P], WqT[r, h // 2, :], WkT[r, h // 2, :],
                          start=True, stop=True).then_inc(folded, 1)

            pe.wait_ge(fold_free, HEADS + WORK_BANKS)
            with pe.Fori(0, B) as b:
                turn_h(A, b)
                A.work.wait_copied(pe, b, "hT")
                product(A, b, "lat", Wd[:, :], hT[:, :])
                for h in range(HEADS):
                    if h == 2:
                        A.work.wait_copied(pe, b, "lat")
                    if 2 <= h < 2 + 2 * TILES:
                        k = h - 2
                        product(A, b, f"v{k}", latT[:, k // 2 * P:(k // 2 + 1) * P],
                                Wv[:, k % 2 * 512:(k % 2 + 1) * 512])
                    product(A, b, f"q{h}", M[:, h, :], hT[:, :])
                for h in (HEADS - 3, HEADS - 2, HEADS - 1):
                    A.work.wait_copied(pe, b, f"q{h}")
                attention(A, b, lambda h, c0, c1: QP[:, h, c0:c1], lambda h, c0, c1: latT[:, c0:c1],
                          lambda h, j: VA[:, j, h, :], 1)
                output(A, b, [(yT[:, k, :], Wo[:, k, :]) for k in range(HEADS // 2)])

            def small_attention(s, tag, names, wv, wo):
                with pe.Fori(0, B) as b:
                    turn_h(s, b)
                    s.work.wait_copied(pe, b, "hT")
                    for name, w in names:
                        product(s, b, name, w, hT[:, :])
                    s.work.wait_free(pe, b, "v")
                    for i in range(TILES):
                        last = pe.matmul(work[s.work.bank("v")][:, i * C:(i + 1) * C], hT[:, i * P:(i + 1) * P], wv,
                                         start=True, stop=True)
                    last.then_inc(s.work.ready.sem, 1)
                    s.work.wait_copied(pe, b, "v")
                    pe.wait_ge(s_stack[tag].sem, s_stack[tag].at(b, 16 * 18))
                    attention(s, b, lambda h, c0, c1: QS[0:STACK, h, c0:c1], lambda h, c0, c1: KS[0:STACK, h, c0:c1],
                              lambda h, j: VS[:, j, h // 8, h % 8 * P:(h % 8 + 1) * P], 8)
                    output(s, b, [(yT[:, 0, :], wo)])

            pe.wait_ge(loaded_b, 16 * 15)
            pe.wait_ge(zeroed, 1 + 2 * TILES)
            small_attention(SB, "b", (("q", BWq), ("qr", BWqr), ("k", BWk), ("kr", BWkr)), BWv, BWo)

            pe.wait_ge(loaded_moe, 16 * 5)
            with pe.Fori(0, B) as b:
                s = M_
                turn_h(s, b)
                s.work.wait_copied(pe, b, "hT")
                s.work.wait_free(pe, b, "logits")
                for i in range(TILES):
                    last = pe.matmul(work[s.work.bank("logits")][:, i * EXPERTS:(i + 1) * EXPERTS],
                                     hT[:, i * P:(i + 1) * P], Wg[:, :], start=True, stop=True)
                last.then_inc(s.work.ready.sem, 1)
                pe.wait_ge(m_masks.sem, m_masks.at(b, 1))
                s.work.wait_free(pe, b, "count")
                bank = work[s.work.bank("count")][:, 0:TILES * EXPERTS]
                pe.matmul(bank, trib[:, :], maskb16[:, :, :].rearrange("p i e -> p (i e)"), start=True, stop=False)
                pe.matmul(bank, onesb[:, :], before16[:, :, :].rearrange("p i e -> p (i e)"), start=False, stop=True
                          ).then_inc(s.work.ready.sem, 1)
                pe.wait_ge(m_gate.sem, m_gate.at(b, 1))
                s.work.wait_free(pe, b, "gT")
                for i in range(TILES):
                    last = pe.transpose(work[s.work.bank("gT")][0:EXPERTS, i * P:(i + 1) * P], ge[:, i, :], identf[:, :])
                last.then_inc(s.work.ready.sem, 1)
                s.work.wait_copied(pe, b, "gT")
                s.work.wait_free(pe, b, "b2")
                for i in range(TILES):
                    last = pe.matmul(work[s.work.bank("b2")][:, i * C:(i + 1) * C], geT[:, i, :], b2s[:, :],
                                     start=True, stop=True)
                last.then_inc(s.work.ready.sem, 1)

                def expert_out(e):
                    for f in range(FT):
                        s.work.wait_copied(pe, b, f"h{e}.{f}")
                    pe.wait_ge(m_acc.sem, m_acc.at(b, e - PV_BANKS + 1))
                    for i in range(TILES):
                        for f in range(FT):
                            last = pe.matmul(pv[e % PV_BANKS][:, i * C:(i + 1) * C],
                                             hid2(e)[:, f, i * P:(i + 1) * P], W2[:, e * FT + f, :],
                                             start=f == 0, stop=f == FT - 1)
                    last.then_inc(m_out.sem, 1)

                for e in range(EXPERTS):
                    for f in range(FT):
                        product(s, b, f"h{e}.{f}", W1[:, e, f * P:(f + 1) * P], hT[:, :])
                    if e >= 1:
                        expert_out(e - 1)
                expert_out(EXPERTS - 1)

            small_attention(SC, "c", (("q", CWq), ("k", CWk)), CWv, CWo)

            pe.wait_ge(ffn_weights, 1)
            with pe.Fori(0, B) as b:
                s = F_
                turn_h(s, b)
                s.work.wait_copied(pe, b, "hT")
                for f in range(HT):
                    product(s, b, f"g{f}", Wf[:, f * P:(f + 1) * P], hT[:, :])
                    product(s, b, f"u{f}", Wf[:, HID + f * P:HID + (f + 1) * P], hT[:, :])
                for f in range(HT):
                    s.work.wait_copied(pe, b, f"u{f}")
                s.work.wait_free(pe, b, "out")
                for i in range(TILES):
                    for f in range(HT):
                        last = pe.matmul(work[s.work.bank("out")][:, i * C:(i + 1) * C],
                                         hidF[:, f, i * P:(i + 1) * P],
                                         Wf[:, 2 * HID + f * C:2 * HID + (f + 1) * C], start=f == 0, stop=f == HT - 1)
                last.then_inc(s.work.ready.sem, 1)

        @block.scalar
        def _(act):
            def free(s, name):
                return s.work.free[s.work.bank(name)].sem

            def bank(s, name):
                return work[s.work.bank(name)]

            def exponentials(s, b, scale):
                for n in range(ST_TILES):
                    act.wait_ge(s.scores.sem, s.scores.at(b, n + 1))
                    act.wait_ge(s.pv.sem, s.pv.at(b, n - P_RING + 1))
                    nc.scalar.activation(PT[:, n % P_RING, :], st[n % ST_BANKS][:, :], ACT.Exp, scale=scale
                                         ).then_inc(s.probs.sem, 1)

            def copy(s, b, name, dst, src=None):
                s.work.wait_ready(act, b, name)
                nc.scalar.activation(dst, bank(s, name)[:, :] if src is None else src, ACT.Copy
                                     ).then_inc(free(s, name), 1)

            for h in range(HEADS):
                act.wait_ge(folded, h + 1)
                nc.scalar.activation(M[:, h, :], work[h % WORK_BANKS][:, 0:P], ACT.Copy).then_inc(fold_free, 1)

            act.wait_ge(setup, 5)
            with act.Fori(0, B) as b:
                copy(A, b, "hT", hT[:, :])
                copy(A, b, "lat", latT[:, :])
                for h in range(HEADS):
                    if 2 <= h < 2 + 2 * TILES and h % 2 == 0:
                        copy(A, b, f"v{h - 2}", *value_blocks(h - 2))
                    if h % 2 == 1:
                        copy(A, b, f"q{h}", QP[:, h, :])
                exponentials(A, b, HD_A ** -0.5)

            def small(s, rope):
                with act.Fori(0, B) as b:
                    if rope:
                        s.work.wait_ready(act, b, "hT")
                        nc.scalar.activation(hT[:, :], bank(s, "hT")[:, :], ACT.Identity, bias=ln[:, 1:2],
                                             scale=ln[:, 0:1]).then_inc(free(s, "hT"), 1)
                    else:
                        copy(s, b, "hT", hT[:, :])
                    s.work.wait_ready(act, b, "v")
                    src = bank(s, "v")[:, :].rearrange("p (i h d) -> p i h d", i=TILES, d=HD_S)
                    for half in range(2):
                        dst = VS[:, :, half, 64 * half:64 * half + 8 * 136].rearrange("p i (h c) -> p i h c", c=136)
                        last = nc.scalar.activation(dst[:, :, :, 0:HD_S], src[:, :, half * 8:half * 8 + 8, :], ACT.Copy)
                    last.then_inc(free(s, "v"), 1)
                    exponentials(s, b, HD_S ** -0.5)

            act.wait_ge(loaded_b, 16 * 15)
            act.wait_ge(zeroed, 1 + 2 * TILES)
            small(SB, True)

            act.wait_ge(loaded_moe, 16 * 5)
            with act.Fori(0, B) as b:
                s = M_
                s.work.wait_ready(act, b, "hT")
                nc.scalar.activation(hT[:, :], bank(s, "hT")[:, :], ACT.Identity, bias=ln[:, 3:4],
                                     scale=ln[:, 2:3]).then_inc(free(s, "hT"), 1)
                s.work.wait_copied(act, b, "logits")
                nc.scalar.activation(gates[:, :, :], lg[:, :, :], ACT.Exp).then_inc(m_exp.sem, 1)
                for e in range(EXPERTS):
                    for f in range(FT):
                        s.work.wait_ready(act, b, f"h{e}.{f}")
                        nc.scalar.activation(hid2(e)[:, f, :], bank(s, f"h{e}.{f}")[:, :], ACT.Gelu,
                                             bias=b1s[:, e, f:f + 1]).then_inc(free(s, f"h{e}.{f}"), 1)

            small(SC, False)

            with act.Fori(0, B) as b:
                s = F_
                copy(s, b, "hT", hT[:, :])
                for f in range(HT):
                    s.work.wait_ready(act, b, f"g{f}")
                    nc.scalar.activation(siluF[:, f, :], bank(s, f"g{f}")[:, :], ACT.Silu
                                         ).then_inc(free(s, f"g{f}"), 1)

        @block.vector
        def _(dve):
            v = nc.vector

            class Steps:

                def __init__(self, s, b):
                    self.s, self.b, self.n = s, b, 0

                def __call__(self, ins):
                    self.n += 1
                    ins.then_inc(self.s.step.sem, 1)
                    dve.wait_ge(self.s.step.sem, self.s.step.at(self.b, self.n))

                def end(self):
                    assert self.n == self.s.step.per, (self.s.step.sem, self.n)

            def free(s, name):
                return s.work.free[s.work.bank(name)].sem

            def bank(s, name):
                return work[s.work.bank(name)]

            def layernorm(s, b, step, k, src, dst):
                for i in range(TILES):
                    last = v.bn_stats(stats[:, i, :], src[:, i, :])
                step(last)
                even, odd = stats[:, :, 0:3], stats[:, :, 3:6]
                v.tensor_tensor(mean[:, :, 0], even[:, :, 1], odd[:, :, 1], ALU.add)
                v.tensor_tensor(mean[:, :, 1], even[:, :, 1], odd[:, :, 1], ALU.subtract)
                step(v.tensor_tensor(mean[:, :, 2], even[:, :, 2], odd[:, :, 2], ALU.add))
                v.tensor_scalar(mv[:, :, 0], mean[:, :, 0], 0.5, None, ALU.mult)
                v.tensor_scalar(mv[:, :, 1], mean[:, :, 2], 1.0 / C, EPS, ALU.mult, ALU.add)
                step(v.scalar_tensor_tensor(mean[:, :, 3], mean[:, :, 1], 0.25, mean[:, :, 1], ALU.mult, ALU.mult))
                v.tensor_tensor(veps[:, :], mv[:, :, 1], mean[:, :, 3], ALU.add).then_inc(s.var.sem, 1)
                dve.wait_ge(s.rstd.sem, s.rstd.at(b, k + 1))
                for i in range(TILES):
                    last = v.tensor_scalar(dst[:, i, :], src[:, i, :], mv[:, i, 0:1], rstd[:, i:i + 1],
                                           ALU.subtract, ALU.mult)
                return last

            def row_maxima(s, b, m):
                s.work.wait_ready(dve, b, f"max{m}")
                src, g = bank(s, f"max{m}"), m // GROUP_TILES
                blocks = max_tile(m)
                if len(blocks) == 2 and blocks[0][3] == blocks[1][3]:
                    h, i, _, w = blocks[0]
                    last = v.tensor_reduce(MX[:, g % 2, i, h % GROUP:h % GROUP + 2],
                                           src[:, :].rearrange("p (h k) -> p h k", h=2), AX_X, ALU.max, negate=True)
                else:
                    for h, i, c, w in blocks:
                        last = v.tensor_reduce(MX[:, g % 2, i, h % GROUP:h % GROUP + 1], src[:, c:c + w], AX_X,
                                               ALU.max, negate=True)
                last.then_inc(free(s, f"max{m}"), 1)

            def split_maxima(s, b, step, g):
                for m in range(GROUP_TILES * (g + 1) - 3, GROUP_TILES * (g + 1)):
                    s.work.wait_copied(dve, b, f"max{m}")
                mx = MX[:, g % 2]
                p1, p2, p3 = [MS[:, :, 32 * k:32 * k + GROUP] for k in range(PIECES)]
                step(v.tensor_copy(p1, mx))
                step(v.tensor_tensor(MR[:, :, :], mx, p1, ALU.subtract))
                step(v.tensor_copy(p2, MR[:, :, :]))
                v.tensor_tensor(p3, MR[:, :, :], p2, ALU.subtract).then_inc(s.pieces.sem, 1)

            def turned(s, b, g):
                s.work.wait_ready(dve, b, f"turn{g}")
                v.tensor_copy(MT[:, g % 2, :], bank(s, f"turn{g}")[:, :].bitcast(BF16)[:, 0:T]
                              ).then_inc(free(s, f"turn{g}"), 1)

            def normalise(s, b, step, n, use, dst):
                dve.wait_ge(s.pv.sem, s.pv.at(b, n + 1))
                y = slice(64 * (use % 2), 64 * (use % 2) + 64)
                z = slice(64 - 64 * (use % 2), 128 - 64 * (use % 2))
                step(v.reciprocal(rsum[y, :], pv[use % PV_BANKS][z, :]))
                v.tensor_tensor(dst[y, :], pv[use % PV_BANKS][y, :], rsum[y, :], ALU.mult).then_inc(s.y.sem, 1)

            def attention(s, b, step, per_bank, dst_of):
                for m in range(GROUP_TILES):
                    row_maxima(s, b, m)
                for m in range(GROUP_TILES, AHEAD):
                    row_maxima(s, b, m)
                split_maxima(s, b, step, 0)
                turned(s, b, 0)
                for n in range(ST_TILES + LAG):
                    if n + AHEAD < ST_TILES:
                        row_maxima(s, b, n + AHEAD)
                    g = n // GROUP_TILES + 1
                    if g < HEADS // GROUP and n % GROUP_TILES == GROUP_TILES - 3:
                        split_maxima(s, b, step, g)
                    if g < HEADS // GROUP and n % GROUP_TILES == GROUP_TILES - 2:
                        turned(s, b, g)
                    if n >= LAG and (n - LAG) % PAIR_TILES >= 3:
                        h = 2 * ((n - LAG) // PAIR_TILES) + (n - LAG) % PAIR_TILES - 3
                        if h % per_bank == per_bank - 1:
                            normalise(s, b, step, n - LAG, h // per_bank, dst_of(h // per_bank))

            dve.wait_ge(loaded_x, 16)
            dve.wait_ge(setup, 5)
            with dve.Fori(0, B) as b:
                s, step = A, Steps(A, b)
                xb = X[:, bass.ds(b * TILES, TILES), :]
                layernorm(s, b, step, 0, xb, H).then_inc(s.normed.sem, 1)
                for h in range(HEADS):
                    if 2 <= h < 2 + 2 * TILES and h % 2 == 1:
                        dst, src = value_blocks(h - 2)
                        s.work.wait_ready(dve, b, f"v{h - 2}")
                        v.tensor_copy(dst, src).then_inc(free(s, f"v{h - 2}"), 1)
                    if h % 2 == 0:
                        s.work.wait_ready(dve, b, f"q{h}")
                        v.tensor_copy(QP[:, h, :], bank(s, f"q{h}")[:, :]).then_inc(free(s, f"q{h}"), 1)
                attention(s, b, step, 1, lambda use: yT[:, use // 2, :])
                s.work.wait_ready(dve, b, "out")
                v.tensor_tensor(xb, X[:, bass.ds(b * TILES, TILES), :],
                                bank(s, "out")[:, :].rearrange("p (i c) -> p i c", c=C), ALU.add
                                ).then_inc(free(s, "out"), 1)
                step.end()

            def split_operand(s, b, step, w, src, tag):
                step(v.tensor_copy(piece[:, w, 0, :], src))
                step(v.tensor_tensor(rot[:, 0, :], src, piece[:, w, 0, :], ALU.subtract))
                step(v.tensor_copy(piece[:, w, 1, :], rot[:, 0, :]))
                v.tensor_tensor(piece[:, w, 2, :], rot[:, 0, :], piece[:, w, 1, :], ALU.subtract
                                ).then_inc(s_split[tag].sem, 1)
                dve.wait_ge(s_split[tag].sem, s_split[tag].at(b, w + 1))

            dve.wait_ge(loaded_const, 16 * CONSTS)
            A.work.wait_copied(dve, B - 1, "out")
            with dve.Fori(0, B) as b:
                s, step = SB, Steps(SB, b)
                step(layernorm(s, b, step, 0, X[:, bass.ds(b * TILES, TILES), :], Ub))
                layernorm(s, b, step, 1, Ub, H).then_inc(s.normed.sem, 1)
                for w, (name, turn) in enumerate((("q", "qr"), ("k", "kr"))):
                    s.work.wait_ready(dve, b, name)
                    v.tensor_tensor(rot[:, 0, :], bank(s, name)[:, :], cos[:, :], ALU.mult).then_inc(free(s, name), 1)
                    s.work.wait_ready(dve, b, turn)
                    v.tensor_tensor(rot[:, 1, :], bank(s, turn)[:, :], sin[:, :], ALU.mult).then_inc(free(s, turn), 1)
                    s.work.wait_copied(dve, b, name)
                    s.work.wait_copied(dve, b, turn)
                    step(v.tensor_tensor(qk[:, w, :], rot[:, 0, :], rot[:, 1, :], ALU.add))
                    split_operand(s, b, step, w, qk[:, w, :], "b")
                attention(s, b, step, 8, lambda use: yT[:, 0, :])
                s.work.wait_ready(dve, b, "out")
                v.tensor_tensor(U[:, bass.ds(b * TILES, TILES), :], Ub[:, :, :],
                                bank(s, "out")[:, :].rearrange("p (i c) -> p i c", c=C), ALU.add
                                ).then_inc(free(s, "out"), 1)
                step.end()

            SB.work.wait_copied(dve, B - 1, "out")
            with dve.Fori(0, B) as b:
                s, step = M_, Steps(M_, b)
                layernorm(s, b, step, 0, U[:, bass.ds(b * TILES, TILES), :], H).then_inc(s.normed.sem, 1)

                def spread(row):
                    return row.rearrange("p (i o) -> p i o", o=1).to_broadcast([P, TILES, EXPERTS])

                s.work.wait_ready(dve, b, "logits")
                logits = bank(s, "logits")[:, 0:TILES * EXPERTS].rearrange("p (i e) -> p i e", e=EXPERTS)
                step(v.tensor_reduce(lmax[:, :], logits, AX_X, ALU.max))
                v.tensor_tensor(lg[:, :, :], logits, spread(lmax[:, :]), ALU.subtract
                                ).then_inc(free(s, "logits"), 1)
                dve.wait_ge(m_exp.sem, m_exp.at(b, 1))
                step(v.tensor_reduce(lsum[:, :], gates[:, :, :], AX_X, ALU.add))
                step(v.reciprocal(lsum[:, :], lsum[:, :]))
                step(v.tensor_tensor(gates[:, :, :], gates[:, :, :], spread(lsum[:, :]), ALU.mult))

                def first_peak(src, dst):
                    step(v.tensor_reduce(lmax[:, :], src, AX_X, ALU.max))
                    step(v.tensor_tensor(rank[:, :, :], src, spread(lmax[:, :]), ALU.is_equal))
                    step(v.tensor_tensor(rank[:, :, :], rank[:, :, :], order[:, :, :], ALU.mult))
                    step(v.tensor_reduce(lmax[:, :], rank[:, :, :], AX_X, ALU.max))
                    step(v.tensor_tensor(dst, rank[:, :, :], spread(lmax[:, :]), ALU.is_equal))

                first_peak(gates[:, :, :], maskf[:, :, :])
                step(v.scalar_tensor_tensor(gsel[:, :, :], maskf[:, :, :], -2.0, gates[:, :, :], ALU.mult, ALU.add))
                first_peak(gsel[:, :, :], keep[:, :, :])
                step(v.tensor_tensor(maskf[:, :, :], maskf[:, :, :], keep[:, :, :], ALU.add))
                for i in range(TILES):
                    step(v.tensor_tensor(before[:, i + 1, :], before[:, i, :], maskf[:, i, :], ALU.add))
                v.tensor_copy(maskb16[:, :, :], maskf[:, :, :])
                step(v.tensor_copy(before16[:, :, :], before[:, 0:TILES, :]))
                v.tensor_copy(before[:, 0, :], before[:, TILES, :]).then_inc(m_masks.sem, 1)
                s.work.wait_ready(dve, b, "count")
                count = bank(s, "count")[:, 0:TILES * EXPERTS].rearrange("p (i e) -> p i e", e=EXPERTS)
                v.tensor_scalar(keep[:, :, :], count, float(CAP), None, ALU.is_le).then_inc(free(s, "count"), 1)
                s.work.wait_copied(dve, b, "count")
                step(v.tensor_tensor(keep[:, :, :], keep[:, :, :], maskf[:, :, :], ALU.mult))
                v.tensor_tensor(ge[:, :, :], keep[:, :, :], gates[:, :, :], ALU.mult).then_inc(m_gate.sem, 1)
                s.work.wait_ready(dve, b, "gT")
                v.tensor_copy(geT[:, :, :].rearrange("e i c -> e (i c)"), bank(s, "gT")[0:EXPERTS, :]
                              ).then_inc(free(s, "gT"), 1)
                s.work.wait_ready(dve, b, "b2")
                v.tensor_tensor(acc[:, :, :], U[:, bass.ds(b * TILES, TILES), :],
                                bank(s, "b2")[:, :].rearrange("p (i c) -> p i c", c=C), ALU.add
                                ).then_inc(free(s, "b2"), 1)
                s.work.wait_copied(dve, b, "b2")
                for e in range(EXPERTS):
                    dve.wait_ge(m_out.sem, m_out.at(b, e + 1))
                    for i in range(TILES):
                        last = v.scalar_tensor_tensor(acc[:, i, :], pv[e % PV_BANKS][:, i * C:(i + 1) * C],
                                                      ge[:, i, e:e + 1], acc[:, i, :], ALU.mult, ALU.add)
                    last.then_inc(m_acc.sem, 1)
                    dve.wait_ge(m_acc.sem, m_acc.at(b, e + 1))
                v.tensor_tensor(X[:, bass.ds(b * TILES, TILES), :], X[:, bass.ds(b * TILES, TILES), :],
                                acc[:, :, :], ALU.add).then_inc(s.done.sem, 1)
                step.end()

            dve.wait_ge(M_.done.sem, B)
            with dve.Fori(0, B) as b:
                s, step = SC, Steps(SC, b)
                xb = X[:, bass.ds(b * TILES, TILES), :]
                layernorm(s, b, step, 0, xb, H).then_inc(s.normed.sem, 1)
                for w, name in enumerate("qk"):
                    s.work.wait_ready(dve, b, name)
                    v.tensor_copy(qk[:, w, :], bank(s, name)[:, :]).then_inc(free(s, name), 1)
                    s.work.wait_copied(dve, b, name)
                    split_operand(s, b, step, w, qk[:, w, :], "c")
                attention(s, b, step, 8, lambda use: yT[:, 0, :])
                s.work.wait_ready(dve, b, "out")
                v.tensor_tensor(acc[:, :, :], bos[:, :, :], bank(s, "out")[:, :].rearrange("p (i c) -> p i c", c=C),
                                ALU.add).then_inc(free(s, "out"), 1)
                s.work.wait_copied(dve, b, "out")
                v.tensor_tensor(xb, xb, acc[:, :, :], ALU.add).then_inc(s.done.sem, 1)
                step.end()

            dve.wait_ge(loaded_f, 16 * 3)
            v.tensor_scalar(Wf[:, :], WfI[:, :], float(np.float32(1.0 / 127.0)), None, ALU.mult).then_inc(ffn_weights, 1)
            dve.wait_ge(SC.done.sem, B)
            with dve.Fori(0, B) as b:
                s, step = F_, Steps(F_, b)
                xb = X[:, bass.ds(b * TILES, TILES), :]
                layernorm(s, b, step, 0, xb, H).then_inc(s.normed.sem, 1)
                for f in range(HT):
                    s.work.wait_copied(dve, b, f"g{f}")
                    s.work.wait_ready(dve, b, f"u{f}")
                    v.tensor_tensor(hidF[:, f, :], bank(s, f"u{f}")[:, :], siluF[:, f, :], ALU.mult
                                    ).then_inc(free(s, f"u{f}"), 1)
                s.work.wait_ready(dve, b, "out")
                v.tensor_tensor(xb, xb, bank(s, "out")[:, :].rearrange("p (i c) -> p i c", c=C), ALU.add
                                ).then_inc(free(s, "out"), 1)
                step.end()


def constants():
    r = np.arange(P)
    ident = np.eye(P, dtype=np.float32)
    mask = np.where(r[None, :] > r[:, None], np.float32(-1e30), np.float32(0))
    sel = np.zeros((P, GROUP, P), np.float32)
    for k in range(PIECES):
        for j in range(GROUP):
            sel[32 * k + j, j, :] = 1
    inv_freq = np.float32(1.0) / np.float32(10000.0) ** (np.arange(0, HD_S, 2, dtype=np.float32) / np.float32(HD_S))
    ang = np.arange(T, dtype=np.float32)[None, :] * inv_freq.astype(np.float32)[:, None]
    cos = np.tile(np.cos(ang).astype(np.float32), (C // len(inv_freq), 1))
    sin = np.tile(np.sin(ang).astype(np.float32), (C // len(inv_freq), 1))
    tri = (r[:, None] <= r[None, :]).astype(np.float32)
    order = np.broadcast_to(EXPERTS - np.arange(EXPERTS, dtype=np.float32), (P, TILES, EXPERTS))
    return dict(ident=ident, mask=mask, maskT=mask.T, cos=cos, sin=sin, sel=sel, tri=tri, order=order.astype(np.float32))


def kernel(**inputs):
    import concourse.bacc as _bacc
    from concourse import mybir as _mybir
    from concourse.bass_utils import run_bass_kernel_spmd as _run

    a = {k: np.asarray(v) for k, v in inputs.items()}
    up = a["L0_attn_w_kv_up"]
    hd = HEADS * HD_A
    qkv = a["L0_ffn_Wqkv"].reshape(C, HEADS, 3 * HD_S)
    bq, bk, bv = [qkv[:, :, k * HD_S:(k + 1) * HD_S] for k in range(3)]

    def turned(w):
        return np.concatenate([w[:, :, HD_S // 2:], w[:, :, :HD_S // 2]], axis=2)

    data = {
        "x": a["L0_attn_x"].reshape(B * T, C),
        "w_down": a["L0_attn_w_kv_down"], "w_upv": up[:, hd:],
        "w_qT": a["L0_attn_w_q"].T, "w_kT": up[:, :hd].T, "w_out": a["L0_attn_w_out"],
        "ln1g": a["L0_ffn_ln1_g"].reshape(C, 1), "ln1b": a["L0_ffn_ln1_b"].reshape(C, 1),
        "b_wq": bq.reshape(C, C), "b_wqr": turned(bq).reshape(C, C),
        "b_wk": bk.reshape(C, C), "b_wkr": turned(bk).reshape(C, C), "b_wv": bv.reshape(C, C),
        "b_wo": a["L0_ffn_Wproj"],
        "ln2g": a["L0_ffn_ln2_g"].reshape(C, 1), "ln2b": a["L0_ffn_ln2_b"].reshape(C, 1),
        "w_gate": a["L0_ffn_Wgate"], "w1": a["L0_ffn_W1"],
        "b1": a["L0_ffn_b1"].reshape(EXPERTS * FT, P).T,
        "w2": a["L0_ffn_W2"].reshape(EXPERTS * FFN, C), "b2": a["L0_ffn_b2"],
        "c_wq": a["L1_attn_Wq"], "c_wk": a["L1_attn_Wk"], "c_wv": a["L1_attn_Wv"], "c_wo": a["L1_attn_Wo"],
        "c_bo": a["L1_attn_bo"].reshape(1, 1, C),
        "f_gate": a["L1_ffn_w_gate"].T, "f_up": a["L1_ffn_w_up"].T, "f_down": a["L1_ffn_w_down"].T,
    }
    table = constants()
    sign = np.where(np.arange(C) % HD_S < HD_S // 2, np.float32(-1), np.float32(1))[:, None]
    table["sin"] = table["sin"] * sign
    data.update(table)

    nc = _bacc.Bacc("TRN2", target_bir_lowering=False, num_devices=1)
    arrays, args = {}, []
    for name, value in data.items():
        value = np.ascontiguousarray(value)
        arrays[f"in_{name}"] = value
        args.append(nc.dram_tensor(f"in_{name}", value.shape, _mybir.dt.from_np(value.dtype),
                                   kind="ExternalInput").ap())
    args.append(nc.dram_tensor("out_0", (B * T, C), F32, kind="ExternalOutput").ap())
    program(nc, *args)
    r = _run(nc, [arrays], core_ids=[0])
    return r.results[0]["out_0"].reshape(B, T, C)
```

```python
from contextlib import ExitStack

import numpy as np

import concourse.bass as bass
from concourse import mybir

F32 = mybir.dt.float32
F32R = mybir.dt.float32r
BF16 = mybir.dt.bfloat16
I32 = mybir.dt.int32
ALU = mybir.AluOpType
ACT = mybir.ActivationFunctionType
AX_X = mybir.AxisListType.X

P = 128
B, T, C = 4, 512, 128
TILES = T // P
HEADS = 16
HD_A = 64
HD_S = C // HEADS
PIECES = 3
STACK = PIECES * PIECES * HD_S
EXPERTS, FFN, CAP = 8, 512, 512
FT = FFN // P
HID = 384
HT = HID // P
EPS = 1e-5
GROUP = 4
GROUPS = HEADS // GROUP
PAIR_TILES = 5
ST_TILES = HEADS // 2 * PAIR_TILES
GROUP_TILES = GROUP // 2 * PAIR_TILES
AHEAD = 13
CONSTS, TABLES = 2, 5
LAG = 4
STEPS = ST_TILES + LAG
P_RING = 5
FULL_RING = 4
ST_BANKS = 3
PV_BANKS = 2
WORK_BANKS = 3
STRIPE = P + HD_S
BLOCKS = 5 * P
NORM_STEP, TURN_STEP, LATENT_STEP, OPERAND_STEP = 1, 5, 10, 9
STACK_READS = 2 * PIECES


def query_step(h):
    return max(PAIR_TILES * (h // 2 + 1) + 1, TURN_STEP + 2) + 2 * (h % 2)


def value_step(k):
    return None if k % 2 else 26 + k


def pair_tile(n):
    a, k = 2 * (n // PAIR_TILES), n % PAIR_TILES
    return [
        [(a, 0, 0, 512)],
        [(a, 1, 0, 384), (a, 3, 384, 128)],
        [(a + 1, 0, 0, 512)],
        [(a, 2, 0, 256), (a + 1, 2, 256, 256)],
        [(a + 1, 1, 0, 384), (a + 1, 3, 384, 128)],
    ][k]


def max_tile(m):
    a, k = 2 * (m // PAIR_TILES), m % PAIR_TILES
    return [
        [(a, 3, 0, 512)],
        [(a, 2, 0, 384), (a, 0, 384, 128)],
        [(a + 1, 3, 0, 512)],
        [(a, 1, 0, 256), (a + 1, 1, 256, 256)],
        [(a + 1, 2, 0, 384), (a + 1, 0, 384, 128)],
    ][k]


class Tally:

    def __init__(self, sem, per, start=0):
        self.sem, self.per, self.start = sem, per, start

    def at(self, b, k):
        return b * self.per + (self.start + k)

    def after(self, batches, per):
        return Tally(self.sem, per, self.start + batches * self.per)


class Work:

    def __init__(self, names, ready, free):
        self.names, self.ready, self.free = names, ready, free
        self.index = {name: n for n, name in enumerate(names)}
        assert len(self.index) == len(names)

    @classmethod
    def first(cls, names, ready, free):
        return cls(names, Tally(ready, len(names)), [Tally(f, u, 1) for f, u in zip(free, cls.uses(names))])

    @staticmethod
    def uses(names):
        return [len(range(k, len(names), WORK_BANKS)) for k in range(WORK_BANKS)]

    def then(self, batches, names):
        return Work(names, self.ready.after(batches, len(names)),
                    [t.after(batches, u) for t, u in zip(self.free, self.uses(names))])

    def bank(self, name):
        return self.index[name] % WORK_BANKS

    def wait_free(self, eng, b, name):
        n = self.index[name]
        t = self.free[n % WORK_BANKS]
        eng.wait_ge(t.sem, t.at(b, n // WORK_BANKS))

    def wait_copied(self, eng, b, name):
        n = self.index[name]
        t = self.free[n % WORK_BANKS]
        eng.wait_ge(t.sem, t.at(b, n // WORK_BANKS + 1))

    def wait_ready(self, eng, b, name):
        eng.wait_ge(self.ready.sem, self.ready.at(b, self.index[name] + 1))


def first_operands():
    names = ["hT", "lat"]
    for k in range(2 * TILES):
        names += [f"q{2 * k}", f"q{2 * k + 1}", f"v{k}"]
    return names


def step_names(n, following):
    names = []
    if n + AHEAD < ST_TILES:
        names.append(f"max{n + AHEAD}")
    if n % GROUP_TILES == GROUP_TILES - 2 and n // GROUP_TILES + 1 < GROUPS:
        names.append(f"turn{n // GROUP_TILES + 1}")
    return names + following(n)


def attention_names(following, tail):
    names = [f"max{m}" for m in range(AHEAD)] + ["turn0"]
    for n in range(STEPS):
        names += step_names(n, following)
    return names + ["out"] + tail


def nothing(n):
    return []


def first_following(n):
    names = ["hT"] * (n == TURN_STEP) + ["lat"] * (n == LATENT_STEP)
    names += [f"q{h}" for h in range(HEADS) if query_step(h) == n]
    return names + [f"v{k}" for k in range(2 * TILES) if value_step(k) == n]


FIRST_TAIL = [f"v{k}" for k in range(2 * TILES) if value_step(k) is None]


def small_following(products):
    def at(n):
        names = ["hT"] * (n == TURN_STEP)
        return names + [x for k, x in enumerate(products) if n == OPERAND_STEP + 2 * k]
    return at


def program(nc, x, w_down, w_upv, w_qT, w_kT, w_out, ln1g, ln1b, b_wq, b_wqr, b_wk, b_wkr, b_wv, b_wo,
            ln2g, ln2b, w_gate, w1, b1, w2, b2, c_wq, c_wk, c_wv, c_wo, c_bo, f_gate, f_up, f_down,
            ident_d, mask_d, maskT_d, cos_d, sin_d, sel_d, tri_d, order_d, out):
    with ExitStack() as ctx:
        def sb(name, shape, dt=F32):
            return ctx.enter_context(nc.sbuf_tensor(name, shape, dt))

        def sem(name):
            return ctx.enter_context(nc.semaphore(name))

        work = [ctx.enter_context(nc.psum_tensor(f"work{k}", [P, 512], F32)) for k in range(WORK_BANKS)]
        st = [ctx.enter_context(nc.psum_tensor(f"scores{k}", [P, 512], F32)) for k in range(ST_BANKS)]
        pv = [ctx.enter_context(nc.psum_tensor(f"values{k}", [P, 512], F32)) for k in range(PV_BANKS)]

        X = sb("X", [P, B * TILES, C])
        H = sb("H", [P, TILES, C])
        stats = sb("stats", [P, TILES, 6])
        mean = sb("mean", [P, TILES, 4])
        mv = sb("mv", [P, TILES, 2])
        veps = sb("veps", [P, TILES])
        rstd = sb("rstd", [P, TILES])
        neghalf = sb("neghalf", [P, TILES])
        hT = sb("hT", [P, T])
        latent = sb("latent", [P, T])
        yT = sb("yT", [P, HEADS // 2, T])
        U = yT[:, 4:8, :].rearrange("p a (i c) -> p (a i) c", c=C)
        Ub = latent[:, :].rearrange("p (i c) -> p i c", c=C)
        acc = Ub
        rsum = sb("rsum", [HD_A, T])
        full = sb("full", [P, FULL_RING, 512])
        PH = sb("PH", [P, P_RING, 512], F32R)
        PL = sb("PL", [P, P_RING, 512], F32R)
        MX = sb("MX", [P, 2, TILES, GROUP])
        MR = sb("MR", [P, TILES, GROUP])
        MS = sb("MS", [P, TILES, P], BF16)
        MT = sb("MT", [P, 2, T], BF16)

        def shared(*groups):
            out, most = [], 0
            for group in groups:
                size = 0
                with ExitStack() as lent:
                    for name, shape, dt in group:
                        out.append(lent.enter_context(nc.sbuf_tensor(name, shape, dt)))
                        size += int(np.prod(shape[1:])) * (2 if dt == BF16 else 4)
                most = max(most, size)
            sb("under_" + groups[0][0][0], [P, most // 4])
            return out

        QH, QL, QS, KS, W1, W2 = shared(
            [("QH", [P, HEADS, T], F32R), ("QL", [P, HEADS, T], F32R)],
            [("QS", [P, HEADS, T], BF16), ("KS", [P, HEADS, T], BF16)],
            [("W1", [P, EXPERTS, FFN], F32), ("W2", [P, EXPERTS * FT, C], F32)])
        VH, VL, VS = shared(
            [("VH", [P, TILES, HEADS, P], F32R), ("VL", [P, TILES, HEADS, HD_A], F32R)],
            [("VS", [P, TILES * GROUPS, BLOCKS], F32R)])
        M, Wv, Wo, latH, latL, cos, sin, piece, rot, qk, WfI, Wf = shared(
            [("M", [P, HEADS, P], F32), ("Wv", [P, HEADS * HD_A], F32), ("Wo", [P, HEADS // 2, C], F32),
             ("latH", [P, T], F32R), ("latL", [P, T], F32R)],
            [("cos", [P, T], F32), ("sin", [P, T], F32), ("piece", [P, 2, PIECES, T], BF16),
             ("rot", [P, 2, T], F32), ("qk", [P, T], F32)],
            [("WfI", [P, 3 * HID], I32), ("Wf", [P, 3 * HID], F32)])
        identf = sb("identf", [P, P])
        identb = sb("identb", [P, P], BF16)
        maskb = sb("maskb", [P, P], BF16)
        maskTb = sb("maskTb", [P, P], BF16)
        selb = sb("selb", [P, GROUP, P], BF16)
        trib = sb("trib", [P, P], BF16)
        onesb = sb("onesb", [P, P], BF16)
        Wd = sb("Wd", [P, P])
        WqT = yT[:, 0:2, :].rearrange("p a (b c) -> p (a b) c", c=C)
        WkT = yT[:, 2:4, :].rearrange("p a (b c) -> p (a b) c", c=C)
        small = sb("small", [P, 12, C])
        BWq, BWqr, BWk, BWkr, BWv, CWq, CWk, CWv = [small[:, k, :] for k in range(8)]
        BWo, CWo = small[:, 8:10, :], small[:, 10:12, :]
        bo = sb("bo", [P, C])
        bos = bo[:, :].rearrange("p (o c) -> p o c", o=1).to_broadcast([P, TILES, C])
        ln = sb("ln", [P, 4])
        Wg = sb("Wg", [P, EXPERTS])
        b1s = sb("b1s", [P, EXPERTS, FT])
        b2s = sb("b2s", [EXPERTS, C])
        hidF = yT[:, 0:HT, :]
        siluF = yT[:, HT:2 * HT, :]
        lg = sb("lg", [P, TILES, EXPERTS])
        lmax = sb("lmax", [P, TILES])
        lsum = sb("lsum", [P, TILES])
        gates = sb("gates", [P, TILES, EXPERTS])
        rank = sb("rank", [P, TILES, EXPERTS])
        order = sb("order", [P, TILES, EXPERTS])
        gsel = sb("gsel", [P, TILES, EXPERTS])
        maskf = sb("maskf", [P, TILES, EXPERTS])
        before = sb("before", [P, TILES + 1, EXPERTS])
        maskb16 = sb("maskb16", [P, TILES, EXPERTS], BF16)
        before16 = sb("before16", [P, TILES, EXPERTS], BF16)
        keep = sb("keep", [P, TILES, EXPERTS])
        ge = sb("ge", [P, TILES, EXPERTS])
        geT = rsum[0:EXPERTS, :].rearrange("e (i c) -> e i c", c=P)

        q_pieces = nc.dram_tensor("q_pieces", [HEADS, PIECES, HD_S, T], BF16).ap()
        k_pieces = nc.dram_tensor("k_pieces", [HEADS, 2 * PIECES - 1, HD_S, T], BF16).ap()

        loaded_x, loaded_a, loaded_const = sem("loaded_x"), sem("loaded_a"), sem("loaded_const")
        loaded_tables, loaded_rot = sem("loaded_tables"), sem("loaded_rot")
        loaded_b, loaded_moe, loaded_f = sem("loaded_b"), sem("loaded_moe"), sem("loaded_f")
        setup = sem("setup")
        folded, fold_free = sem("folded"), sem("fold_free")
        zeroed = sem("zeroed")
        stored = sem("stored")
        ffn_weights = sem("ffn_weights")

        class Stage:

            def __init__(self, work, **tallies):
                self.work, self.tallies = work, tallies
                self.var, self.rstd, self.normed, self.step = [tallies.get(k) for k in (
                    "var", "rstd", "normed", "step")]
                self.scores, self.probs, self.low, self.pv = [tallies.get(k) for k in (
                    "scores", "probs", "low", "pv")]
                self.y, self.pieces, self.high, self.latents = [tallies.get(k) for k in (
                    "y", "pieces", "high", "latents")]
                self.split, self.spilt, self.stack, self.stripes = [tallies.get(k) for k in (
                    "split", "spilt", "stack", "stripes")]
                self.done = tallies.get("done")

            @classmethod
            def first(cls, tag, names, norms=1, **others):
                work = Work.first(names, sem(f"{tag}_product_ready"),
                                  [sem(f"{tag}_bank{k}_free") for k in range(WORK_BANKS)])
                tallies = {"var": (norms, 0), "rstd": (norms, 0), "normed": (1, 0), **others}
                return cls(work, **{k: Tally(sem(f"{tag}_{k}"), per, start) for k, (per, start) in tallies.items()})

            def then(self, batches, names, **per):
                return Stage(self.work.then(batches, names),
                             **{k: t.after(batches, per.get(k, t.per)) for k, t in self.tallies.items()})

        def attention_phases(tag, before, following, tail, uses, before_steps, norms=1, last_steps=0, **others):
            first = Stage.first(tag, before, norms=norms, step=(before_steps, 0), scores=(0, 0), probs=(0, ST_BANKS),
                                low=(0, FULL_RING), pv=(0, P_RING), y=(0, PV_BANKS), pieces=(0, 0), **others)
            core = dict(scores=ST_TILES, probs=ST_TILES, low=ST_TILES, pv=ST_TILES, y=uses, pieces=GROUPS)
            own = 3 * GROUPS + uses + last_steps
            loop = first.then(1, attention_names(following, tail), step=before_steps + own, **core)
            none = {k: 0 for k in ("var", "rstd", "normed", *others)}
            last = loop.then(B - 1, attention_names(nothing, []), step=own, **core, **none)
            return first, loop, last

        def small_phases(tag, products, norms, steps, last_steps=0):
            return attention_phases(tag, ["hT", *products, "v"], small_following(products), ["v"], GROUPS, steps,
                                    norms, last_steps, split=(2, 0), spilt=(16 * (3 * PIECES - 1), 0), stack=(16 * STACK_READS * GROUPS, 0),
                                    stripes=(1, 0))

        A0, A1, A2 = attention_phases("a", first_operands(), first_following, FIRST_TAIL, HEADS, 3,
                                      high=(HEADS + 2 * TILES + 1, 0), latents=(1, 0))
        B0, B1, B2 = small_phases("b", ["q", "qr", "k", "kr"], 2, 15)
        C0, C1, C2 = small_phases("c", ["q", "k"], 1, 9, 1)
        m_names = ["hT", "logits", "count", "gT", "b2"] + [f"h{e}.{f}" for e in range(EXPERTS) for f in range(FT)]
        f_names = ["hT"] + [f"{w}{f}" for f in range(HT) for w in "gu"] + ["out"]
        M_ = Stage.first("m", m_names, step=(25, 0), done=(1, 0))
        F_ = Stage.first("f", f_names, step=(3, 0))
        m_exp = Tally(sem("m_exp_ready"), 1)
        m_masks = Tally(sem("m_masks_ready"), 1)
        m_gate = Tally(sem("m_gates_ready"), 1)
        m_out = Tally(sem("m_expert_ready"), EXPERTS)
        m_acc = Tally(sem("m_expert_added"), EXPERTS, PV_BANKS)
        stages = [A0, B0, M_, C0, F_]

        def hid2(e):
            return (full, yT)[e % 2][:, 0:FT, :]

        def first_values(k):
            i, heads = k // 2, slice(k % 2 * 8, k % 2 * 8 + 8)
            return VH[:, i, heads, 0:HD_A], VL[:, i, heads, :]

        def stripes(place):
            at = VS[:, :, 4 * HD_S * place:4 * HD_S * place + GROUP * STRIPE]
            return at.rearrange("p g (h c) -> p g h c", c=STRIPE)[:, :, :, 0:HD_S]

        block = ctx.enter_context(nc.Block())

        @block.sync
        def _(sp):
            for s in stages:
                for t in s.work.free:
                    sp.sem_inc(t.sem, t.start)
            for s in (A0, B0, C0):
                for t in (s.probs, s.low, s.pv, s.y):
                    sp.sem_inc(t.sem, t.start)
            sp.sem_inc(m_acc.sem, m_acc.start)
            sp.sem_inc(fold_free, WORK_BANKS)
            sp.dma_start(X[:, :, :], x.rearrange("(t p) c -> p t c", p=P)).then_inc(loaded_x, 16)
            for dst, src in ((identf[:, :], ident_d), (order[:, :, :], order_d)):
                sp.dma_start(dst, src).then_inc(loaded_const, 16)
            for dst, src in ((WqT, w_qT.rearrange("(a p) c -> p a c", p=P)),
                             (WkT, w_kT.rearrange("(a p) c -> p a c", p=P)),
                             (Wd[:, :], w_down), (Wv[:, :], w_upv),
                             (Wo[:, :, :], w_out.rearrange("(a p) c -> p a c", p=P))):
                sp.dma_start(dst, src).then_inc(loaded_a, 16)
            for dst, src in ((BWq, b_wq), (BWqr, b_wqr), (BWk, b_wk), (BWkr, b_wkr), (BWv, b_wv),
                             (BWo, b_wo.rearrange("(a p) c -> p a c", p=P)),
                             (CWq, c_wq), (CWk, c_wk), (CWv, c_wv),
                             (CWo, c_wo.rearrange("(a p) c -> p a c", p=P)),
                             (bo[:, :], c_bo.to_broadcast([P, C])),
                             (ln[:, 0:1], ln1g), (ln[:, 1:2], ln1b), (ln[:, 2:3], ln2g), (ln[:, 3:4], ln2b)):
                sp.dma_start(dst, src).then_inc(loaded_b, 16)
            def spill_and_stack(s, b, free_of):
                for w, home in enumerate((q_pieces, k_pieces)):
                    sp.wait_ge(s.split.sem, s.split.at(b, w + 1))
                    for place in range(home.shape[1]):
                        sp.dma_start(home[:, place], piece[:, w, place % PIECES, :]).then_inc(s.spilt.sem, 16)
                sp.wait_ge(s.spilt.sem, s.spilt.at(b, s.spilt.per))
                for g in range(GROUPS):
                    if free_of is not None:
                        sp.wait_ge(free_of.scores.sem, free_of.scores.at(b, GROUP_TILES * (g + 1)))
                    heads = slice(GROUP * g, GROUP * g + GROUP)
                    for r in range(PIECES):
                        rows = slice(r * PIECES * HD_S, (r + 1) * PIECES * HD_S)
                        sp.dma_start(QS[rows, heads, :], q_pieces[heads].rearrange("h g d t -> (g d) h t")
                                     ).then_inc(s.stack.sem, 16)
                        sp.dma_start(KS[rows, heads, :], k_pieces[heads, r:r + PIECES].rearrange("h g d t -> (g d) h t")
                                     ).then_inc(s.stack.sem, 16)

            A2.work.wait_copied(sp, 0, "out")
            for dst, src in ((cos[:, :], cos_d), (sin[:, :], sin_d)):
                sp.dma_start(dst, src).then_inc(loaded_rot, 16)
            spill_and_stack(B0, 0, None)
            with sp.Fori(0, B - 1) as b:
                spill_and_stack(B1, b, B1)
            sp.wait_ge(B2.scores.sem, B2.scores.at(0, ST_TILES))
            for dst, src in ((Wg[:, :], w_gate), (W1[:, :, :], w1.rearrange("e d f -> d e f")),
                             (b1s[:, :, :], b1.rearrange("p (e f) -> p e f", e=EXPERTS)),
                             (W2[:, :, :], w2.rearrange("(a p) c -> p a c", p=P)), (b2s[:, :], b2)):
                sp.dma_start(dst, src).then_inc(loaded_moe, 16)

            sp.wait_ge(M_.done.sem, B)
            spill_and_stack(C0, 0, None)
            with sp.Fori(0, B - 1) as b:
                spill_and_stack(C1, b, C1)
            sp.wait_ge(C2.spilt.sem, C2.spilt.at(0, 0))
            for dst, src in ((WfI[:, 0:HID], f_gate), (WfI[:, HID:2 * HID], f_up),
                             (WfI[:, 2 * HID:3 * HID].rearrange("p (a c) -> p a c", c=C),
                              f_down.rearrange("(a p) c -> p a c", p=P))):
                sp.dma_start(dst, src).then_inc(loaded_f, 16)
            with sp.Fori(0, B) as b:
                F_.work.wait_copied(sp, b, "out")
                sp.dma_start(out.rearrange("(t p) c -> p t c", p=P)[:, bass.ds(b * TILES, TILES), :],
                             X[:, bass.ds(b * TILES, TILES), :]).then_inc(stored, 16)
            sp.wait_ge(stored, 16 * B)

        @block.gpsimd
        def _(pool):
            for dst, src in ((identb[:, :], ident_d), (maskb[:, :], mask_d), (maskTb[:, :], maskT_d),
                             (selb[:, :, :], sel_d), (trib[:, :], tri_d)):
                pool.dma_start(dst, src).then_inc(loaded_tables, 16)
            nc.gpsimd.memset(neghalf[:, :], -0.5).then_inc(setup, 1)
            nc.gpsimd.memset(VH[:, :, :, :].bitcast(F32), 1.0).then_inc(setup, 1)
            nc.gpsimd.memset(MS[:, :, :], 0.0).then_inc(setup, 1)
            nc.gpsimd.memset(onesb[:, :], 1.0).then_inc(setup, 1)
            nc.gpsimd.memset(before[:, 0, :], 0.0).then_inc(setup, 1)
            pool.wait_ge(setup, 5)

            def inverse_root(s, b, k):
                pool.wait_ge(s.var.sem, s.var.at(b, k + 1))
                nc.gpsimd.tensor_tensor(rstd[:, :], veps[:, :], neghalf[:, :], ALU.pow).then_inc(s.rstd.sem, 1)

            def low_part(s, b, n):
                pool.wait_ge(s.probs.sem, s.probs.at(b, n + 1))
                nc.gpsimd.tensor_tensor(PL[:, n % P_RING, :], full[:, n % FULL_RING, :],
                                        PH[:, n % P_RING, :].bitcast(F32), ALU.subtract).then_inc(s.low.sem, 1)

            def attention(s, b, norms):
                for n in range(ST_TILES):
                    if n == NORM_STEP:
                        for k in range(norms):
                            inverse_root(s, b, k)
                    low_part(s, b, n)

            def stage(phases, norms):
                first, loop, last = phases
                for k in range(norms):
                    inverse_root(first, 0, k)
                with pool.Fori(0, B - 1) as b:
                    attention(loop, b, norms)
                attention(last, 0, 0)

            stage((A0, A1, A2), 1)
            pool.wait_ge(A2.pv.sem, A2.pv.at(0, ST_TILES))
            nc.gpsimd.memset(VS[:, :, :].bitcast(F32), 0.0).then_inc(zeroed, 1)
            pool.wait_ge(zeroed, 1)
            for place in (2, 3):
                for i in range(TILES):
                    nc.gpsimd.memset(stripes(place)[:, GROUPS * i:GROUPS * (i + 1)].bitcast(F32), 1.0
                                     ).then_inc(zeroed, 1)
            stage((B0, B1, B2), 2)
            with pool.Fori(0, B) as b:
                inverse_root(M_, b, 0)
            stage((C0, C1, C2), 1)
            with pool.Fori(0, B) as b:
                inverse_root(F_, b, 0)

        @block.tensor
        def _(pe):
            def turn_h(s, b):
                pe.wait_ge(s.normed.sem, s.normed.at(b, 1))
                s.work.wait_free(pe, b, "hT")
                for i in range(TILES):
                    last = pe.transpose(work[s.work.bank("hT")][:, i * P:(i + 1) * P], H[:, i, :], identf[:, :])
                last.then_inc(s.work.ready.sem, 1)

            def product(s, b, name, lhsT, rhs):
                s.work.wait_free(pe, b, name)
                pe.matmul(work[s.work.bank(name)][:, :], lhsT, rhs, start=True, stop=True
                          ).then_inc(s.work.ready.sem, 1)

            def max_scores(s, b, m, passes):
                name = f"max{m}"
                s.work.wait_free(pe, b, name)
                bank = work[s.work.bank(name)]
                for h, i, c, w in max_tile(m):
                    q, k = passes[0]
                    pe.matmul(bank[:, c:c + w], q(h, i * P, (i + 1) * P), k(h, 0, w), start=True, stop=False)
                    last = pe.matmul(bank[:, c + w - P:c + w], identb[:, :], maskb[:, :], start=False, stop=True)
                last.then_inc(s.work.ready.sem, 1)

            def turn_max(s, b, g):
                pe.wait_ge(s.pieces.sem, s.pieces.at(b, g + 1))
                s.work.wait_free(pe, b, f"turn{g}")
                bank = work[s.work.bank(f"turn{g}")][:, :].bitcast(BF16)
                for i in range(TILES):
                    last = pe.transpose(bank[:, i * P:(i + 1) * P], MS[:, i, :], identb[:, :])
                last.then_inc(s.work.ready.sem, 1)

            def scores(s, b, n, passes):
                g = n // GROUP_TILES
                if n % GROUP_TILES == 0:
                    s.work.wait_copied(pe, b, f"turn{g}")
                pe.wait_ge(s.probs.sem, s.probs.at(b, max(n - ST_BANKS + 1, 0)))
                bank = st[n % ST_BANKS]
                for h, j, c, w in pair_tile(n):
                    q0 = j * P
                    for k, (q, key) in enumerate(passes):
                        pe.matmul(bank[:, c:c + w], key(h, q0, q0 + P), q(h, q0, q0 + w), start=k == 0, stop=False)
                    pe.matmul(bank[:, c:c + P], identb[:, :], maskTb[:, :], start=False, stop=False)
                    last = pe.matmul(bank[:, c:c + w], selb[:, h % GROUP, :], MT[:, g % 2, q0:q0 + w],
                                     start=False, stop=True)
                last.then_inc(s.scores.sem, 1)

            def values(s, b, n, high, low, per_bank):
                pe.wait_ge(s.probs.sem, s.probs.at(b, n + 1))
                for part, of in ((PH, high), (PH, low), (PL, high)):
                    if of is None:
                        continue
                    if part is PL:
                        pe.wait_ge(s.low.sem, s.low.at(b, n + 1))
                    for h, j, c, w in pair_tile(n):
                        use = h // per_bank
                        first = part is PH and of is high and j == 0 and h % per_bank == 0
                        if first:
                            pe.wait_ge(s.y.sem, s.y.at(b, use - PV_BANKS + 1))
                        final = part is PL and h % per_bank == per_bank - 1 and (j == 2 if h % 2 == 0 else j == 3)
                        block = of(h, j)
                        last = pe.matmul(pv[use % PV_BANKS][0:block.shape[1], T - w:T], block,
                                         part[:, n % P_RING, c:c + w], start=first, stop=final,
                                         skip_group_check=True)
                last.then_inc(s.pv.sem, 1)

            def attention(s, b, passes, high, low, per_bank, following):
                for m in range(AHEAD):
                    max_scores(s, b, m, passes)
                turn_max(s, b, 0)
                for n in range(STEPS):
                    if n < ST_TILES:
                        scores(s, b, n, passes)
                    if n + AHEAD < ST_TILES:
                        max_scores(s, b, n + AHEAD, passes)
                    if n % GROUP_TILES == GROUP_TILES - 2 and n // GROUP_TILES + 1 < GROUPS:
                        turn_max(s, b, n // GROUP_TILES + 1)
                    if following is not None:
                        following(n)
                    if n >= LAG:
                        values(s, b, n - LAG, high, low, per_bank)

            def output(s, b, rows):
                pe.wait_ge(s.y.sem, s.y.at(b, s.y.per))
                s.work.wait_free(pe, b, "out")
                bank = work[s.work.bank("out")]
                for i in range(TILES):
                    for k, (y, w) in enumerate(rows):
                        last = pe.matmul(bank[:, i * C:(i + 1) * C], y[:, i * P:(i + 1) * P], w,
                                         start=k == 0, stop=k == len(rows) - 1)
                last.then_inc(s.work.ready.sem, 1)

            pe.wait_ge(loaded_a, 16 * 5)
            pe.wait_ge(loaded_const, 16 * CONSTS)
            pe.wait_ge(loaded_tables, 16 * TABLES)
            pe.wait_ge(setup, 5)
            for h in range(HEADS):
                if h >= WORK_BANKS:
                    pe.wait_ge(fold_free, h + 1)
                r = slice(64 * (h % 2), 64 * (h % 2) + 64)
                pe.matmul(work[h % WORK_BANKS][:, 0:P], WqT[r, h // 2, :], WkT[r, h // 2, :],
                          start=True, stop=True).then_inc(folded, 1)

            pe.wait_ge(fold_free, HEADS + WORK_BANKS)

            def query(s, b, h):
                product(s, b, f"q{h}", M[:, h, :], hT[:, :])

            def value(s, b, k):
                product(s, b, f"v{k}", latent[:, k // 2 * P:(k // 2 + 1) * P], Wv[:, k % 2 * 512:(k % 2 + 1) * 512])

            def latents(s, b):
                s.work.wait_copied(pe, b, "hT")
                product(s, b, "lat", Wd[:, :], hT[:, :])

            def operands_ready(s, b):
                for name in s.work.names[-WORK_BANKS:]:
                    s.work.wait_copied(pe, b, name)
                pe.wait_ge(s.latents.sem, s.latents.at(b, 1))

            queries_h, queries_l = lambda h, c0, c1: QH[:, h, c0:c1], lambda h, c0, c1: QL[:, h, c0:c1]
            latents_h, latents_l = lambda h, c0, c1: latH[:, c0:c1], lambda h, c0, c1: latL[:, c0:c1]
            passes = [(queries_h, latents_h), (queries_l, latents_h), (queries_h, latents_l)]
            rows = [(yT[:, k, :], Wo[:, k, :]) for k in range(HEADS // 2)]
            high, low = lambda h, j: VH[:, j, h, :], lambda h, j: VL[:, j, h, :]

            turn_h(A0, 0)
            latents(A0, 0)
            for name in A0.work.names[2:]:
                if name == "v0":
                    A0.work.wait_copied(pe, 0, "lat")
                (query if name[0] == "q" else value)(A0, 0, int(name[1:]))
            operands_ready(A0, 0)
            with pe.Fori(0, B - 1) as b:
                def following(n):
                    if n == TURN_STEP:
                        turn_h(A1, b)
                    if n == LATENT_STEP:
                        latents(A1, b)
                    for h in range(HEADS):
                        if query_step(h) == n:
                            query(A1, b, h)
                    for k in range(2 * TILES):
                        if value_step(k) == n:
                            if k == 0:
                                A1.work.wait_copied(pe, b, "lat")
                            value(A1, b, k)

                attention(A1, b, passes, high, low, 1, following)
                output(A1, b, rows)
                for name in FIRST_TAIL:
                    value(A1, b, int(name[1:]))
                operands_ready(A1, b)
            attention(A2, 0, passes, high, low, 1, None)
            output(A2, 0, rows)

            def small_values(s, b, wv):
                s.work.wait_free(pe, b, "v")
                for i in range(TILES):
                    last = pe.matmul(work[s.work.bank("v")][:, i * C:(i + 1) * C], hT[:, i * P:(i + 1) * P], wv,
                                     start=True, stop=True)
                last.then_inc(s.work.ready.sem, 1)
                s.work.wait_copied(pe, b, "v")
                pe.wait_ge(s.stack.sem, s.stack.at(b, s.stack.per))

            def small_attention(phases, products, wv, wo):
                first, loop, last = phases
                passes = [(lambda h, c0, c1: QS[0:STACK, h, c0:c1], lambda h, c0, c1: KS[0:STACK, h, c0:c1])]
                rows = [(yT[:, k, :], wo[:, k, :]) for k in range(2)]
                high = lambda h, j: VS[:, j * GROUPS + h // GROUP, h % GROUP * P:(h % GROUP + 1) * P]
                turn_h(first, 0)
                first.work.wait_copied(pe, 0, "hT")
                for name, w in products:
                    product(first, 0, name, w, hT[:, :])
                small_values(first, 0, wv)
                with pe.Fori(0, B - 1) as b:
                    def following(n):
                        if n == TURN_STEP:
                            turn_h(loop, b)
                        for k, (name, w) in enumerate(products):
                            if n == OPERAND_STEP + 2 * k:
                                if k == 0:
                                    loop.work.wait_copied(pe, b, "hT")
                                product(loop, b, name, w, hT[:, :])

                    attention(loop, b, passes, high, None, GROUP, following)
                    output(loop, b, rows)
                    small_values(loop, b, wv)
                attention(last, 0, passes, high, None, GROUP, None)
                output(last, 0, rows)

            pe.wait_ge(loaded_b, 16 * 15)
            pe.wait_ge(zeroed, 1 + 2 * TILES)
            small_attention((B0, B1, B2), (("q", BWq), ("qr", BWqr), ("k", BWk), ("kr", BWkr)), BWv, BWo)

            pe.wait_ge(loaded_moe, 16 * 5)
            with pe.Fori(0, B) as b:
                s = M_
                turn_h(s, b)
                s.work.wait_copied(pe, b, "hT")
                s.work.wait_free(pe, b, "logits")
                for i in range(TILES):
                    last = pe.matmul(work[s.work.bank("logits")][:, i * EXPERTS:(i + 1) * EXPERTS],
                                     hT[:, i * P:(i + 1) * P], Wg[:, :], start=True, stop=True)
                last.then_inc(s.work.ready.sem, 1)
                pe.wait_ge(m_masks.sem, m_masks.at(b, 1))
                s.work.wait_free(pe, b, "count")
                bank = work[s.work.bank("count")][:, 0:TILES * EXPERTS]
                pe.matmul(bank, trib[:, :], maskb16[:, :, :].rearrange("p i e -> p (i e)"), start=True, stop=False)
                pe.matmul(bank, onesb[:, :], before16[:, :, :].rearrange("p i e -> p (i e)"), start=False, stop=True
                          ).then_inc(s.work.ready.sem, 1)
                pe.wait_ge(m_gate.sem, m_gate.at(b, 1))
                s.work.wait_free(pe, b, "gT")
                for i in range(TILES):
                    last = pe.transpose(work[s.work.bank("gT")][0:EXPERTS, i * P:(i + 1) * P], ge[:, i, :], identf[:, :])
                last.then_inc(s.work.ready.sem, 1)
                s.work.wait_copied(pe, b, "gT")
                s.work.wait_free(pe, b, "b2")
                for i in range(TILES):
                    last = pe.matmul(work[s.work.bank("b2")][:, i * C:(i + 1) * C], geT[:, i, :], b2s[:, :],
                                     start=True, stop=True)
                last.then_inc(s.work.ready.sem, 1)

                def expert_out(e):
                    for f in range(FT):
                        s.work.wait_copied(pe, b, f"h{e}.{f}")
                    pe.wait_ge(m_acc.sem, m_acc.at(b, e - PV_BANKS + 1))
                    for i in range(TILES):
                        for f in range(FT):
                            last = pe.matmul(pv[e % PV_BANKS][:, i * C:(i + 1) * C],
                                             hid2(e)[:, f, i * P:(i + 1) * P], W2[:, e * FT + f, :],
                                             start=f == 0, stop=f == FT - 1)
                    last.then_inc(m_out.sem, 1)

                for e in range(EXPERTS):
                    for f in range(FT):
                        product(s, b, f"h{e}.{f}", W1[:, e, f * P:(f + 1) * P], hT[:, :])
                    if e >= 1:
                        expert_out(e - 1)
                expert_out(EXPERTS - 1)

            small_attention((C0, C1, C2), (("q", CWq), ("k", CWk)), CWv, CWo)

            pe.wait_ge(ffn_weights, 1)
            with pe.Fori(0, B) as b:
                s = F_
                turn_h(s, b)
                s.work.wait_copied(pe, b, "hT")
                for f in range(HT):
                    product(s, b, f"g{f}", Wf[:, f * P:(f + 1) * P], hT[:, :])
                    product(s, b, f"u{f}", Wf[:, HID + f * P:HID + (f + 1) * P], hT[:, :])
                for f in range(HT):
                    s.work.wait_copied(pe, b, f"u{f}")
                s.work.wait_free(pe, b, "out")
                for i in range(TILES):
                    for f in range(HT):
                        last = pe.matmul(work[s.work.bank("out")][:, i * C:(i + 1) * C],
                                         hidF[:, f, i * P:(i + 1) * P],
                                         Wf[:, 2 * HID + f * C:2 * HID + (f + 1) * C], start=f == 0, stop=f == HT - 1)
                last.then_inc(s.work.ready.sem, 1)

        @block.scalar
        def _(act):
            def free(s, name):
                return s.work.free[s.work.bank(name)].sem

            def bank(s, name):
                return work[s.work.bank(name)]

            def exponential(s, b, n, scale):
                act.wait_ge(s.scores.sem, s.scores.at(b, n + 1))
                act.wait_ge(s.low.sem, s.low.at(b, n - FULL_RING + 1))
                act.wait_ge(s.pv.sem, s.pv.at(b, n - P_RING + 1))
                nc.scalar.activation(full[:, n % FULL_RING, :], st[n % ST_BANKS][:, :], ACT.Exp, scale=scale)
                nc.scalar.activation(PH[:, n % P_RING, :], st[n % ST_BANKS][:, :], ACT.Exp, scale=scale
                                     ).then_inc(s.probs.sem, 1)

            def copy(s, b, name, dst, src=None):
                s.work.wait_ready(act, b, name)
                nc.scalar.activation(dst, bank(s, name)[:, :] if src is None else src, ACT.Copy
                                     ).then_inc(free(s, name), 1)

            for h in range(HEADS):
                act.wait_ge(folded, h + 1)
                nc.scalar.activation(M[:, h, :], work[h % WORK_BANKS][:, 0:P], ACT.Copy).then_inc(fold_free, 1)

            act.wait_ge(setup, 5)

            def high_part(s, b, name, dst, src):
                s.work.wait_ready(act, b, name)
                nc.scalar.activation(dst, src, ACT.Copy).then_inc(s.high.sem, 1)

            def query(s, b, h):
                high_part(s, b, f"q{h}", QH[:, h, :], bank(s, f"q{h}")[:, :])

            def value(s, b, k):
                high_part(s, b, f"v{k}", first_values(k)[0],
                          bank(s, f"v{k}")[:, :].rearrange("p (h c) -> p h c", c=HD_A))

            def latent_high(s, b):
                s.work.wait_copied(act, b, "lat")
                s.work.wait_ready(act, b, s.work.names[-1])
                nc.scalar.activation(latH[:, :], latent[:, :], ACT.Copy).then_inc(s.high.sem, 1)

            copy(A0, 0, "hT", hT[:, :])
            for name in A0.work.names[2:]:
                (query if name[0] == "q" else value)(A0, 0, int(name[1:]))
            latent_high(A0, 0)
            with act.Fori(0, B - 1) as b:
                for n in range(STEPS):
                    if n < ST_TILES:
                        exponential(A1, b, n, HD_A ** -0.5)
                    if n == TURN_STEP:
                        copy(A1, b, "hT", hT[:, :])
                    for h in range(HEADS):
                        if query_step(h) == n:
                            query(A1, b, h)
                    for k in range(2 * TILES):
                        if value_step(k) == n:
                            value(A1, b, k)
                for name in FIRST_TAIL:
                    value(A1, b, int(name[1:]))
                latent_high(A1, b)
            for n in range(ST_TILES):
                exponential(A2, 0, n, HD_A ** -0.5)

            def small_values(s, b):
                s.work.wait_ready(act, b, "v")
                src = bank(s, "v")[:, :].rearrange("p (g h d) -> p g h d", h=GROUP, d=HD_S)
                nc.scalar.activation(stripes(0), src, ACT.Copy).then_inc(s.stripes.sem, 1)

            def small_hT(s, b, rope):
                if rope:
                    s.work.wait_ready(act, b, "hT")
                    nc.scalar.activation(hT[:, :], bank(s, "hT")[:, :], ACT.Identity, bias=ln[:, 1:2],
                                         scale=ln[:, 0:1]).then_inc(free(s, "hT"), 1)
                else:
                    copy(s, b, "hT", hT[:, :])

            def small(phases, rope):
                first, loop, last = phases
                small_hT(first, 0, rope)
                small_values(first, 0)
                with act.Fori(0, B - 1) as b:
                    for n in range(ST_TILES):
                        exponential(loop, b, n, HD_S ** -0.5)
                        if n == TURN_STEP:
                            small_hT(loop, b, rope)
                    small_values(loop, b)
                for n in range(ST_TILES):
                    exponential(last, 0, n, HD_S ** -0.5)

            act.wait_ge(loaded_b, 16 * 15)
            act.wait_ge(zeroed, 1 + 2 * TILES)
            small((B0, B1, B2), True)

            act.wait_ge(loaded_moe, 16 * 5)
            with act.Fori(0, B) as b:
                s = M_
                s.work.wait_ready(act, b, "hT")
                nc.scalar.activation(hT[:, :], bank(s, "hT")[:, :], ACT.Identity, bias=ln[:, 3:4],
                                     scale=ln[:, 2:3]).then_inc(free(s, "hT"), 1)
                s.work.wait_copied(act, b, "logits")
                nc.scalar.activation(gates[:, :, :], lg[:, :, :], ACT.Exp).then_inc(m_exp.sem, 1)
                for e in range(EXPERTS):
                    for f in range(FT):
                        s.work.wait_ready(act, b, f"h{e}.{f}")
                        nc.scalar.activation(hid2(e)[:, f, :], bank(s, f"h{e}.{f}")[:, :], ACT.Gelu,
                                             bias=b1s[:, e, f:f + 1]).then_inc(free(s, f"h{e}.{f}"), 1)

            small((C0, C1, C2), False)

            with act.Fori(0, B) as b:
                s = F_
                copy(s, b, "hT", hT[:, :])
                for f in range(HT):
                    s.work.wait_ready(act, b, f"g{f}")
                    nc.scalar.activation(siluF[:, f, :], bank(s, f"g{f}")[:, :], ACT.Silu
                                         ).then_inc(free(s, f"g{f}"), 1)

        @block.vector
        def _(dve):
            v = nc.vector

            class Steps:

                def __init__(self, s, b):
                    self.s, self.b, self.n = s, b, 0

                def __call__(self, ins):
                    self.n += 1
                    ins.then_inc(self.s.step.sem, 1)
                    dve.wait_ge(self.s.step.sem, self.s.step.at(self.b, self.n))

                def end(self):
                    assert self.n == self.s.step.per, (self.s.step.sem, self.n)

            def free(s, name):
                return s.work.free[s.work.bank(name)].sem

            def bank(s, name):
                return work[s.work.bank(name)]

            def layernorm(s, b, step, k, src, dst):
                for i in range(TILES):
                    last = v.bn_stats(stats[:, i, :], src[:, i, :])
                step(last)
                even, odd = stats[:, :, 0:3], stats[:, :, 3:6]
                v.tensor_tensor(mean[:, :, 0], even[:, :, 1], odd[:, :, 1], ALU.add)
                v.tensor_tensor(mean[:, :, 1], even[:, :, 1], odd[:, :, 1], ALU.subtract)
                step(v.tensor_tensor(mean[:, :, 2], even[:, :, 2], odd[:, :, 2], ALU.add))
                v.tensor_scalar(mv[:, :, 0], mean[:, :, 0], 0.5, None, ALU.mult)
                v.tensor_scalar(mv[:, :, 1], mean[:, :, 2], 1.0 / C, EPS, ALU.mult, ALU.add)
                step(v.scalar_tensor_tensor(mean[:, :, 3], mean[:, :, 1], 0.25, mean[:, :, 1], ALU.mult, ALU.mult))
                v.tensor_tensor(veps[:, :], mv[:, :, 1], mean[:, :, 3], ALU.add).then_inc(s.var.sem, 1)
                dve.wait_ge(s.rstd.sem, s.rstd.at(b, k + 1))
                for i in range(TILES):
                    last = v.tensor_scalar(dst[:, i, :], src[:, i, :], mv[:, i, 0:1], rstd[:, i:i + 1],
                                           ALU.subtract, ALU.mult)
                return last

            def row_maxima(s, b, m):
                s.work.wait_ready(dve, b, f"max{m}")
                src, g = bank(s, f"max{m}"), m // GROUP_TILES
                blocks = max_tile(m)
                if len(blocks) == 2 and blocks[0][3] == blocks[1][3]:
                    h, i, _, w = blocks[0]
                    last = v.tensor_reduce(MX[:, g % 2, i, h % GROUP:h % GROUP + 2],
                                           src[:, :].rearrange("p (h k) -> p h k", h=2), AX_X, ALU.max, negate=True)
                else:
                    for h, i, c, w in blocks:
                        last = v.tensor_reduce(MX[:, g % 2, i, h % GROUP:h % GROUP + 1], src[:, c:c + w], AX_X,
                                               ALU.max, negate=True)
                last.then_inc(free(s, f"max{m}"), 1)

            def split_maxima(s, b, step, g):
                for m in range(GROUP_TILES * (g + 1) - 3, GROUP_TILES * (g + 1)):
                    s.work.wait_copied(dve, b, f"max{m}")
                mx = MX[:, g % 2]
                p1, p2, p3 = [MS[:, :, 32 * k:32 * k + GROUP] for k in range(PIECES)]
                step(v.tensor_copy(p1, mx))
                step(v.tensor_tensor(MR[:, :, :], mx, p1, ALU.subtract))
                step(v.tensor_copy(p2, MR[:, :, :]))
                v.tensor_tensor(p3, MR[:, :, :], p2, ALU.subtract).then_inc(s.pieces.sem, 1)

            def turned(s, b, g):
                s.work.wait_ready(dve, b, f"turn{g}")
                v.tensor_copy(MT[:, g % 2, :], bank(s, f"turn{g}")[:, :].bitcast(BF16)[:, 0:T]
                              ).then_inc(free(s, f"turn{g}"), 1)

            def normalise(s, b, step, n, use, dst):
                dve.wait_ge(s.pv.sem, s.pv.at(b, n + 1))
                dve.wait_ge(s.y.sem, s.y.at(b, use))
                step(v.reciprocal(rsum[:, :], pv[use % PV_BANKS][HD_A:2 * HD_A, :]))
                v.tensor_tensor(dst, pv[use % PV_BANKS][0:HD_A, :], rsum[:, :], ALU.mult).then_inc(s.y.sem, 1)

            def rows_of(use):
                return yT[HD_A * (use % 2):HD_A * (use % 2 + 1), use // 2, :]

            def attention(s, b, step, per_bank, following):
                for m in range(AHEAD):
                    row_maxima(s, b, m)
                split_maxima(s, b, step, 0)
                turned(s, b, 0)
                for n in range(STEPS):
                    if n + AHEAD < ST_TILES:
                        row_maxima(s, b, n + AHEAD)
                    g = n // GROUP_TILES + 1
                    if g < GROUPS and n % GROUP_TILES == GROUP_TILES - 3:
                        split_maxima(s, b, step, g)
                    if g < GROUPS and n % GROUP_TILES == GROUP_TILES - 2:
                        turned(s, b, g)
                    if following is not None:
                        following(n)
                    if n >= LAG and (n - LAG) % PAIR_TILES >= 3:
                        h = 2 * ((n - LAG) // PAIR_TILES) + (n - LAG) % PAIR_TILES - 3
                        if h % per_bank == per_bank - 1:
                            normalise(s, b, step, n - LAG, h // per_bank, rows_of(h // per_bank))

            def batch(a, b):
                return a[:, bass.ds(b * TILES, TILES), :]

            def tokens(s, name):
                return bank(s, name)[:, :].rearrange("p (i c) -> p i c", c=C)

            dve.wait_ge(loaded_x, 16)
            dve.wait_ge(setup, 5)

            class Lows:

                def __init__(self, s, b):
                    self.s, self.b, self.n = s, b, 0

                def wait(self):
                    self.n += 1
                    dve.wait_ge(self.s.high.sem, self.s.high.at(self.b, self.n))

            def latent_copy(s, b):
                s.work.wait_ready(dve, b, "lat")
                v.tensor_copy(latent[:, :], bank(s, "lat")[:, :]).then_inc(free(s, "lat"), 1)

            def query_low(s, b, lows, h):
                lows.wait()
                v.tensor_tensor(QL[:, h, :], bank(s, f"q{h}")[:, :], QH[:, h, :].bitcast(F32), ALU.subtract
                                ).then_inc(free(s, f"q{h}"), 1)

            def value_low(s, b, lows, k):
                high, low = first_values(k)
                lows.wait()
                v.tensor_tensor(low, bank(s, f"v{k}")[:, :].rearrange("p (h c) -> p h c", c=HD_A),
                                high.bitcast(F32), ALU.subtract).then_inc(free(s, f"v{k}"), 1)

            def latent_low(s, b, lows):
                lows.wait()
                v.tensor_tensor(latL[:, :], latent[:, :], latH[:, :].bitcast(F32), ALU.subtract
                                ).then_inc(s.latents.sem, 1)

            step, lows = Steps(A0, 0), Lows(A0, 0)
            layernorm(A0, 0, step, 0, X[:, 0:TILES, :], H).then_inc(A0.normed.sem, 1)
            latent_copy(A0, 0)
            for name in A0.work.names[2:]:
                (query_low if name[0] == "q" else value_low)(A0, 0, lows, int(name[1:]))
            latent_low(A0, 0, lows)
            step.end()
            with dve.Fori(0, B - 1) as b:
                s, step, lows = A1, Steps(A1, b), Lows(A1, b)

                def following(n):
                    if n == NORM_STEP:
                        layernorm(s, b, step, 0, batch(X, b + 1), H).then_inc(s.normed.sem, 1)
                    if n == LATENT_STEP:
                        latent_copy(s, b)
                    for h in range(HEADS):
                        if query_step(h) == n:
                            query_low(s, b, lows, h)
                    for k in range(2 * TILES):
                        if value_step(k) == n:
                            value_low(s, b, lows, k)

                attention(s, b, step, 1, following)
                s.work.wait_ready(dve, b, "out")
                v.tensor_tensor(batch(X, b), batch(X, b), tokens(s, "out"), ALU.add).then_inc(free(s, "out"), 1)
                for name in FIRST_TAIL:
                    value_low(s, b, lows, int(name[1:]))
                latent_low(s, b, lows)
                step.end()
            step = Steps(A2, 0)
            attention(A2, 0, step, 1, None)
            A2.work.wait_ready(dve, 0, "out")
            v.tensor_tensor(batch(X, B - 1), batch(X, B - 1), tokens(A2, "out"), ALU.add
                            ).then_inc(free(A2, "out"), 1)
            step.end()

            def split_operand(s, b, step, w):
                step(v.tensor_copy(piece[:, w, 0, :], qk[:, :]))
                step(v.tensor_tensor(rot[:, 0, :], qk[:, :], piece[:, w, 0, :], ALU.subtract))
                step(v.tensor_copy(piece[:, w, 1, :], rot[:, 0, :]))
                v.tensor_tensor(piece[:, w, 2, :], rot[:, 0, :], piece[:, w, 1, :], ALU.subtract
                                ).then_inc(s.split.sem, 1)
                dve.wait_ge(s.split.sem, s.split.at(b, w + 1))

            def pieces_out(s, b, w):
                if w == 0:
                    dve.wait_ge(s.spilt.sem, s.spilt.at(b, 0))

            def stripes_low(s, b):
                dve.wait_ge(s.stripes.sem, s.stripes.at(b, 1))
                src = bank(s, "v")[:, :].rearrange("p (g h d) -> p g h d", h=GROUP, d=HD_S)
                v.tensor_tensor(stripes(1), src, stripes(0).bitcast(F32), ALU.subtract).then_inc(free(s, "v"), 1)

            def second_norms(s, b, step, xb, ub):
                step(layernorm(s, b, step, 0, xb, Ub))
                v.tensor_scalar(ub, Ub[:, :, :], 1.0, None, ALU.mult)
                layernorm(s, b, step, 1, Ub, H).then_inc(s.normed.sem, 1)

            def rotated(s, b, step, w):
                name, turn = (("q", "qr"), ("k", "kr"))[w]
                pieces_out(s, b, w)
                s.work.wait_ready(dve, b, name)
                v.tensor_tensor(rot[:, 0, :], bank(s, name)[:, :], cos[:, :], ALU.mult).then_inc(free(s, name), 1)
                s.work.wait_ready(dve, b, turn)
                v.tensor_tensor(rot[:, 1, :], bank(s, turn)[:, :], sin[:, :], ALU.mult).then_inc(free(s, turn), 1)
                s.work.wait_copied(dve, b, name)
                s.work.wait_copied(dve, b, turn)
                step(v.tensor_tensor(qk[:, :], rot[:, 0, :], rot[:, 1, :], ALU.add))
                split_operand(s, b, step, w)

            A2.work.wait_copied(dve, 0, "out")
            dve.wait_ge(zeroed, 1 + 2 * TILES)
            step = Steps(B0, 0)
            second_norms(B0, 0, step, X[:, 0:TILES, :], U[:, 0:TILES, :])
            dve.wait_ge(loaded_rot, 32)
            rotated(B0, 0, step, 0)
            rotated(B0, 0, step, 1)
            stripes_low(B0, 0)
            step.end()
            with dve.Fori(0, B - 1) as b:
                s, step = B1, Steps(B1, b)

                def following(n):
                    if n == NORM_STEP:
                        second_norms(s, b, step, batch(X, b + 1), batch(U, b + 1))
                    for w in range(2):
                        if n == OPERAND_STEP + 4 * w + 2:
                            rotated(s, b, step, w)

                attention(s, b, step, GROUP, following)
                s.work.wait_ready(dve, b, "out")
                v.tensor_tensor(batch(U, b), batch(U, b), tokens(s, "out"), ALU.add).then_inc(free(s, "out"), 1)
                stripes_low(s, b)
                step.end()
            step = Steps(B2, 0)
            attention(B2, 0, step, GROUP, None)
            B2.work.wait_ready(dve, 0, "out")
            v.tensor_tensor(batch(U, B - 1), batch(U, B - 1), tokens(B2, "out"), ALU.add
                            ).then_inc(free(B2, "out"), 1)
            step.end()

            B2.work.wait_copied(dve, 0, "out")
            with dve.Fori(0, B) as b:
                s, step = M_, Steps(M_, b)
                layernorm(s, b, step, 0, U[:, bass.ds(b * TILES, TILES), :], H).then_inc(s.normed.sem, 1)

                def spread(row):
                    return row.rearrange("p (i o) -> p i o", o=1).to_broadcast([P, TILES, EXPERTS])

                s.work.wait_ready(dve, b, "logits")
                logits = bank(s, "logits")[:, 0:TILES * EXPERTS].rearrange("p (i e) -> p i e", e=EXPERTS)
                step(v.tensor_reduce(lmax[:, :], logits, AX_X, ALU.max))
                v.tensor_tensor(lg[:, :, :], logits, spread(lmax[:, :]), ALU.subtract
                                ).then_inc(free(s, "logits"), 1)
                dve.wait_ge(m_exp.sem, m_exp.at(b, 1))
                step(v.tensor_reduce(lsum[:, :], gates[:, :, :], AX_X, ALU.add))
                step(v.reciprocal(lsum[:, :], lsum[:, :]))
                step(v.tensor_tensor(gates[:, :, :], gates[:, :, :], spread(lsum[:, :]), ALU.mult))

                def first_peak(src, dst):
                    step(v.tensor_reduce(lmax[:, :], src, AX_X, ALU.max))
                    step(v.tensor_tensor(rank[:, :, :], src, spread(lmax[:, :]), ALU.is_equal))
                    step(v.tensor_tensor(rank[:, :, :], rank[:, :, :], order[:, :, :], ALU.mult))
                    step(v.tensor_reduce(lmax[:, :], rank[:, :, :], AX_X, ALU.max))
                    step(v.tensor_tensor(dst, rank[:, :, :], spread(lmax[:, :]), ALU.is_equal))

                first_peak(gates[:, :, :], maskf[:, :, :])
                step(v.scalar_tensor_tensor(gsel[:, :, :], maskf[:, :, :], -2.0, gates[:, :, :], ALU.mult, ALU.add))
                first_peak(gsel[:, :, :], keep[:, :, :])
                step(v.tensor_tensor(maskf[:, :, :], maskf[:, :, :], keep[:, :, :], ALU.add))
                for i in range(TILES):
                    step(v.tensor_tensor(before[:, i + 1, :], before[:, i, :], maskf[:, i, :], ALU.add))
                v.tensor_copy(maskb16[:, :, :], maskf[:, :, :])
                step(v.tensor_copy(before16[:, :, :], before[:, 0:TILES, :]))
                v.tensor_copy(before[:, 0, :], before[:, TILES, :]).then_inc(m_masks.sem, 1)
                s.work.wait_ready(dve, b, "count")
                count = bank(s, "count")[:, 0:TILES * EXPERTS].rearrange("p (i e) -> p i e", e=EXPERTS)
                v.tensor_scalar(keep[:, :, :], count, float(CAP), None, ALU.is_le).then_inc(free(s, "count"), 1)
                s.work.wait_copied(dve, b, "count")
                step(v.tensor_tensor(keep[:, :, :], keep[:, :, :], maskf[:, :, :], ALU.mult))
                v.tensor_tensor(ge[:, :, :], keep[:, :, :], gates[:, :, :], ALU.mult).then_inc(m_gate.sem, 1)
                s.work.wait_ready(dve, b, "gT")
                v.tensor_copy(rsum[0:EXPERTS, :], bank(s, "gT")[0:EXPERTS, :]
                              ).then_inc(free(s, "gT"), 1)
                s.work.wait_ready(dve, b, "b2")
                v.tensor_tensor(acc[:, :, :], U[:, bass.ds(b * TILES, TILES), :],
                                bank(s, "b2")[:, :].rearrange("p (i c) -> p i c", c=C), ALU.add
                                ).then_inc(free(s, "b2"), 1)
                s.work.wait_copied(dve, b, "b2")
                for e in range(EXPERTS):
                    dve.wait_ge(m_out.sem, m_out.at(b, e + 1))
                    for i in range(TILES):
                        last = v.scalar_tensor_tensor(acc[:, i, :], pv[e % PV_BANKS][:, i * C:(i + 1) * C],
                                                      ge[:, i, e:e + 1], acc[:, i, :], ALU.mult, ALU.add)
                    last.then_inc(m_acc.sem, 1)
                    dve.wait_ge(m_acc.sem, m_acc.at(b, e + 1))
                v.tensor_tensor(X[:, bass.ds(b * TILES, TILES), :], X[:, bass.ds(b * TILES, TILES), :],
                                acc[:, :, :], ALU.add).then_inc(s.done.sem, 1)
                step.end()

            def plain(s, b, step, w):
                name = "qk"[w]
                pieces_out(s, b, w)
                s.work.wait_ready(dve, b, name)
                v.tensor_copy(qk[:, :], bank(s, name)[:, :]).then_inc(free(s, name), 1)
                s.work.wait_copied(dve, b, name)
                split_operand(s, b, step, w)

            dve.wait_ge(M_.done.sem, B)
            step = Steps(C0, 0)
            layernorm(C0, 0, step, 0, X[:, 0:TILES, :], H).then_inc(C0.normed.sem, 1)
            plain(C0, 0, step, 0)
            plain(C0, 0, step, 1)
            stripes_low(C0, 0)
            step.end()
            with dve.Fori(0, B - 1) as b:
                s, step = C1, Steps(C1, b)

                def following(n):
                    if n == NORM_STEP:
                        layernorm(s, b, step, 0, batch(X, b + 1), H).then_inc(s.normed.sem, 1)
                    for w in range(2):
                        if n == OPERAND_STEP + 2 * w:
                            plain(s, b, step, w)

                attention(s, b, step, GROUP, following)
                s.work.wait_ready(dve, b, "out")
                step(v.tensor_tensor(batch(X, b), batch(X, b), bos, ALU.add))
                v.tensor_tensor(batch(X, b), batch(X, b), tokens(s, "out"), ALU.add).then_inc(free(s, "out"), 1)
                stripes_low(s, b)
                step.end()
            step = Steps(C2, 0)
            attention(C2, 0, step, GROUP, None)
            C2.work.wait_ready(dve, 0, "out")
            step(v.tensor_tensor(batch(X, B - 1), batch(X, B - 1), bos, ALU.add))
            v.tensor_tensor(batch(X, B - 1), batch(X, B - 1), tokens(C2, "out"), ALU.add
                            ).then_inc(free(C2, "out"), 1)
            step.end()

            dve.wait_ge(loaded_f, 16 * 3)
            v.tensor_scalar(Wf[:, :], WfI[:, :], float(np.float32(1.0 / 127.0)), None, ALU.mult).then_inc(ffn_weights, 1)
            C2.work.wait_copied(dve, 0, "out")
            with dve.Fori(0, B) as b:
                s, step = F_, Steps(F_, b)
                xb = X[:, bass.ds(b * TILES, TILES), :]
                layernorm(s, b, step, 0, xb, H).then_inc(s.normed.sem, 1)
                for f in range(HT):
                    s.work.wait_copied(dve, b, f"g{f}")
                    s.work.wait_ready(dve, b, f"u{f}")
                    v.tensor_tensor(hidF[:, f, :], bank(s, f"u{f}")[:, :], siluF[:, f, :], ALU.mult
                                    ).then_inc(free(s, f"u{f}"), 1)
                s.work.wait_ready(dve, b, "out")
                v.tensor_tensor(xb, xb, bank(s, "out")[:, :].rearrange("p (i c) -> p i c", c=C), ALU.add
                                ).then_inc(free(s, "out"), 1)
                step.end()


def constants():
    r = np.arange(P)
    ident = np.eye(P, dtype=np.float32)
    mask = np.where(r[None, :] > r[:, None], np.float32(-1e30), np.float32(0))
    sel = np.zeros((P, GROUP, P), np.float32)
    for k in range(PIECES):
        for j in range(GROUP):
            sel[32 * k + j, j, :] = 1
    inv_freq = np.float32(1.0) / np.float32(10000.0) ** (np.arange(0, HD_S, 2, dtype=np.float32) / np.float32(HD_S))
    ang = np.arange(T, dtype=np.float32)[None, :] * inv_freq.astype(np.float32)[:, None]
    cos = np.tile(np.cos(ang).astype(np.float32), (C // len(inv_freq), 1))
    sin = np.tile(np.sin(ang).astype(np.float32), (C // len(inv_freq), 1))
    tri = (r[:, None] <= r[None, :]).astype(np.float32)
    order = np.broadcast_to(EXPERTS - np.arange(EXPERTS, dtype=np.float32), (P, TILES, EXPERTS))
    return dict(ident=ident, mask=mask, maskT=mask.T, cos=cos, sin=sin, sel=sel, tri=tri, order=order.astype(np.float32))


def kernel(**inputs):
    import concourse.bacc as _bacc
    from concourse import mybir as _mybir
    from concourse.bass_utils import run_bass_kernel_spmd as _run

    a = {k: np.asarray(v) for k, v in inputs.items()}
    up = a["L0_attn_w_kv_up"]
    hd = HEADS * HD_A
    qkv = a["L0_ffn_Wqkv"].reshape(C, HEADS, 3 * HD_S)
    bq, bk, bv = [qkv[:, :, k * HD_S:(k + 1) * HD_S] for k in range(3)]

    def turned(w):
        return np.concatenate([w[:, :, HD_S // 2:], w[:, :, :HD_S // 2]], axis=2)

    def twice(w):
        w = w.reshape(GROUPS, 1, C // GROUPS, C)
        return np.concatenate([w, w], axis=1).reshape(2 * C, C)

    data = {
        "x": a["L0_attn_x"].reshape(B * T, C),
        "w_down": a["L0_attn_w_kv_down"], "w_upv": up[:, hd:],
        "w_qT": a["L0_attn_w_q"].T, "w_kT": up[:, :hd].T, "w_out": a["L0_attn_w_out"],
        "ln1g": a["L0_ffn_ln1_g"].reshape(C, 1), "ln1b": a["L0_ffn_ln1_b"].reshape(C, 1),
        "b_wq": bq.reshape(C, C), "b_wqr": turned(bq).reshape(C, C),
        "b_wk": bk.reshape(C, C), "b_wkr": turned(bk).reshape(C, C), "b_wv": bv.reshape(C, C),
        "b_wo": twice(a["L0_ffn_Wproj"]),
        "ln2g": a["L0_ffn_ln2_g"].reshape(C, 1), "ln2b": a["L0_ffn_ln2_b"].reshape(C, 1),
        "w_gate": a["L0_ffn_Wgate"], "w1": a["L0_ffn_W1"],
        "b1": a["L0_ffn_b1"].reshape(EXPERTS * FT, P).T,
        "w2": a["L0_ffn_W2"].reshape(EXPERTS * FFN, C), "b2": a["L0_ffn_b2"],
        "c_wq": a["L1_attn_Wq"], "c_wk": a["L1_attn_Wk"], "c_wv": a["L1_attn_Wv"], "c_wo": twice(a["L1_attn_Wo"]),
        "c_bo": a["L1_attn_bo"].reshape(1, C),
        "f_gate": a["L1_ffn_w_gate"].T, "f_up": a["L1_ffn_w_up"].T, "f_down": a["L1_ffn_w_down"].T,
    }
    table = constants()
    sign = np.where(np.arange(C) % HD_S < HD_S // 2, np.float32(-1), np.float32(1))[:, None]
    table["sin"] = table["sin"] * sign
    data.update(table)

    nc = _bacc.Bacc("TRN2", target_bir_lowering=False, num_devices=1)
    arrays, args = {}, []
    for name, value in data.items():
        value = np.ascontiguousarray(value)
        arrays[f"in_{name}"] = value
        args.append(nc.dram_tensor(f"in_{name}", value.shape, _mybir.dt.from_np(value.dtype),
                                   kind="ExternalInput").ap())
    args.append(nc.dram_tensor("out_0", (B * T, C), F32, kind="ExternalOutput").ap())
    program(nc, *args)
    r = _run(nc, [arrays], core_ids=[0])
    return r.results[0]["out_0"].reshape(B, T, C)
```

```python
from contextlib import ExitStack

import numpy as np

import concourse.bass as bass
from concourse import mybir

F32 = mybir.dt.float32
F32R = mybir.dt.float32r
BF16 = mybir.dt.bfloat16
I32 = mybir.dt.int32
ALU = mybir.AluOpType
ACT = mybir.ActivationFunctionType
AX_X = mybir.AxisListType.X

P = 128
HALF = P // 2
B, T, C = 4, 512, 128
TILES = T // P
HEADS = 16
HD_A = 64
HD_S = C // HEADS
PIECES = 3
STACK = PIECES * PIECES * HD_S
EXPERTS, FFN, CAP = 8, 512, 512
FT = FFN // P
HID = 384
HT = HID // P
EPS = 1e-5
GROUP = 4
GROUPS = HEADS // GROUP
SHIFT_ROW = 96
SHIFTED = SHIFT_ROW + PIECES * GROUP
PAIR_TILES = 5
ST_TILES = HEADS // 2 * PAIR_TILES
GROUP_TILES = GROUP // 2 * PAIR_TILES
AHEAD = 15
CONSTS, TABLES = 2, 6
M_STEPS = 26
LAG = 3
STEPS = ST_TILES + LAG
P_RING = 4
FULL_RING = 4
ST_BANKS = 3
PV_BANKS = 2
WORK_BANKS = 3
STRIPE = P + HD_S
BLOCKS = 5 * P
NORM_STEP, NORM_WAIT, TURN_STEP, LATENT_STEP = 0, 2, 5, 10
SMALL_TURN_STEP, OPERAND_STEP = 6, 8
STACK_READS = 2 * PIECES


def query_step(h):
    return min(max(PAIR_TILES * (h // 2 + 1) + 1, TURN_STEP + 2) + 2 * (h % 2), STEPS - 1)


EARLY_VALUES = range(0, 2 * TILES, 2)
LATE_VALUES = range(1, 2 * TILES, 2)
LATE_BEFORE, LATE_AFTER = LATE_VALUES[:TILES // 2], LATE_VALUES[TILES // 2:]


def value_step(k):
    return 26 + k


def pair_tile(n):
    a, k = 2 * (n // PAIR_TILES), n % PAIR_TILES
    return [
        [(a, 0, 0, 512)],
        [(a, 1, 0, 384), (a, 3, 384, 128)],
        [(a + 1, 0, 0, 512)],
        [(a, 2, 0, 256), (a + 1, 2, 256, 256)],
        [(a + 1, 1, 0, 384), (a + 1, 3, 384, 128)],
    ][k]


def max_tile(m):
    a, k = 2 * (m // PAIR_TILES), m % PAIR_TILES
    return [
        [(a, 3, 0, 512)],
        [(a, 2, 0, 384), (a, 0, 384, 128)],
        [(a + 1, 3, 0, 512)],
        [(a, 1, 0, 256), (a + 1, 1, 256, 256)],
        [(a + 1, 2, 0, 384), (a + 1, 0, 384, 128)],
    ][k]


class Tally:

    def __init__(self, sem, per, start=0):
        self.sem, self.per, self.start = sem, per, start

    def at(self, b, k):
        return b * self.per + (self.start + k)

    def after(self, batches, per):
        return Tally(self.sem, per, self.start + batches * self.per)


class Work:

    def __init__(self, names, ready, free):
        self.names, self.ready, self.free = names, ready, free
        self.index = {name: n for n, name in enumerate(names)}
        assert len(self.index) == len(names)

    @classmethod
    def first(cls, names, ready, free):
        return cls(names, Tally(ready, len(names)), [Tally(f, u, 1) for f, u in zip(free, cls.uses(names))])

    @staticmethod
    def uses(names):
        return [len(range(k, len(names), WORK_BANKS)) for k in range(WORK_BANKS)]

    def then(self, batches, names):
        return Work(names, self.ready.after(batches, len(names)),
                    [t.after(batches, u) for t, u in zip(self.free, self.uses(names))])

    def bank(self, name):
        return self.index[name] % WORK_BANKS

    def wait_free(self, eng, b, name):
        n = self.index[name]
        t = self.free[n % WORK_BANKS]
        eng.wait_ge(t.sem, t.at(b, n // WORK_BANKS))

    def wait_copied(self, eng, b, name):
        n = self.index[name]
        t = self.free[n % WORK_BANKS]
        eng.wait_ge(t.sem, t.at(b, n // WORK_BANKS + 1))

    def wait_ready(self, eng, b, name):
        eng.wait_ge(self.ready.sem, self.ready.at(b, self.index[name] + 1))


def first_operands():
    return ["hT", "lat"] + [f"q{h}" for h in range(HEADS)] + [f"v{k}" for k in range(2 * TILES)]


def max_of(n):
    m = n + AHEAD
    return m % ST_TILES, m >= ST_TILES


def attention_names(own, following, tail):
    names = []
    for n in range(STEPS):
        m, is_next = max_of(n)
        if n < ST_TILES and not is_next:
            names.append(f"max{m}")
        if n < ST_TILES and is_next and following is not None:
            names.append(f"next_max{m}")
        g = n // GROUP_TILES + 1
        if n < ST_TILES and n % GROUP_TILES == GROUP_TILES - 3:
            if g < GROUPS:
                names.append(f"turn{g}")
            elif following is not None:
                names.append("next_turn")
        names += own(n)
        if following is not None:
            names += following(n)
    return names + tail


FIRST_MAXIMA = [f"max{m}" for m in range(AHEAD)] + ["turn0"]
ROTATED = {"q": 0, "qr": 1, "k": 4, "kr": 5}
PLAIN = {"q": 0, "k": 4}
SECOND_NORM_STEP, SECOND_TURN_STEP, SECOND_OPERAND_STEP = 11, 17, 20


def nothing(n):
    return []


def before_second(n):
    return (["hT"] * (n == SECOND_TURN_STEP)
            + [x for x, later in ROTATED.items() if n == SECOND_OPERAND_STEP + later])


def first_following(n):
    names = ["hT"] * (n == TURN_STEP) + ["lat"] * (n == LATENT_STEP)
    names += [f"q{h}" for h in range(HEADS) if query_step(h) == n]
    return names + [f"v{k}" for k in EARLY_VALUES if value_step(k) == n]


LOGITS_STEP, PEAK_STEP, EXP_STEP, FIRST_CHOICE_STEP, SECOND_CHOICE_STEP, COUNT_STEP, KEEP_STEP = 9, 10, 11, 13, 15, 19, 20


WEIGHT_STEP = 22


def before_experts(n):
    return (["hT"] * (n == SMALL_TURN_STEP) + ["logits"] * (n == LOGITS_STEP)
            + ["count"] * (n == COUNT_STEP))


def before_ffn(n):
    return ["hT"] * (n == SMALL_TURN_STEP)


def expert_names(following):
    names = []
    for e in range(EXPERTS):
        names += [f"h{e}.{f}" for f in range(FT)] + ["gT"] * (e == 0) + ["b2"] * (e == 1) + following(e)
    return names


def next_routing(e):
    return ["hT"] * (e == 2) + ["logits"] * (e == 3) + ["count"] * (e == 6)


def third_attention(e):
    return ["hT"] * (e == 2) + ["q"] * (e == 3) + ["k"] * (e == 4)


FFN_NAMES = [f"{w}{f}" for f in range(HT) for w in "gu"]


def small_following(products):
    def at(n):
        names = ["hT"] * (n == SMALL_TURN_STEP)
        return names + [x for x, later in products.items() if n == OPERAND_STEP + later]
    return at


def finished(n, per_bank):
    k = n % PAIR_TILES
    if n < 0 or k < PAIR_TILES - 2:
        return None
    h = 2 * (n // PAIR_TILES) + k - (PAIR_TILES - 2)
    return h // per_bank if h % per_bank == per_bank - 1 else None


def last_tile(use, per_bank):
    h = use * per_bank + per_bank - 1
    return PAIR_TILES * (h // 2) + PAIR_TILES - 2 + h % 2


def division_steps(per_bank):
    at = {}
    for p in range(HEADS // per_bank // 2):
        for k in range(TILES + 1):
            at.setdefault(min(last_tile(2 * p + 1, per_bank) + LAG + 2 + k, STEPS), []).append((p, k))
    return at


def program(nc, x, w_down, w_upv, w_qT, w_kT, w_out, ln1g, ln1b, w_small,
            ln2g, ln2b, w_gate, w1, b1, w2, b2, c_bo, f_gate, f_up, f_down,
            ident_d, mask_d, maskT_d, cos_d, sin_d, sel_d, ksel_d, tri_d, order_d, out):
    with ExitStack() as ctx:
        def sb(name, shape, dt=F32):
            return ctx.enter_context(nc.sbuf_tensor(name, shape, dt))

        def sem(name):
            return ctx.enter_context(nc.semaphore(name))

        work = [ctx.enter_context(nc.psum_tensor(f"work{k}", [P, 512], F32)) for k in range(WORK_BANKS)]
        st = [ctx.enter_context(nc.psum_tensor(f"scores{k}", [P, 512], F32)) for k in range(ST_BANKS)]
        pv = [ctx.enter_context(nc.psum_tensor(f"values{k}", [P, 512], F32)) for k in range(PV_BANKS)]

        X = sb("X", [P, B * TILES, C])
        H = sb("H", [P, TILES, C])
        qk = H[:, :, :].rearrange("p i c -> p (i c)")
        small = sb("small", [P, 12, C])
        stats = sb("stats", [P, TILES, 6])
        mean = sb("mean", [P, TILES, 4])
        mv = sb("mv", [P, TILES, 2])
        veps = sb("veps", [P, TILES])
        rstd = sb("rstd", [P, TILES])
        neghalf = sb("neghalf", [P, TILES])
        hT = sb("hT", [P, T])
        latent = sb("latent", [P, T])
        yT = sb("yT", [P, HEADS // 2, T])
        U = yT[:, 4:8, :].rearrange("p a (i c) -> p (a i) c", c=C)
        Ub = latent[:, :].rearrange("p (i c) -> p i c", c=C)
        acc = Ub
        sums = sb("sums", [P, 2, T])
        full = sb("full", [P, FULL_RING, 512])
        PH = sb("PH", [P, P_RING, 512], F32R)
        PL = sb("PL", [P, P_RING, 512], F32R)
        MX = sb("MX", [P, 2, TILES, GROUP])
        MR = sb("MR", [P, TILES, GROUP])
        MS = sb("MS", [P, TILES, P], BF16)
        MT = sb("MT", [P, 2, T], BF16)

        def shared(*groups):
            out, most = [], 0
            for group in groups:
                size = 0
                with ExitStack() as lent:
                    for name, shape, dt in group:
                        out.append(lent.enter_context(nc.sbuf_tensor(name, shape, dt)))
                        size += int(np.prod(shape[1:])) * (2 if dt == BF16 else 4)
                most = max(most, size)
            sb("under_" + groups[0][0][0], [P, most // 4])
            return out

        QH, QL, QS, KS, W1, W2, _, W1H = shared(
            [("QH", [P, HEADS, T], F32R), ("QL", [P, HEADS, T], F32R)],
            [("QS", [P, HEADS, T], BF16), ("KS", [P, HEADS, T], BF16),
             ("W1", [P, EXPERTS, FFN], F32), ("W2", [P, EXPERTS * FT, C], F32)],
            [("under_stacks", [P, HEADS * T], F32), ("W1H", [P, EXPERTS, FFN], F32R)])
        VH, VL, VS, W1Lb = shared(
            [("VH", [P, TILES, HEADS, P], F32R), ("VL", [P, TILES, HEADS, HD_A], F32R)],
            [("VS", [P, TILES * GROUPS, BLOCKS], F32R), ("W1Lb", [P, EXPERTS // 2, FFN], F32R)])
        M, Wv, latN, Wo, latH, latL, piece, cos, rot, sin, W1La, _, hEH, _, hEL, WfI, Wf = shared(
            [("M", [P, HEADS, P], F32), ("Wv", [P, HEADS * HD_A], F32), ("latN", [P, T], F32R),
             ("Wo", [P, HEADS // 2, C], F32), ("latH", [P, T], F32R), ("latL", [P, T], F32R)],
            [("piece", [P, 2, PIECES, T], BF16), ("cos", [P, T], F32), ("rot", [P, 2, T], F32), ("sin", [P, T], F32),
             ("W1La", [P, EXPERTS // 2, FFN], F32R)],
            [("under_piece", [P, PIECES * T], F32), ("hEH", [P, T], F32R), ("under_rot", [P, 2 * T], F32),
             ("hEL", [P, T], F32R)],
            [("WfI", [P, 3 * HID], I32), ("Wf", [P, 3 * HID], F32)])
        identf = sb("identf", [P, P])
        identb = sb("identb", [P, P], BF16)
        maskb = sb("maskb", [P, P], BF16)
        maskTb = sb("maskTb", [P, P], BF16)
        selb = sb("selb", [P, GROUP, P], BF16)
        ksel = sb("ksel", [SHIFTED - STACK, GROUP, HALF], BF16)
        trib = sb("trib", [P, P], BF16)
        onesb = sb("onesb", [P, P], BF16)
        Wd, bo = shared([("Wd", [P, P], F32)], [("bo", [P, C], F32)])
        WqT = yT[:, 0:2, :].rearrange("p a (b c) -> p (a b) c", c=C)
        WkT = yT[:, 2:4, :].rearrange("p a (b c) -> p (a b) c", c=C)
        BWq, BWqr, BWk, BWkr, BWv, CWq, CWk, CWv = [small[:, k, :] for k in range(8)]
        BWo, CWo = small[:, 8:10, :], small[:, 10:12, :]
        bos = bo[:, :].rearrange("p (o c) -> p o c", o=1).to_broadcast([P, TILES, C])
        ln = sb("ln", [P, 4])
        Wg = sb("Wg", [P, EXPERTS])
        b1s = sb("b1s", [P, EXPERTS, FT])
        b2s = sb("b2s", [EXPERTS, C])
        hidF = yT[:, 0:HT, :]
        siluF = yT[:, HT:2 * HT, :]
        lg = sb("lg", [P, TILES, EXPERTS])
        lmax = sb("lmax", [P, TILES])
        lsum = sb("lsum", [P, TILES])
        gates = sb("gates", [P, TILES, EXPERTS])
        next_ge = sb("next_ge", [P, TILES, EXPERTS])
        rank = sb("rank", [P, TILES, EXPERTS])
        order = sb("order", [P, TILES, EXPERTS])
        gsel = sb("gsel", [P, TILES, EXPERTS])
        maskf = sb("maskf", [P, TILES, EXPERTS])
        before = sb("before", [P, TILES + 1, EXPERTS])
        maskb16 = sb("maskb16", [P, TILES, EXPERTS], BF16)
        before16 = sb("before16", [P, TILES, EXPERTS], BF16)
        keep = sb("keep", [P, TILES, EXPERTS])
        ge = sb("ge", [P, TILES, EXPERTS])
        geT = sums[0:EXPERTS, 0, :].rearrange("e (i c) -> e i c", c=P)

        q_pieces = nc.dram_tensor("q_pieces", [HEADS, PIECES, HD_S, T], BF16).ap()
        k_pieces = nc.dram_tensor("k_pieces", [HEADS, 2 * PIECES - 1, HD_S, T], BF16).ap()

        loaded_x, loaded_rest, loaded_fold = sem("loaded_x"), sem("loaded_rest"), sem("loaded_fold")
        loaded_a, loaded_const = sem("loaded_a"), sem("loaded_const")
        loaded_tables, loaded_rot = sem("loaded_tables"), sem("loaded_rot")
        loaded_b, loaded_moe, loaded_f = sem("loaded_b"), sem("loaded_moe"), sem("loaded_f")
        setup, ones_filled = sem("setup"), sem("ones_filled")
        folded, fold_free = sem("folded"), sem("fold_free")
        zeroed = sem("zeroed")
        last_rows = sem("last_rows")
        stored = sem("stored")
        ffn_weights = sem("ffn_weights")
        w1_rounded, w1_low, w1_high = sem("w1_rounded"), sem("w1_low"), sem("w1_high")

        class Stage:

            def __init__(self, work, **tallies):
                self.work, self.tallies = work, tallies
                self.var, self.rstd, self.normed, self.step = [tallies.get(k) for k in (
                    "var", "rstd", "normed", "step")]
                self.scores, self.probs, self.low, self.pv = [tallies.get(k) for k in (
                    "scores", "probs", "low", "pv")]
                self.y, self.pieces, self.high, self.latents = [tallies.get(k) for k in (
                    "y", "pieces", "high", "latents")]
                self.split, self.spilt, self.stripes, self.done = [tallies.get(k) for k in (
                    "split", "spilt", "stripes", "done")]
                self.inverse, self.rows = [tallies.get(k) for k in ("inverse", "rows")]
                self.exp, self.masks, self.gate, self.taken, self.inputs = [tallies.get(k) for k in (
                    "exp", "masks", "gate", "taken", "inputs")]
                self.expert, self.added = tallies.get("expert"), tallies.get("added")
                self.summed = tallies.get("summed")
                self.stack = [tallies.get(f"stack{g}") for g in range(GROUPS)]

            @classmethod
            def first(cls, tag, work, norms=1, **others):
                tallies = {"var": (norms, 0), "rstd": (norms, 0), "normed": (1, 0), **others}
                return cls(work, **{k: Tally(sem(f"{tag}_{k}"), per, start) for k, (per, start) in tallies.items()})

            def then(self, batches, work, **per):
                return Stage(work,
                             **{k: t.after(batches, per.get(k, t.per)) for k, t in self.tallies.items()})

        def attention_phases(tag, work, following, tail, last_own, last_tail, uses, steps, norms=1, last_steps=0, **others):
            first = Stage.first(tag, work, norms=norms, step=(steps + 3, 0), scores=(0, 0),
                                probs=(0, ST_BANKS), low=(0, FULL_RING), pv=(0, P_RING), y=(0, PV_BANKS), summed=(0, 0),
                                inverse=(0, 0), rows=(0, 2 * TILES), pieces=(1, 0),
                                **{k: (per[0], 0) for k, per in others.items()})
            core = dict(scores=ST_TILES, probs=ST_TILES, low=ST_TILES, pv=ST_TILES, y=uses, summed=uses,
                        inverse=uses // 2 * TILES, rows=uses // 2 * TILES)
            loop = first.then(1, work.then(1, attention_names(nothing, following, tail)), step=steps + 3 * GROUPS + last_steps,
                              pieces=GROUPS, **core, **{k: per[1] for k, per in others.items()})
            last = loop.then(B - 1, loop.work.then(B - 1, attention_names(last_own, None, last_tail)), step=3 * (GROUPS - 1) + last_steps,
                             pieces=GROUPS - 1, var=0, rstd=0, normed=0, **core,
                             **{k: per[2] for k, per in others.items()})
            return first, loop, last

        def small_phases(tag, work, products, last_own, norms, steps, last_steps=0):
            spills = 16 * (3 * PIECES - 1)
            stacks = {f"stack{g}": (16 * STACK_READS, 16 * STACK_READS, 0) for g in range(GROUPS)}
            return attention_phases(tag, work, small_following(products), ["v", "out"], last_own, ["out"], GROUPS, steps,
                                    norms, last_steps, split=(2, 2, 0), spilt=(spills, spills, 0),
                                    stripes=(1, 1, 0), **stacks)

        highs = HEADS + 2 * TILES + 1
        A0, A1, A2 = attention_phases("a", Work.first(first_operands() + FIRST_MAXIMA, sem("product_ready"),
                                                      [sem(f"bank{k}_free") for k in range(WORK_BANKS)]),
                                      first_following, [*(f"v{k}" for k in LATE_BEFORE), "out",
                                                        *(f"v{k}" for k in LATE_AFTER)],
                                      before_second, FIRST_MAXIMA + ["v", "out"], HEADS, 3,
                                      high=(highs, highs, 0), latents=(1, 1, 0))
        B0, B1, B2 = small_phases("b", A2.work, ROTATED, before_experts, 2, 15)
        M0 = Stage.first("m", B2.work, step=(M_STEPS, 0), exp=(1, 0), masks=(1, 0), gate=(1, 0), taken=(1, 0), inputs=(1, 0),
                         expert=(0, 0), added=(0, PV_BANKS), done=(0, 0))
        M1 = M0.then(1, B2.work.then(1, expert_names(next_routing)), expert=EXPERTS, added=EXPERTS, done=1)
        M2 = M1.then(B - 1, M1.work.then(B - 1, expert_names(third_attention) + FIRST_MAXIMA + ["v"]),
                     step=0, exp=0, masks=0, gate=0, taken=0, inputs=0, var=0, rstd=0, normed=0)
        C0, C1, C2 = small_phases("c", M2.work, PLAIN, before_ffn, 1, 9, 1)
        F0 = Stage.first("f", C2.work, step=(3, 0))
        F1 = F0.then(1, C2.work.then(1, FFN_NAMES + ["hT", "out"]))
        F2 = F1.then(B - 1, F1.work.then(B - 1, FFN_NAMES + ["out"]))

        def w1_low_part(e):
            return (W1La, W1Lb)[e // (EXPERTS // 2)][:, e % (EXPERTS // 2), :]

        def hid2(e):
            return (full, yT)[e % 2][:, 0:FT, :]

        def first_values(k):
            i, heads = k // 2, slice(k % 2 * 8, k % 2 * 8 + 8)
            return VH[:, i, heads, 0:HD_A], VL[:, i, heads, :]

        def stripes(place):
            at = VS[:, :, 4 * HD_S * place:4 * HD_S * place + GROUP * STRIPE]
            return at.rearrange("p g (h c) -> p g h c", c=STRIPE)[:, :, :, 0:HD_S]

        block = ctx.enter_context(nc.Block())

        @block.sync
        def _(sp):
            for t in A0.work.free:
                sp.sem_inc(t.sem, t.start)
            for s in (A0, B0, C0):
                for t in (s.probs, s.low, s.pv, s.y, s.rows):
                    sp.sem_inc(t.sem, t.start)
            sp.sem_inc(M0.added.sem, M0.added.start)
            sp.sem_inc(fold_free, WORK_BANKS)
            tokens_in = x.rearrange("(t p) c -> p t c", p=P)
            sp.dma_start(X[:, 0:TILES, :], tokens_in[:, 0:TILES, :]).then_inc(loaded_x, 16)
            for dst, src in ((WqT, w_qT.rearrange("(a p) c -> p a c", p=P)),
                             (WkT, w_kT.rearrange("(a p) c -> p a c", p=P))):
                sp.dma_start(dst, src).then_inc(loaded_fold, 16)
            for dst, src in ((identf[:, :], ident_d), (order[:, :, :], order_d)):
                sp.dma_start(dst, src).then_inc(loaded_const, 16)
            sp.dma_start(X[:, TILES:, :], tokens_in[:, TILES:, :]).then_inc(loaded_rest, 16)
            for dst, src in ((Wd[:, :], w_down), (Wv[:, :], w_upv),
                             (Wo[:, :, :], w_out.rearrange("(a p) c -> p a c", p=P))):
                sp.dma_start(dst, src).then_inc(loaded_a, 16)
            for dst, src in ((ln[:, 0:1], ln1g), (ln[:, 1:2], ln1b), (ln[:, 2:3], ln2g), (ln[:, 3:4], ln2b)):
                sp.dma_start(dst, src).then_inc(loaded_b, 16)
            sp.dma_start(small[:, :, :], w_small.rearrange("(a p) c -> p a c", p=P)).then_inc(loaded_b, 16)

            def spill(s, b):
                for w, home in enumerate((q_pieces, k_pieces)):
                    sp.wait_ge(s.split.sem, s.split.at(b, w + 1))
                    for place in range(home.shape[1]):
                        sp.dma_start(home[:, place], piece[:, w, place % PIECES, :]).then_inc(s.spilt.sem, 16)
                sp.wait_ge(s.spilt.sem, s.spilt.at(b, s.spilt.per))

            def stack_queries(s, g):
                heads = slice(GROUP * g, GROUP * g + GROUP)
                for r in range(PIECES):
                    rows = slice(r * PIECES * HD_S, (r + 1) * PIECES * HD_S)
                    sp.dma_start(QS[rows, heads, :], q_pieces[heads].rearrange("h g d t -> (g d) h t")
                                 ).then_inc(s.stack[g].sem, 16)

            def stack_keys(s, g):
                heads = slice(GROUP * g, GROUP * g + GROUP)
                for r in range(PIECES):
                    rows = slice(r * PIECES * HD_S, (r + 1) * PIECES * HD_S)
                    sp.dma_start(KS[rows, heads, :], k_pieces[heads, r:r + PIECES].rearrange("h g d t -> (g d) h t")
                                 ).then_inc(s.stack[g].sem, 16)

            def spill_and_stack(s, b):
                spill(s, b)
                for g in range(GROUPS):
                    sp.wait_ge(s.scores.sem, s.scores.at(b, GROUP_TILES * (g + 1)))
                    stack_queries(s, g)
                    stack_keys(s, g)

            sp.wait_ge(loaded_tables, 16 * TABLES)
            sp.wait_ge(A2.scores.sem, A2.scores.at(0, 1))
            for dst, src in ((cos[:, :], cos_d), (sin[:, :], sin_d)):
                sp.dma_start(dst, src).then_inc(loaded_rot, 16)
            spill(B0, 0)
            for g in range(GROUPS):
                sp.wait_ge(A2.scores.sem, A2.scores.at(0, PAIR_TILES * (g + 1)))
                stack_queries(B0, g)
                rows = QS[STACK:SHIFT_ROW, GROUP * g:GROUP * g + GROUP, :].rearrange("p h (i c) -> p (h i) c", c=HALF)
                sp.dma_start(rows, ksel[0:SHIFT_ROW - STACK, 0:1, :].to_broadcast(
                    [SHIFT_ROW - STACK, GROUP * T // HALF, HALF])).then_inc(last_rows, 16)
            for g in range(GROUPS):
                sp.wait_ge(A2.scores.sem, A2.scores.at(0, PAIR_TILES * (GROUPS + g + 1)))
                stack_keys(B0, g)
            for h in range(HEADS):
                k = h % GROUP
                sp.dma_start(KS[STACK:SHIFTED, h, :].rearrange("p (i c) -> p i c", c=HALF),
                             ksel[:, k:k + 1, :].to_broadcast([SHIFTED - STACK, T // HALF, HALF])).then_inc(last_rows, 16)
            for dst, src in ((bo[:, :], c_bo.to_broadcast([P, C])), (Wg[:, :], w_gate), (W1[:, :, :], w1.rearrange("e d f -> d e f")),
                             (b1s[:, :, :], b1.rearrange("p (e f) -> p e f", e=EXPERTS)),
                             (W2[:, :, :], w2.rearrange("(a p) c -> p a c", p=P)), (b2s[:, :], b2)):
                sp.dma_start(dst, src).then_inc(loaded_moe, 16)
            with sp.Fori(0, B - 1) as b:
                spill_and_stack(B1, b)
            sp.wait_ge(B2.scores.sem, B2.scores.at(0, ST_TILES))
            spill(C0, 0)
            for g in range(GROUPS):
                stack_queries(C0, g)
                stack_keys(C0, g)
            with sp.Fori(0, B - 1) as b:
                spill_and_stack(C1, b)
            sp.wait_ge(C2.spilt.sem, C2.spilt.at(0, 0))
            for dst, src in ((WfI[:, 0:HID], f_gate), (WfI[:, HID:2 * HID], f_up),
                             (WfI[:, 2 * HID:3 * HID].rearrange("p (a c) -> p a c", c=C),
                              f_down.rearrange("(a p) c -> p a c", p=P))):
                sp.dma_start(dst, src).then_inc(loaded_f, 16)
            def store(s, b, to):
                s.work.wait_copied(sp, b, "out")
                rows = bass.ds(to * TILES, TILES)
                sp.dma_start(out.rearrange("(t p) c -> p t c", p=P)[:, rows, :], X[:, rows, :]).then_inc(stored, 16)

            with sp.Fori(0, B - 1) as b:
                store(F1, b, b)
            store(F2, 0, B - 1)
            sp.wait_ge(stored, 16 * B)

        @block.gpsimd
        def _(pool):
            nc.gpsimd.memset(neghalf[:, :], -0.5).then_inc(setup, 1)
            nc.gpsimd.memset(MS[:, :, :], 0.0).then_inc(setup, 1)
            nc.gpsimd.memset(onesb[:, :], 1.0).then_inc(setup, 1)
            nc.gpsimd.memset(before[:, 0, :], 0.0).then_inc(setup, 1)
            pool.wait_ge(setup, 4)
            for dst, src in ((identb[:, :], ident_d), (maskb[:, :], mask_d), (maskTb[:, :], maskT_d),
                             (selb[:, :, :], sel_d), (ksel[:, :, :], ksel_d), (trib[:, :], tri_d)):
                pool.dma_start(dst, src).then_inc(loaded_tables, 16)

            def inverse_root(s, b, k):
                pool.wait_ge(s.var.sem, s.var.at(b, k + 1))
                nc.gpsimd.tensor_tensor(rstd[:, :], veps[:, :], neghalf[:, :], ALU.pow).then_inc(s.rstd.sem, 1)

            def low_part(s, b, n):
                pool.wait_ge(s.probs.sem, s.probs.at(b, n + 1))
                nc.gpsimd.tensor_tensor(PL[:, n % P_RING, :], full[:, n % FULL_RING, :],
                                        PH[:, n % P_RING, :].bitcast(F32), ALU.subtract).then_inc(s.low.sem, 1)

            def attention(s, b, following, norms, norm_step):
                for n in range(ST_TILES):
                    low_part(s, b, n)
                    for k in range(norms):
                        if n == norm_step + k * NORM_WAIT:
                            inverse_root(following, b, k)

            def stage(phases, norms, following, last_norms, last_norm_step):
                _, loop, last = phases
                with pool.Fori(0, B - 1) as b:
                    attention(loop, b, loop, norms, NORM_STEP)
                attention(last, 0, following, last_norms, last_norm_step)

            inverse_root(A0, 0, 0)
            nc.gpsimd.memset(VH[:, :, :, HD_A:2 * HD_A].bitcast(F32), 1.0).then_inc(ones_filled, 1)
            stage((A0, A1, A2), 1, B0, 2, SECOND_NORM_STEP)
            pool.wait_ge(A2.pv.sem, A2.pv.at(0, ST_TILES))
            nc.gpsimd.memset(VS[:, :, :].bitcast(F32), 0.0).then_inc(zeroed, 1)
            pool.wait_ge(zeroed, 1)
            for place in (2, 3):
                for i in range(TILES):
                    nc.gpsimd.memset(stripes(place)[:, GROUPS * i:GROUPS * (i + 1)].bitcast(F32), 1.0
                                     ).then_inc(zeroed, 1)
            stage((B0, B1, B2), 2, M0, 1, NORM_STEP)

            def inputs_low(s, b):
                pool.wait_ge(s.taken.sem, s.taken.at(b, 1))
                nc.gpsimd.tensor_tensor(hEL[:, :], hT[:, :], hEH[:, :].bitcast(F32), ALU.subtract
                                        ).then_inc(s.inputs.sem, 1)

            inputs_low(M0, 0)
            with pool.Fori(0, B - 1) as b:
                inverse_root(M1, b, 0)
                inputs_low(M1, b)
            inverse_root(C0, 0, 0)
            stage((C0, C1, C2), 1, F0, 1, NORM_STEP)
            with pool.Fori(0, B - 1) as b:
                inverse_root(F1, b, 0)

        @block.tensor
        def _(pe):
            def turn_h(s, b):
                pe.wait_ge(s.normed.sem, s.normed.at(b, 1))
                s.work.wait_free(pe, b, "hT")
                for i in range(TILES):
                    last = pe.transpose(work[s.work.bank("hT")][:, i * P:(i + 1) * P], H[:, i, :], identf[:, :])
                last.then_inc(s.work.ready.sem, 1)

            def product(s, b, name, lhsT, rhs):
                s.work.wait_free(pe, b, name)
                pe.matmul(work[s.work.bank(name)][:, :], lhsT, rhs, start=True, stop=True
                          ).then_inc(s.work.ready.sem, 1)

            def max_scores(s, b, name, m, passes):
                s.work.wait_free(pe, b, name)
                bank = work[s.work.bank(name)]
                for h, i, c, w in max_tile(m):
                    q, k = passes[0]
                    pe.matmul(bank[:, c:c + w], q(h, i * P, (i + 1) * P), k(h, 0, w), start=True, stop=False)
                    last = pe.matmul(bank[:, c + w - P:c + w], identb[:, :], maskb[:, :], start=False, stop=True)
                last.then_inc(s.work.ready.sem, 1)

            def turn_max(s, b, name, k):
                pe.wait_ge(s.pieces.sem, s.pieces.at(b, k))
                s.work.wait_free(pe, b, name)
                bank = work[s.work.bank(name)][:, :].bitcast(BF16)
                for i in range(TILES):
                    last = pe.transpose(bank[:, i * P:(i + 1) * P], MS[:, i, :], identb[:, :])
                last.then_inc(s.work.ready.sem, 1)

            def scores(s, b, n, passes):
                g = n // GROUP_TILES
                if g > 0 and n % GROUP_TILES == 0:
                    s.work.wait_copied(pe, b, f"turn{g}")
                pe.wait_ge(s.probs.sem, s.probs.at(b, max(n - ST_BANKS + 1, 0)))
                bank = st[n % ST_BANKS]
                for h, j, c, w in pair_tile(n):
                    q0 = j * P
                    for k, (q, key) in enumerate(passes):
                        pe.matmul(bank[:, c:c + w], key(h, q0, q0 + P), q(h, q0, q0 + w), start=k == 0, stop=False)
                    small = s.high is None
                    last = pe.matmul(bank[:, c:c + P], identb[:, :], maskTb[:, :], start=False, stop=small)
                    if not small:
                        last = pe.matmul(bank[:, c:c + w], selb[:, h % GROUP, :], MT[:, g % 2, q0:q0 + w],
                                         start=False, stop=True)
                last.then_inc(s.scores.sem, 1)

            def values(s, b, n, high, low, per_bank):
                pe.wait_ge(s.probs.sem, s.probs.at(b, n + 1))
                for part, of in ((PH, high), (PH, low), (PL, high)):
                    if of is None:
                        continue
                    if part is PL:
                        pe.wait_ge(s.low.sem, s.low.at(b, n + 1))
                    for h, j, c, w in pair_tile(n):
                        use = h // per_bank
                        first = part is PH and of is high and j == 0 and h % per_bank == 0
                        if first:
                            pe.wait_ge(s.y.sem, s.y.at(b, use - PV_BANKS + 1))
                        final = part is PL and h % per_bank == per_bank - 1 and (j == 2 if h % 2 == 0 else j == 3)
                        block = of(h, j)
                        last = pe.matmul(pv[use % PV_BANKS][0:block.shape[1], T - w:T], block,
                                         part[:, n % P_RING, c:c + w], start=first, stop=final,
                                         skip_group_check=True)
                last.then_inc(s.pv.sem, 1)

            def copied(s, b, names):
                for k in range(WORK_BANKS):
                    there = [name for name in names if s.work.bank(name) == k]
                    if there:
                        s.work.wait_copied(pe, b, there[-1])

            def first_maxima(s, passes):
                for m in range(AHEAD):
                    max_scores(s, 0, f"max{m}", m, passes)
                turn_max(s, 0, "turn0", 1)
                s.work.wait_copied(pe, 0, "turn0")

            def attention(s, b, passes, of_maxima, high, low, per_bank, own, following, next_maxima):
                for n in range(STEPS):
                    if n < ST_TILES:
                        scores(s, b, n, passes)
                        m, is_next = max_of(n)
                        if not is_next:
                            max_scores(s, b, f"max{m}", m, of_maxima)
                        elif following is not None:
                            max_scores(s, b, f"next_max{m}", m, next_maxima(n))
                        g = n // GROUP_TILES + 1
                        if n % GROUP_TILES == GROUP_TILES - 3:
                            if g < GROUPS:
                                turn_max(s, b, f"turn{g}", g)
                            elif following is not None:
                                turn_max(s, b, "next_turn", GROUPS)
                    own(n)
                    if following is not None:
                        following(n)
                    if n >= LAG:
                        values(s, b, n - LAG, high, low, per_bank)
                if following is not None:
                    s.work.wait_copied(pe, b, "next_turn")

            def output(s, b, rows):
                s.work.wait_free(pe, b, "out")
                bank = work[s.work.bank("out")]
                for i in range(TILES):
                    pe.wait_ge(s.rows.sem, s.rows.at(b, s.rows.per - TILES + i + 1))
                    for k, (y, w) in enumerate(rows):
                        last = pe.matmul(bank[:, i * C:(i + 1) * C], y[:, i * P:(i + 1) * P], w,
                                         start=k == 0, stop=k == len(rows) - 1)
                last.then_inc(s.work.ready.sem, 1)

            pe.wait_ge(loaded_fold, 16 * 2)
            for h in range(HEADS):
                if h >= WORK_BANKS:
                    pe.wait_ge(fold_free, h + 1)
                r = slice(64 * (h % 2), 64 * (h % 2) + 64)
                pe.matmul(work[h % WORK_BANKS][:, 0:P], WqT[r, h // 2, :], WkT[r, h // 2, :],
                          start=True, stop=True).then_inc(folded, 1)

            pe.wait_ge(fold_free, HEADS + WORK_BANKS)
            pe.wait_ge(loaded_a, 16 * 3)
            pe.wait_ge(loaded_const, 16 * CONSTS)

            def query(s, b, h):
                product(s, b, f"q{h}", M[:, h, :], hT[:, :])

            def value(s, b, k):
                product(s, b, f"v{k}", latent[:, k // 2 * P:(k // 2 + 1) * P], Wv[:, k % 2 * 512:(k % 2 + 1) * 512])

            def latents(s, b):
                s.work.wait_copied(pe, b, "hT")
                product(s, b, "lat", Wd[:, :], hT[:, :])

            def operands_ready(s, b):
                copied(s, b, [f"q{h}" for h in range(HEADS)] + [f"v{k}" for k in range(2 * TILES)])
                pe.wait_ge(s.latents.sem, s.latents.at(b, 1))

            queries_h, queries_l = lambda h, c0, c1: QH[:, h, c0:c1], lambda h, c0, c1: QL[:, h, c0:c1]
            latents_h, latents_l = lambda h, c0, c1: latH[:, c0:c1], lambda h, c0, c1: latL[:, c0:c1]
            passes = [(queries_h, latents_h), (queries_l, latents_h), (queries_h, latents_l)]
            next_passes = [(queries_h, lambda h, c0, c1: latN[:, c0:c1])]
            rows = [(yT[:, k, :], Wo[:, k, :]) for k in range(HEADS // 2)]
            high, low = lambda h, j: VH[:, j, h, :], lambda h, j: VL[:, j, h, :]

            def first_attention(s, b, following, beside, late_before, late_after):
                def next_maxima(n):
                    if n + AHEAD == ST_TILES:
                        copied(s, b, [f"q{h}" for h in range(HEADS) if query_step(h) < n])
                    return next_passes

                attention(s, b, passes, passes, high, low, 1, beside, following, next_maxima)
                late_before()
                output(s, b, rows)
                late_after()

            turn_h(A0, 0)
            latents(A0, 0)
            for name in first_operands()[2:]:
                if name == "v0":
                    A0.work.wait_copied(pe, 0, "lat")
                (query if name[0] == "q" else value)(A0, 0, int(name[1:]))
            operands_ready(A0, 0)
            pe.wait_ge(loaded_tables, 16 * TABLES)
            pe.wait_ge(setup, 4)
            first_maxima(A0, passes)
            pe.wait_ge(ones_filled, 1)
            with pe.Fori(0, B - 1) as b:
                def following(n):
                    if n == TURN_STEP:
                        turn_h(A1, b)
                    if n == LATENT_STEP:
                        latents(A1, b)
                    for h in range(HEADS):
                        if query_step(h) == n:
                            query(A1, b, h)
                    for k in EARLY_VALUES:
                        if value_step(k) == n:
                            if k == 0:
                                A1.work.wait_copied(pe, b, "lat")
                            value(A1, b, k)

                def late_values(which):
                    for k in which:
                        value(A1, b, k)

                first_attention(A1, b, following, lambda n: None, lambda: late_values(LATE_BEFORE),
                                lambda: late_values(LATE_AFTER))
                operands_ready(A1, b)

            def small_values(s, b, wv):
                s.work.wait_free(pe, b, "v")
                for i in range(TILES):
                    last = pe.matmul(work[s.work.bank("v")][:, i * C:(i + 1) * C], hT[:, i * P:(i + 1) * P], wv,
                                     start=True, stop=True)
                last.then_inc(s.work.ready.sem, 1)

            def stacked(s, b, groups):
                for g in groups:
                    pe.wait_ge(s.stack[g].sem, s.stack[g].at(b, s.stack[g].per))

            def small_attention(phases, products, later, wv, wo, before, beside_last):
                first, loop, last = phases
                rows = [(yT[:, k, :], wo[:, k, :]) for k in range(2)]
                high = lambda h, j: VS[:, j * GROUPS + h // GROUP, h % GROUP * P:(h % GROUP + 1) * P]

                def small(s, b, following, beside):
                    def next_maxima(n):
                        if (n + AHEAD) % GROUP_TILES == 0:
                            stacked(s, b, [(n + AHEAD - ST_TILES) // GROUP_TILES])
                        return stacks

                    attention(s, b, shifted, stacks, high, None, GROUP, beside, following, next_maxima)
                    if following is not None:
                        small_values(s, b, wv)
                    output(s, b, rows)

                before()
                with pe.Fori(0, B - 1) as b:
                    def following(n):
                        if n == SMALL_TURN_STEP:
                            turn_h(loop, b)
                        for name, w in products:
                            if n == OPERAND_STEP + later[name]:
                                if name == "q":
                                    loop.work.wait_copied(pe, b, "hT")
                                product(loop, b, name, w, hT[:, :])

                    small(loop, b, following, lambda n: None)
                    stacked(loop, b, range(GROUPS))
                    loop.work.wait_copied(pe, b, "v")
                small(last, 0, None, beside_last)

            def logits(s, b):
                s.work.wait_copied(pe, b, "hT")
                s.work.wait_free(pe, b, "logits")
                for i in range(TILES):
                    last = pe.matmul(work[s.work.bank("logits")][:, i * EXPERTS:(i + 1) * EXPERTS],
                                     hT[:, i * P:(i + 1) * P], Wg[:, :], start=True, stop=True)
                last.then_inc(s.work.ready.sem, 1)

            def count(s, b):
                pe.wait_ge(s.masks.sem, s.masks.at(b, 1))
                s.work.wait_free(pe, b, "count")
                bank = work[s.work.bank("count")][:, 0:TILES * EXPERTS]
                pe.matmul(bank, trib[:, :], maskb16[:, :, :].rearrange("p i e -> p (i e)"), start=True, stop=False)
                pe.matmul(bank, onesb[:, :], before16[:, :, :].rearrange("p i e -> p (i e)"), start=False, stop=True
                          ).then_inc(s.work.ready.sem, 1)

            def routed(s, b):
                pe.wait_ge(s.inputs.sem, s.inputs.at(b, 1))

            def expert_out(s, b, e):
                for f in range(FT):
                    s.work.wait_copied(pe, b, f"h{e}.{f}")
                pe.wait_ge(s.added.sem, s.added.at(b, e - PV_BANKS + 1))
                for i in range(TILES):
                    for f in range(FT):
                        last = pe.matmul(pv[e % PV_BANKS][:, i * C:(i + 1) * C],
                                         hid2(e)[:, f, i * P:(i + 1) * P], W2[:, e * FT + f, :],
                                         start=f == 0, stop=f == FT - 1)
                last.then_inc(s.expert.sem, 1)

            def experts(s, b, following):
                for e in range(EXPERTS):
                    for f in range(FT):
                        name, columns = f"h{e}.{f}", slice(f * P, (f + 1) * P)
                        s.work.wait_free(pe, b, name)
                        bank, high, low = work[s.work.bank(name)], W1H[:, e, columns], w1_low_part(e)[:, columns]
                        pe.matmul(bank[:, :], high, hEH[:, :], start=True, stop=False)
                        pe.matmul(bank[:, :], low, hEH[:, :], start=False, stop=False)
                        pe.matmul(bank[:, :], high, hEL[:, :], start=False, stop=True).then_inc(s.work.ready.sem, 1)
                    if e == 0:
                        pe.wait_ge(s.gate.sem, s.gate.at(b, 0))
                        s.work.wait_free(pe, b, "gT")
                        for i in range(TILES):
                            last = pe.transpose(work[s.work.bank("gT")][0:EXPERTS, i * P:(i + 1) * P], ge[:, i, :],
                                                identf[:, :])
                        last.then_inc(s.work.ready.sem, 1)
                    if e == 1:
                        s.work.wait_copied(pe, b, "gT")
                        s.work.wait_free(pe, b, "b2")
                        for i in range(TILES):
                            last = pe.matmul(work[s.work.bank("b2")][:, i * C:(i + 1) * C], geT[:, i, :], b2s[:, :],
                                             start=True, stop=True)
                        last.then_inc(s.work.ready.sem, 1)
                    following(e)
                    if e >= 1:
                        expert_out(s, b, e - 1)
                expert_out(s, b, EXPERTS - 1)

            second_products = tuple(zip(ROTATED, (BWq, BWqr, BWk, BWkr)))
            stacks = [(lambda h, c0, c1: QS[0:STACK, h, c0:c1], lambda h, c0, c1: KS[0:STACK, h, c0:c1])]
            shifted = [(lambda h, c0, c1: QS[0:SHIFTED, h, c0:c1], lambda h, c0, c1: KS[0:SHIFTED, h, c0:c1])]

            def second_operands(n):
                if n == SECOND_TURN_STEP:
                    turn_h(B0, 0)
                for name, w in second_products:
                    if n == SECOND_OPERAND_STEP + ROTATED[name]:
                        if name == "q":
                            B0.work.wait_copied(pe, 0, "hT")
                        product(B0, 0, name, w, hT[:, :])

            def second_maxima():
                stacked(B0, 0, range(GROUPS))
                first_maxima(B0, stacks)
                small_values(B0, 0, BWv)

            pe.wait_ge(loaded_b, 16 * 5)
            first_attention(A2, 0, None, second_operands, second_maxima, lambda: None)
            pe.wait_ge(last_rows, 16 * (GROUPS + HEADS))
            B0.work.wait_copied(pe, 0, "v")

            def first_routing(n):
                if n == SMALL_TURN_STEP:
                    turn_h(M0, 0)
                if n == LOGITS_STEP:
                    logits(M0, 0)
                if n == COUNT_STEP:
                    count(M0, 0)

            pe.wait_ge(loaded_moe, 16 * 6)
            small_attention((B0, B1, B2), second_products, ROTATED, BWv, BWo, lambda: None, first_routing)
            routed(M0, 0)
            pe.wait_ge(w1_high, EXPERTS)

            with pe.Fori(0, B - 1) as b:
                def routing(e):
                    if e == 2:
                        turn_h(M1, b)
                    if e == 3:
                        logits(M1, b)
                    if e == 6:
                        count(M1, b)

                experts(M1, b, routing)
                routed(M1, b)

            third_products = (("q", CWq), ("k", CWk))

            def before_third():
                def following(e):
                    if e == 2:
                        turn_h(C0, 0)
                    if e == 3:
                        C0.work.wait_copied(pe, 0, "hT")
                    for k, (name, w) in enumerate(third_products):
                        if e == 3 + k:
                            product(C0, 0, name, w, hT[:, :])

                experts(M2, 0, following)
                stacked(C0, 0, range(GROUPS))
                first_maxima(C0, stacks)
                small_values(C0, 0, CWv)
                C0.work.wait_copied(pe, 0, "v")

            def first_ffn(n):
                if n == SMALL_TURN_STEP:
                    turn_h(F0, 0)

            small_attention((C0, C1, C2), third_products, PLAIN, CWv, CWo, before_third, first_ffn)
            C2.work.wait_copied(pe, 0, "hT")

            pe.wait_ge(ffn_weights, 1)

            def ffn(s, b, is_next):
                for f in range(HT):
                    product(s, b, f"g{f}", Wf[:, f * P:(f + 1) * P], hT[:, :])
                    product(s, b, f"u{f}", Wf[:, HID + f * P:HID + (f + 1) * P], hT[:, :])
                if is_next:
                    turn_h(s, b)
                for f in range(HT):
                    s.work.wait_copied(pe, b, f"u{f}")
                s.work.wait_free(pe, b, "out")
                for i in range(TILES):
                    for f in range(HT):
                        last = pe.matmul(work[s.work.bank("out")][:, i * C:(i + 1) * C],
                                         hidF[:, f, i * P:(i + 1) * P],
                                         Wf[:, 2 * HID + f * C:2 * HID + (f + 1) * C], start=f == 0, stop=f == HT - 1)
                last.then_inc(s.work.ready.sem, 1)
                if is_next:
                    s.work.wait_copied(pe, b, "hT")

            with pe.Fori(0, B - 1) as b:
                ffn(F1, b, True)
            ffn(F2, 0, False)

        @block.scalar
        def _(act):
            def free(s, name):
                return s.work.free[s.work.bank(name)].sem

            def bank(s, name):
                return work[s.work.bank(name)]

            def exponential(s, b, n, scale):
                act.wait_ge(s.scores.sem, s.scores.at(b, n + 1))
                act.wait_ge(s.low.sem, s.low.at(b, n - FULL_RING + 1))
                act.wait_ge(s.pv.sem, s.pv.at(b, n - P_RING + 1))
                nc.scalar.activation(full[:, n % FULL_RING, :], st[n % ST_BANKS][:, :], ACT.Exp, scale=scale)
                nc.scalar.activation(PH[:, n % P_RING, :], st[n % ST_BANKS][:, :], ACT.Exp, scale=scale
                                     ).then_inc(s.probs.sem, 1)

            def copy(s, b, name, dst, src=None):
                s.work.wait_ready(act, b, name)
                nc.scalar.activation(dst, bank(s, name)[:, :] if src is None else src, ACT.Copy
                                     ).then_inc(free(s, name), 1)

            def take_out(s, b, use, per_bank):
                half = slice(HD_A * (use % 2), HD_A * (use % 2 + 1))
                act.wait_ge(s.pv.sem, s.pv.at(b, last_tile(use, per_bank) + 1))
                act.wait_ge(s.rows.sem, s.rows.at(b, TILES * (use // 2 - 1)))
                nc.scalar.activation(sums[half, use // 2 % 2, :], pv[use % PV_BANKS][HD_A:2 * HD_A, :], ACT.Copy
                                     ).then_inc(s.summed.sem, 1)
                nc.scalar.activation(yT[half, use // 2, :], pv[use % PV_BANKS][0:HD_A, :], ACT.Copy
                                     ).then_inc(s.y.sem, 1)

            def attention(s, b, scale, per_bank, more):
                for n in range(STEPS + 1):
                    if n < ST_TILES:
                        exponential(s, b, n, scale)
                    use = finished(n - LAG - 1, per_bank)
                    if use is not None:
                        take_out(s, b, use, per_bank)
                    more(n)

            for h in range(HEADS):
                act.wait_ge(folded, h + 1)
                nc.scalar.activation(M[:, h, :], work[h % WORK_BANKS][:, 0:P], ACT.Copy).then_inc(fold_free, 1)

            def high_part(s, b, name, dst, src):
                s.work.wait_ready(act, b, name)
                nc.scalar.activation(dst, src, ACT.Copy).then_inc(s.high.sem, 1)

            def query(s, b, h):
                high_part(s, b, f"q{h}", QH[:, h, :], bank(s, f"q{h}")[:, :])

            def value(s, b, k):
                high_part(s, b, f"v{k}", first_values(k)[0],
                          bank(s, f"v{k}")[:, :].rearrange("p (h c) -> p h c", c=HD_A))

            def latent_high(s, b):
                s.work.wait_copied(act, b, "lat")
                nc.scalar.activation(latH[:, :], latent[:, :], ACT.Copy).then_inc(s.high.sem, 1)

            copy(A0, 0, "hT", hT[:, :])
            for name in first_operands()[2:]:
                (query if name[0] == "q" else value)(A0, 0, int(name[1:]))
            latent_high(A0, 0)
            with act.Fori(0, B - 1) as b:
                def more(n):
                    if n == TURN_STEP:
                        copy(A1, b, "hT", hT[:, :])
                    for h in range(HEADS):
                        if query_step(h) == n:
                            query(A1, b, h)
                    for k in EARLY_VALUES:
                        if value_step(k) == n:
                            value(A1, b, k)

                attention(A1, b, HD_A ** -0.5, 1, more)
                for k in LATE_BEFORE:
                    value(A1, b, k)
                latent_high(A1, b)
                for k in LATE_AFTER:
                    value(A1, b, k)

            def small_values(s, b):
                s.work.wait_ready(act, b, "v")
                src = bank(s, "v")[:, :].rearrange("p (g h d) -> p g h d", h=GROUP, d=HD_S)
                nc.scalar.activation(stripes(0), src, ACT.Copy).then_inc(s.stripes.sem, 1)

            def small_hT(s, b, rope):
                if rope:
                    s.work.wait_ready(act, b, "hT")
                    nc.scalar.activation(hT[:, :], bank(s, "hT")[:, :], ACT.Identity, bias=ln[:, 1:2],
                                         scale=ln[:, 0:1]).then_inc(free(s, "hT"), 1)
                else:
                    copy(s, b, "hT", hT[:, :])

            def small(phases, rope, beside):
                _, loop, last = phases
                with act.Fori(0, B - 1) as b:
                    def more(n):
                        if n == SMALL_TURN_STEP:
                            small_hT(loop, b, rope)

                    attention(loop, b, HD_S ** -0.5, GROUP, more)
                    small_values(loop, b)
                attention(last, 0, HD_S ** -0.5, GROUP, beside)

            def routing_hT(s, b):
                s.work.wait_ready(act, b, "hT")
                nc.scalar.activation(hT[:, :], bank(s, "hT")[:, :], ACT.Identity, bias=ln[:, 3:4],
                                     scale=ln[:, 2:3]).then_inc(free(s, "hT"), 1)

            def routing_exp(s, b):
                s.work.wait_copied(act, b, "logits")
                nc.scalar.activation(gates[:, :, :], lg[:, :, :], ACT.Exp).then_inc(s.exp.sem, 1)

            def take(s, b):
                s.work.wait_copied(act, b, "hT")
                nc.scalar.activation(hEH[:, :], hT[:, :], ACT.Copy).then_inc(s.taken.sem, 1)

            def experts(s, b, following):
                for e in range(EXPERTS):
                    for f in range(FT):
                        s.work.wait_ready(act, b, f"h{e}.{f}")
                        nc.scalar.activation(hid2(e)[:, f, :], bank(s, f"h{e}.{f}")[:, :], ACT.Gelu,
                                             bias=b1s[:, e, f:f + 1]).then_inc(free(s, f"h{e}.{f}"), 1)
                    following(e)

            def first_routing(n):
                if n == SMALL_TURN_STEP:
                    routing_hT(M0, 0)
                if n == EXP_STEP:
                    routing_exp(M0, 0)
                e = n - WEIGHT_STEP
                if 0 <= e < EXPERTS:
                    nc.scalar.activation(w1_low_part(e), W1[:, e, :], ACT.Copy).then_inc(w1_rounded, 1)
                if 0 <= e - 2 < EXPERTS:
                    act.wait_ge(w1_low, e - 1)
                    nc.scalar.activation(W1H[:, e - 2, :], W1[:, e - 2, :], ACT.Copy).then_inc(w1_high, 1)
                if n == STEPS:
                    take(M0, 0)

            def before_second(n):
                if n == SECOND_TURN_STEP:
                    small_hT(B0, 0, True)

            act.wait_ge(loaded_b, 16 * 5)
            attention(A2, 0, HD_A ** -0.5, 1, before_second)
            act.wait_ge(loaded_moe, 16 * 6)
            act.wait_ge(zeroed, 1 + 2 * TILES)
            small_values(B0, 0)
            small((B0, B1, B2), True, first_routing)

            with act.Fori(0, B - 1) as b:
                def routing(e):
                    if e == 2:
                        routing_hT(M1, b)
                    if e == 4:
                        routing_exp(M1, b)

                experts(M1, b, routing)
                take(M1, b)

            def before_third(e):
                if e == 2:
                    small_hT(C0, 0, False)

            experts(M2, 0, before_third)
            small_values(C0, 0)

            def first_ffn(n):
                if n == SMALL_TURN_STEP:
                    copy(F0, 0, "hT", hT[:, :])

            small((C0, C1, C2), False, first_ffn)

            def ffn(s, b, is_next):
                for f in range(HT):
                    s.work.wait_ready(act, b, f"g{f}")
                    nc.scalar.activation(siluF[:, f, :], bank(s, f"g{f}")[:, :], ACT.Silu
                                         ).then_inc(free(s, f"g{f}"), 1)
                if is_next:
                    copy(s, b, "hT", hT[:, :])

            with act.Fori(0, B - 1) as b:
                ffn(F1, b, True)
            ffn(F2, 0, False)

        @block.vector
        def _(dve):
            v = nc.vector

            class Steps:

                def __init__(self, s, b):
                    self.s, self.b, self.n = s, b, 0

                def __call__(self, ins):
                    self.n += 1
                    ins.then_inc(self.s.step.sem, 1)
                    dve.wait_ge(self.s.step.sem, self.s.step.at(self.b, self.n))

                def end(self):
                    assert self.n == self.s.step.per, (self.s.step.sem, self.n)

            def free(s, name):
                return s.work.free[s.work.bank(name)].sem

            def bank(s, name):
                return work[s.work.bank(name)]

            def spread_of(s, b, step, src):
                for i in range(TILES):
                    last = v.bn_stats(stats[:, i, :], src[:, i, :])
                step(last)
                even, odd = stats[:, :, 0:3], stats[:, :, 3:6]
                v.tensor_tensor(mean[:, :, 0], even[:, :, 1], odd[:, :, 1], ALU.add)
                v.tensor_tensor(mean[:, :, 1], even[:, :, 1], odd[:, :, 1], ALU.subtract)
                step(v.tensor_tensor(mean[:, :, 2], even[:, :, 2], odd[:, :, 2], ALU.add))
                v.tensor_scalar(mv[:, :, 0], mean[:, :, 0], 0.5, None, ALU.mult)
                v.tensor_scalar(mv[:, :, 1], mean[:, :, 2], 1.0 / C, EPS, ALU.mult, ALU.add)
                step(v.scalar_tensor_tensor(mean[:, :, 3], mean[:, :, 1], 0.25, mean[:, :, 1], ALU.mult, ALU.mult))
                v.tensor_tensor(veps[:, :], mv[:, :, 1], mean[:, :, 3], ALU.add).then_inc(s.var.sem, 1)

            def normalised(s, b, k, src, dst):
                dve.wait_ge(s.rstd.sem, s.rstd.at(b, k + 1))
                for i in range(TILES):
                    last = v.tensor_scalar(dst[:, i, :], src[:, i, :], mv[:, i, 0:1], rstd[:, i:i + 1],
                                           ALU.subtract, ALU.mult)
                return last

            def layernorm(s, b, step, k, src, dst):
                spread_of(s, b, step, src)
                return normalised(s, b, k, src, dst)

            def norm_at(s, b, step, n, first, src):
                if n == first:
                    spread_of(s, b, step, src)
                if n == first + NORM_WAIT:
                    normalised(s, b, 0, src, H).then_inc(s.normed.sem, 1)

            def row_maxima(s, b, name, m):
                s.work.wait_ready(dve, b, name)
                src, g = bank(s, name), m // GROUP_TILES
                blocks = max_tile(m)
                if len(blocks) == 2 and blocks[0][3] == blocks[1][3]:
                    h, i, _, w = blocks[0]
                    last = v.tensor_reduce(MX[:, g % 2, i, h % GROUP:h % GROUP + 2],
                                           src[:, :].rearrange("p (h k) -> p h k", h=2), AX_X, ALU.max, negate=True)
                else:
                    for h, i, c, w in blocks:
                        last = v.tensor_reduce(MX[:, g % 2, i, h % GROUP:h % GROUP + 1], src[:, c:c + w], AX_X,
                                               ALU.max, negate=True)
                last.then_inc(free(s, name), 1)

            def split_maxima(s, b, step, g, prefix):
                for m in range(GROUP_TILES * (g + 1) - 3, GROUP_TILES * (g + 1)):
                    s.work.wait_copied(dve, b, f"{prefix}{m}")
                mx = MX[:, g % 2]
                at = [SHIFT_ROW + GROUP * k if s.high is None else 32 * k for k in range(PIECES)]
                p1, p2, p3 = [MS[:, :, c:c + GROUP] for c in at]
                step(v.tensor_copy(p1, mx))
                step(v.tensor_tensor(MR[:, :, :], mx, p1, ALU.subtract))
                step(v.tensor_copy(p2, MR[:, :, :]))
                v.tensor_tensor(p3, MR[:, :, :], p2, ALU.subtract).then_inc(s.pieces.sem, 1)

            def turned(s, b, name, g):
                s.work.wait_ready(dve, b, name)
                src = bank(s, name)[:, :].bitcast(BF16)
                if s.high is None:
                    rows = src[SHIFT_ROW:SHIFTED, 0:T].rearrange("p (o t) -> p o t", o=1)
                    last = v.tensor_copy(QS[SHIFT_ROW:SHIFTED, GROUP * g:GROUP * g + GROUP, :],
                                         rows.to_broadcast([SHIFTED - SHIFT_ROW, GROUP, T]))
                else:
                    last = v.tensor_copy(MT[:, g % 2, :], src[:, 0:T])
                last.then_inc(free(s, name), 1)

            def divide(s, b, p, k):
                if k == 0:
                    dve.wait_ge(s.summed.sem, s.summed.at(b, 2 * p + 2))
                if k == 1:
                    dve.wait_ge(s.y.sem, s.y.at(b, 2 * p + 2))
                if k > 0:
                    dve.wait_ge(s.inverse.sem, s.inverse.at(b, TILES * p + k))
                    tokens = slice((k - 1) * P, k * P)
                    v.tensor_tensor(yT[:, p, tokens], yT[:, p, tokens], sums[:, p % 2, tokens], ALU.mult
                                    ).then_inc(s.rows.sem, 1)
                if k < TILES:
                    tokens = slice(k * P, (k + 1) * P)
                    v.reciprocal(sums[:, p % 2, tokens], sums[:, p % 2, tokens]).then_inc(s.inverse.sem, 1)

            def first_maxima(s, step):
                for m in range(AHEAD):
                    row_maxima(s, 0, f"max{m}", m)
                split_maxima(s, 0, step, 0, "max")
                turned(s, 0, "turn0", 0)

            def attention(s, b, step, per_bank, own, following):
                divisions = division_steps(per_bank)
                for n in range(STEPS + 1):
                    if n < ST_TILES:
                        m, is_next = max_of(n)
                        if not is_next:
                            row_maxima(s, b, f"max{m}", m)
                        elif following is not None:
                            row_maxima(s, b, f"next_max{m}", m)
                        g = n // GROUP_TILES + 1
                        if g < GROUPS and n % GROUP_TILES == GROUP_TILES - 5:
                            split_maxima(s, b, step, g, "max")
                        if g < GROUPS and n % GROUP_TILES == GROUP_TILES - 3:
                            turned(s, b, f"turn{g}", g)
                        if following is not None and n == ST_TILES - 5:
                            split_maxima(s, b, step, 0, "next_max")
                        if following is not None and n == ST_TILES - 3:
                            turned(s, b, "next_turn", 0)
                    own(n)
                    if following is not None:
                        following(n)
                    for p, k in divisions.get(n, []):
                        divide(s, b, p, k)

            def batch(a, b):
                return a[:, bass.ds(b * TILES, TILES), :]

            def tokens(s, name):
                return bank(s, name)[:, :].rearrange("p (i c) -> p i c", c=C)

            dve.wait_ge(loaded_x, 16)
            dve.wait_ge(setup, 4)

            class Lows:

                def __init__(self, s, b):
                    self.s, self.b, self.n = s, b, 0

                def wait(self):
                    self.n += 1
                    dve.wait_ge(self.s.high.sem, self.s.high.at(self.b, self.n))

            def latent_copy(s, b):
                s.work.wait_ready(dve, b, "lat")
                v.tensor_copy(latN[:, :], bank(s, "lat")[:, :])
                v.tensor_copy(latent[:, :], bank(s, "lat")[:, :]).then_inc(free(s, "lat"), 1)

            def query_low(s, b, lows, h):
                lows.wait()
                v.tensor_tensor(QL[:, h, :], bank(s, f"q{h}")[:, :], QH[:, h, :].bitcast(F32), ALU.subtract
                                ).then_inc(free(s, f"q{h}"), 1)

            def value_low(s, b, lows, k):
                high, low = first_values(k)
                lows.wait()
                v.tensor_tensor(low, bank(s, f"v{k}")[:, :].rearrange("p (h c) -> p h c", c=HD_A),
                                high.bitcast(F32), ALU.subtract).then_inc(free(s, f"v{k}"), 1)

            def latent_low(s, b, lows):
                lows.wait()
                v.tensor_tensor(latL[:, :], latent[:, :], latH[:, :].bitcast(F32), ALU.subtract
                                ).then_inc(s.latents.sem, 1)

            step, lows = Steps(A0, 0), Lows(A0, 0)
            layernorm(A0, 0, step, 0, X[:, 0:TILES, :], H).then_inc(A0.normed.sem, 1)
            latent_copy(A0, 0)
            for name in first_operands()[2:]:
                (query_low if name[0] == "q" else value_low)(A0, 0, lows, int(name[1:]))
            latent_low(A0, 0, lows)
            first_maxima(A0, step)
            dve.wait_ge(loaded_rest, 16)
            step.end()

            with dve.Fori(0, B - 1) as b:
                s, step, lows = A1, Steps(A1, b), Lows(A1, b)

                def following(n):
                    norm_at(s, b, step, n, NORM_STEP, batch(X, b + 1))
                    if n == LATENT_STEP:
                        latent_copy(s, b)
                    for h in range(HEADS):
                        if query_step(h) == n:
                            query_low(s, b, lows, h)
                    for k in EARLY_VALUES:
                        if value_step(k) == n:
                            value_low(s, b, lows, k)

                attention(s, b, step, 1, lambda n: None, following)
                for k in LATE_BEFORE:
                    value_low(s, b, lows, k)
                latent_low(s, b, lows)
                s.work.wait_ready(dve, b, "out")
                v.tensor_tensor(batch(X, b), batch(X, b), tokens(s, "out"), ALU.add).then_inc(free(s, "out"), 1)
                for k in LATE_AFTER:
                    value_low(s, b, lows, k)
                step.end()
            def first_piece(step, w):
                step(v.tensor_copy(piece[:, w, 0, :], qk))

            def other_pieces(s, b, step, w):
                step(v.tensor_tensor(rot[:, 0, :], qk, piece[:, w, 0, :], ALU.subtract))
                step(v.tensor_copy(piece[:, w, 1, :], rot[:, 0, :]))
                v.tensor_tensor(piece[:, w, 2, :], rot[:, 0, :], piece[:, w, 1, :], ALU.subtract
                                ).then_inc(s.split.sem, 1)
                dve.wait_ge(s.split.sem, s.split.at(b, w + 1))

            def pieces_out(s, b, w):
                if w == 0 and s.spilt.start > 0:
                    dve.wait_ge(s.spilt.sem, s.spilt.at(b, 0))

            def stripes_low(s, b):
                dve.wait_ge(s.stripes.sem, s.stripes.at(b, 1))
                src = bank(s, "v")[:, :].rearrange("p (g h d) -> p g h d", h=GROUP, d=HD_S)
                v.tensor_tensor(stripes(1), src, stripes(0).bitcast(F32), ALU.subtract).then_inc(free(s, "v"), 1)

            def second_norms(s, b, step, n, first, xb):
                if n == first:
                    spread_of(s, b, step, xb)
                if n == first + NORM_WAIT:
                    step(normalised(s, b, 0, xb, Ub))
                    spread_of(s, b, step, Ub)
                if n == first + 2 * NORM_WAIT:
                    normalised(s, b, 1, Ub, H).then_inc(s.normed.sem, 1)

            def operand(s, b, step, w, k):
                name, turn = (("q", "qr"), ("k", "kr"))[w]
                if k == 1:
                    s.work.wait_copied(dve, b, name)
                    s.work.wait_copied(dve, b, turn)
                    step(v.tensor_tensor(qk, rot[:, 0, :], rot[:, 1, :], ALU.add))
                    first_piece(step, w)
                if k == 2:
                    other_pieces(s, b, step, w)
                if k > 0:
                    return
                pieces_out(s, b, w)
                s.work.wait_ready(dve, b, name)
                v.tensor_tensor(rot[:, 0, :], bank(s, name)[:, :], cos[:, :], ALU.mult).then_inc(free(s, name), 1)
                s.work.wait_ready(dve, b, turn)
                v.tensor_tensor(rot[:, 1, :], bank(s, turn)[:, :], sin[:, :], ALU.mult).then_inc(free(s, turn), 1)

            step, b_step = Steps(A2, 0), Steps(B0, 0)

            def before_second(n):
                second_norms(B0, 0, b_step, n, SECOND_NORM_STEP, X[:, 0:TILES, :])
                if n == SECOND_OPERAND_STEP:
                    dve.wait_ge(loaded_rot, 32)
                for w in range(2):
                    for k in range(3):
                        if n == SECOND_OPERAND_STEP + 4 * w + 1 + k:
                            operand(B0, 0, b_step, w, k)

            attention(A2, 0, step, 1, before_second, None)
            first_maxima(B0, b_step)
            A2.work.wait_ready(dve, 0, "out")
            v.tensor_tensor(batch(X, B - 1), batch(X, B - 1), tokens(A2, "out"), ALU.add
                            ).then_inc(free(A2, "out"), 1)
            v.tensor_scalar(U[:, 0:TILES, :], Ub[:, :, :], 1.0, None, ALU.mult)
            A2.work.wait_copied(dve, 0, "out")
            dve.wait_ge(zeroed, 1 + 2 * TILES)
            stripes_low(B0, 0)
            step.end()
            b_step.end()
            with dve.Fori(0, B - 1) as b:
                s, step = B1, Steps(B1, b)

                def following(n):
                    second_norms(s, b, step, n, NORM_STEP, batch(X, b + 1))
                    if n == SMALL_TURN_STEP:
                        v.tensor_scalar(batch(U, b + 1), Ub[:, :, :], 1.0, None, ALU.mult)
                    for w in range(2):
                        for k in range(3):
                            if n == OPERAND_STEP + 4 * w + 1 + k:
                                operand(s, b, step, w, k)

                attention(s, b, step, GROUP, lambda n: None, following)
                stripes_low(s, b)
                s.work.wait_ready(dve, b, "out")
                v.tensor_tensor(batch(U, b), batch(U, b), tokens(s, "out"), ALU.add).then_inc(free(s, "out"), 1)
                step.end()

            def spread(row):
                return row.rearrange("p (i o) -> p i o", o=1).to_broadcast([P, TILES, EXPERTS])

            def less_peaks(s, b, step):
                s.work.wait_ready(dve, b, "logits")
                logits = bank(s, "logits")[:, 0:TILES * EXPERTS].rearrange("p (i e) -> p i e", e=EXPERTS)
                step(v.tensor_reduce(lmax[:, :], logits, AX_X, ALU.max))
                v.tensor_tensor(lg[:, :, :], logits, spread(lmax[:, :]), ALU.subtract
                                ).then_inc(free(s, "logits"), 1)

            def first_peak(step, src, dst):
                step(v.tensor_reduce(lmax[:, :], src, AX_X, ALU.max))
                step(v.tensor_tensor(rank[:, :, :], src, spread(lmax[:, :]), ALU.is_equal))
                step(v.tensor_tensor(rank[:, :, :], rank[:, :, :], order[:, :, :], ALU.mult))
                step(v.tensor_reduce(lmax[:, :], rank[:, :, :], AX_X, ALU.max))
                step(v.tensor_tensor(dst, rank[:, :, :], spread(lmax[:, :]), ALU.is_equal))

            def first_choice(s, b, step):
                dve.wait_ge(s.exp.sem, s.exp.at(b, 1))
                step(v.tensor_reduce(lsum[:, :], gates[:, :, :], AX_X, ALU.add))
                step(v.reciprocal(lsum[:, :], lsum[:, :]))
                step(v.tensor_tensor(gates[:, :, :], gates[:, :, :], spread(lsum[:, :]), ALU.mult))
                first_peak(step, gates[:, :, :], maskf[:, :, :])

            def second_choice(s, b, step):
                step(v.scalar_tensor_tensor(gsel[:, :, :], maskf[:, :, :], -2.0, gates[:, :, :], ALU.mult, ALU.add))
                first_peak(step, gsel[:, :, :], keep[:, :, :])
                step(v.tensor_tensor(maskf[:, :, :], maskf[:, :, :], keep[:, :, :], ALU.add))
                for i in range(TILES):
                    step(v.tensor_tensor(before[:, i + 1, :], before[:, i, :], maskf[:, i, :], ALU.add))
                v.tensor_copy(maskb16[:, :, :], maskf[:, :, :])
                step(v.tensor_copy(before16[:, :, :], before[:, 0:TILES, :]))
                v.tensor_copy(before[:, 0, :], before[:, TILES, :]).then_inc(s.masks.sem, 1)

            def kept_gates(s, b, step):
                s.work.wait_ready(dve, b, "count")
                count = bank(s, "count")[:, 0:TILES * EXPERTS].rearrange("p (i e) -> p i e", e=EXPERTS)
                v.tensor_scalar(keep[:, :, :], count, float(CAP), None, ALU.is_le).then_inc(free(s, "count"), 1)
                s.work.wait_copied(dve, b, "count")
                step(v.tensor_tensor(keep[:, :, :], keep[:, :, :], maskf[:, :, :], ALU.mult))
                step(v.tensor_tensor(next_ge[:, :, :], keep[:, :, :], gates[:, :, :], ALU.mult))

            def take(s, b):
                v.tensor_copy(ge[:, :, :], next_ge[:, :, :]).then_inc(s.gate.sem, 1)
                dve.wait_ge(s.gate.sem, s.gate.at(b, 1))

            def add_expert(s, b, e):
                dve.wait_ge(s.expert.sem, s.expert.at(b, e + 1))
                for i in range(TILES):
                    last = v.scalar_tensor_tensor(acc[:, i, :], pv[e % PV_BANKS][:, i * C:(i + 1) * C],
                                                  ge[:, i, e:e + 1], acc[:, i, :], ALU.mult, ALU.add)
                last.then_inc(s.added.sem, 1)
                dve.wait_ge(s.added.sem, s.added.at(b, e + 1))

            def experts(s, b, tokens_of, following):
                for e in range(EXPERTS):
                    if e == 0:
                        s.work.wait_ready(dve, b, "gT")
                        v.tensor_copy(sums[0:EXPERTS, 0, :], bank(s, "gT")[0:EXPERTS, :]
                                      ).then_inc(free(s, "gT"), 1)
                    if e == 1:
                        s.work.wait_ready(dve, b, "b2")
                        v.tensor_tensor(acc[:, :, :], tokens_of(U), tokens(s, "b2"), ALU.add
                                        ).then_inc(free(s, "b2"), 1)
                        s.work.wait_copied(dve, b, "b2")
                    following(e)
                    if e >= 1:
                        add_expert(s, b, e - 1)
                add_expert(s, b, EXPERTS - 1)
                v.tensor_tensor(tokens_of(X), tokens_of(X), acc[:, :, :], ALU.add).then_inc(s.done.sem, 1)

            step, m_step = Steps(B2, 0), Steps(M0, 0)

            def first_routing(n):
                norm_at(M0, 0, m_step, n, NORM_STEP, U[:, 0:TILES, :])
                if n == PEAK_STEP:
                    less_peaks(M0, 0, m_step)
                if n == FIRST_CHOICE_STEP:
                    first_choice(M0, 0, m_step)
                if n == SECOND_CHOICE_STEP:
                    second_choice(M0, 0, m_step)
                if n == KEEP_STEP:
                    kept_gates(M0, 0, m_step)
                e = n - WEIGHT_STEP
                if 0 <= e < EXPERTS:
                    dve.wait_ge(w1_rounded, e + 1)
                    v.tensor_tensor(w1_low_part(e), W1[:, e, :], w1_low_part(e).bitcast(F32), ALU.subtract
                                    ).then_inc(w1_low, 1)

            attention(B2, 0, step, GROUP, first_routing, None)
            B2.work.wait_ready(dve, 0, "out")
            v.tensor_tensor(batch(U, B - 1), batch(U, B - 1), tokens(B2, "out"), ALU.add
                            ).then_inc(free(B2, "out"), 1)
            B2.work.wait_copied(dve, 0, "out")
            take(M0, 0)
            step.end()
            m_step.end()

            with dve.Fori(0, B - 1) as b:
                s, step = M1, Steps(M1, b)

                def routing(e):
                    if e == 0:
                        layernorm(s, b, step, 0, batch(U, b + 1), H).then_inc(s.normed.sem, 1)
                    if e == 4:
                        less_peaks(s, b, step)
                    if e == 5:
                        first_choice(s, b, step)
                        second_choice(s, b, step)
                    if e == 7:
                        kept_gates(s, b, step)

                experts(s, b, lambda a: batch(a, b), routing)
                take(s, b)
                step.end()

            def plain(s, b, step, w, k):
                name = "qk"[w]
                if k == 0:
                    pieces_out(s, b, w)
                    s.work.wait_ready(dve, b, name)
                    v.tensor_copy(qk, bank(s, name)[:, :]).then_inc(free(s, name), 1)
                    s.work.wait_copied(dve, b, name)
                    first_piece(step, w)
                else:
                    other_pieces(s, b, step, w)

            step = Steps(C0, 0)

            def before_third(e):
                if e == 0:
                    layernorm(C0, 0, step, 0, X[:, 0:TILES, :], H).then_inc(C0.normed.sem, 1)
                for w in range(2):
                    if e == 4 + w:
                        plain(C0, 0, step, w, 0)
                        plain(C0, 0, step, w, 1)

            experts(M2, 0, lambda a: batch(a, B - 1), before_third)
            dve.wait_ge(M2.done.sem, M2.done.at(0, 1))
            first_maxima(C0, step)
            stripes_low(C0, 0)
            step.end()
            with dve.Fori(0, B - 1) as b:
                s, step = C1, Steps(C1, b)

                def following(n):
                    norm_at(s, b, step, n, NORM_STEP, batch(X, b + 1))
                    for w in range(2):
                        for k in range(2):
                            if n == OPERAND_STEP + 4 * w + k:
                                plain(s, b, step, w, k)

                attention(s, b, step, GROUP, lambda n: None, following)
                stripes_low(s, b)
                s.work.wait_ready(dve, b, "out")
                step(v.tensor_tensor(batch(X, b), batch(X, b), bos, ALU.add))
                v.tensor_tensor(batch(X, b), batch(X, b), tokens(s, "out"), ALU.add).then_inc(free(s, "out"), 1)
                step.end()
            step, f_step = Steps(C2, 0), Steps(F0, 0)

            def first_ffn(n):
                norm_at(F0, 0, f_step, n, NORM_STEP, X[:, 0:TILES, :])
                if n == OPERAND_STEP:
                    dve.wait_ge(loaded_f, 16 * 3)
                    v.tensor_scalar(Wf[:, :], WfI[:, :], float(np.float32(1.0 / 127.0)), None, ALU.mult
                                    ).then_inc(ffn_weights, 1)

            attention(C2, 0, step, GROUP, first_ffn, None)
            C2.work.wait_ready(dve, 0, "out")
            step(v.tensor_tensor(batch(X, B - 1), batch(X, B - 1), bos, ALU.add))
            v.tensor_tensor(batch(X, B - 1), batch(X, B - 1), tokens(C2, "out"), ALU.add
                            ).then_inc(free(C2, "out"), 1)
            C2.work.wait_copied(dve, 0, "out")
            step.end()
            f_step.end()

            def ffn(s, b, xb):
                for f in range(HT):
                    s.work.wait_copied(dve, b, f"g{f}")
                    s.work.wait_ready(dve, b, f"u{f}")
                    v.tensor_tensor(hidF[:, f, :], bank(s, f"u{f}")[:, :], siluF[:, f, :], ALU.mult
                                    ).then_inc(free(s, f"u{f}"), 1)
                s.work.wait_ready(dve, b, "out")
                v.tensor_tensor(xb, xb, tokens(s, "out"), ALU.add).then_inc(free(s, "out"), 1)

            with dve.Fori(0, B - 1) as b:
                s, step = F1, Steps(F1, b)
                layernorm(s, b, step, 0, batch(X, b + 1), H).then_inc(s.normed.sem, 1)
                ffn(s, b, batch(X, b))
                step.end()
            ffn(F2, 0, batch(X, B - 1))


def constants():
    r = np.arange(P)
    ident = np.eye(P, dtype=np.float32)
    mask = np.where(r[None, :] > r[:, None], np.float32(-1e30), np.float32(0))
    sel = np.zeros((P, GROUP, P), np.float32)
    for k in range(PIECES):
        for j in range(GROUP):
            sel[32 * k + j, j, :] = 1
    ksel = np.zeros((SHIFTED - STACK, GROUP, HALF), np.float32)
    for k in range(PIECES):
        for j in range(GROUP):
            ksel[SHIFT_ROW - STACK + GROUP * k + j, j, :] = 1
    inv_freq = np.float32(1.0) / np.float32(10000.0) ** (np.arange(0, HD_S, 2, dtype=np.float32) / np.float32(HD_S))
    ang = np.arange(T, dtype=np.float32)[None, :] * inv_freq.astype(np.float32)[:, None]
    cos = np.tile(np.cos(ang).astype(np.float32), (C // len(inv_freq), 1))
    sin = np.tile(np.sin(ang).astype(np.float32), (C // len(inv_freq), 1))
    tri = (r[:, None] <= r[None, :]).astype(np.float32)
    order = np.broadcast_to(EXPERTS - np.arange(EXPERTS, dtype=np.float32), (P, TILES, EXPERTS))
    return dict(ident=ident, mask=mask, maskT=mask.T, cos=cos, sin=sin, sel=sel, ksel=ksel, tri=tri, order=order.astype(np.float32))


def kernel(**inputs):
    import concourse.bacc as _bacc
    from concourse import mybir as _mybir
    from concourse.bass_utils import run_bass_kernel_spmd as _run

    a = {k: np.asarray(v) for k, v in inputs.items()}
    up = a["L0_attn_w_kv_up"]
    hd = HEADS * HD_A
    qkv = a["L0_ffn_Wqkv"].reshape(C, HEADS, 3 * HD_S)
    bq, bk, bv = [qkv[:, :, k * HD_S:(k + 1) * HD_S] for k in range(3)]

    def turned(w):
        return np.concatenate([w[:, :, HD_S // 2:], w[:, :, :HD_S // 2]], axis=2)

    def twice(w):
        w = w.reshape(GROUPS, 1, C // GROUPS, C)
        return np.concatenate([w, w], axis=1).reshape(2 * C, C)

    data = {
        "x": a["L0_attn_x"].reshape(B * T, C),
        "w_down": a["L0_attn_w_kv_down"], "w_upv": up[:, hd:],
        "w_qT": a["L0_attn_w_q"].T, "w_kT": up[:, :hd].T, "w_out": a["L0_attn_w_out"],
        "ln1g": a["L0_ffn_ln1_g"].reshape(C, 1), "ln1b": a["L0_ffn_ln1_b"].reshape(C, 1),
        "w_small": np.concatenate([
            *(w.reshape(C, C) for w in (bq, turned(bq), bk, turned(bk), bv)),
            a["L1_attn_Wq"], a["L1_attn_Wk"], a["L1_attn_Wv"],
            twice(a["L0_ffn_Wproj"]), twice(a["L1_attn_Wo"])]),
        "ln2g": a["L0_ffn_ln2_g"].reshape(C, 1), "ln2b": a["L0_ffn_ln2_b"].reshape(C, 1),
        "w_gate": a["L0_ffn_Wgate"], "w1": a["L0_ffn_W1"],
        "b1": a["L0_ffn_b1"].reshape(EXPERTS * FT, P).T,
        "w2": a["L0_ffn_W2"].reshape(EXPERTS * FFN, C), "b2": a["L0_ffn_b2"],
        "c_bo": a["L1_attn_bo"].reshape(1, C),
        "f_gate": a["L1_ffn_w_gate"].T, "f_up": a["L1_ffn_w_up"].T, "f_down": a["L1_ffn_w_down"].T,
    }
    table = constants()
    sign = np.where(np.arange(C) % HD_S < HD_S // 2, np.float32(-1), np.float32(1))[:, None]
    table["sin"] = table["sin"] * sign
    data.update(table)

    nc = _bacc.Bacc("TRN2", target_bir_lowering=False, num_devices=1)
    arrays, args = {}, []
    for name, value in data.items():
        value = np.ascontiguousarray(value)
        arrays[f"in_{name}"] = value
        args.append(nc.dram_tensor(f"in_{name}", value.shape, _mybir.dt.from_np(value.dtype),
                                   kind="ExternalInput").ap())
    args.append(nc.dram_tensor("out_0", (B * T, C), F32, kind="ExternalOutput").ap())
    program(nc, *args)
    r = _run(nc, [arrays], core_ids=[0])
    return r.results[0]["out_0"].reshape(B, T, C)
```
